# Optimizing a Trainium2 kernel written in Bass

```python
import numpy as np
import jax
import jax.numpy as jnp

def _softmax(x, axis=-1):
    return jax.nn.softmax(x, axis=axis)

def _gelu(x):
    return jax.nn.gelu(x, approximate=True)

def _silu(x):
    return jax.nn.silu(x)

def _sigmoid(x):
    return jax.nn.sigmoid(x)

def _layernorm(x, axis=-1, eps=1e-05):
    m = jnp.mean(x, axis=axis, keepdims=True)
    v = jnp.var(x, axis=axis, keepdims=True)
    return (x - m) / jnp.sqrt(v + eps)

def _scatter_add(tgt, idx, src, axis=0):
    return tgt.at[idx].add(src)

def _segment_sum(src, seg, n):
    return jax.ops.segment_sum(src, seg, n)
kernel_name = 'mk_xattn_ffn_d4_seqx_r8_bcae54'

def setup_inputs(seed: int=0):
    np.random.seed(seed)
    _w = jnp.asarray

    def _rec_inputs():
        import jax
        import jax.numpy as jnp
        _rk = jax.random.key(seed)
        x = -0.0002928 + 1 * jax.random.normal(jax.random.fold_in(_rk, 1), (8, 256, 128), jnp.float32)
        _lenS = 256 - jax.random.randint(jax.random.fold_in(_rk, 7), (8,), 0, max(1, 256 // 4) + 1, jnp.int32)
        _lenS2 = 1601 - jax.random.randint(jax.random.fold_in(_rk, 8), (8,), 0, max(1, 1601 // 4) + 1, jnp.int32)
        _ctx_512P = jax.random.normal(jax.random.fold_in(_rk, 11), (8, 16, 64), jnp.float32)
        _ctx_512c = jax.random.dirichlet(jax.random.fold_in(_rk, 511), 0.3 * jnp.ones((16,), jnp.float32), (8, 1601))
        _ctx_512t = jnp.einsum('bsk,bkd->bsd', _ctx_512c, _ctx_512P)
        _ctx_512t = _ctx_512t * jax.lax.rsqrt(jnp.mean(jnp.square(_ctx_512t)) + 1e-12) * 0.953939
        ctx_512 = 0.00222621 + 0.99962 * (_ctx_512t + 0.3 * jax.random.normal(jax.random.fold_in(_rk, 611), (8, 1601, 64), jnp.float32))
        return (x, ctx_512)
    x, ctx_512 = _rec_inputs()

    def _L0_xattn_setup():
        import jax, jax.numpy as jnp
        import numpy as np
        B, T, TC, C, CC, H = (2, 256, 64, 128, 64, 16)
        D = C // H

        def _heads(t):
            b, l, _ = t.shape
            return t.reshape(b, l, H, D).transpose(0, 2, 1, 3)
        key = jax.random.key(seed)
        ks = jax.random.split(key, 18)
        w = lambda k, i, o: jax.random.normal(k, (i, o), jnp.float32) / np.sqrt(i).astype(np.float32)
        return {'x': jax.random.normal(ks[0], (B, T, C), jnp.float32), 'cross_input': jax.random.normal(ks[1], (B, TC, CC), jnp.float32), 'Wk': w(ks[2], C, C), 'bk': jnp.zeros((C,), jnp.float32), 'Wq': w(ks[3], C, C), 'bq': jnp.zeros((C,), jnp.float32), 'Wv': w(ks[4], C, C), 'bv': jnp.zeros((C,), jnp.float32), 'Wck': w(ks[5], CC, C), 'bck': jnp.zeros((C,), jnp.float32), 'Wcq': w(ks[6], C, C), 'bcq': jnp.zeros((C,), jnp.float32), 'Wcv': w(ks[7], CC, C), 'bcv': jnp.zeros((C,), jnp.float32), 'Wp': w(ks[8], C, C), 'bp': jnp.zeros((C,), jnp.float32)}
    _L0_xattn_all = _L0_xattn_setup()
    _L0_xattn_in = {k: v for k, v in _L0_xattn_all.items() if k in ('Wk', 'bk', 'Wq', 'bq', 'Wv', 'bv', 'Wck', 'bck', 'Wcq', 'bcq', 'Wcv', 'bcv', 'Wp', 'bp')}
    del _L0_xattn_all

    def _L0_ffn_setup():
        import jax, jax.numpy as jnp
        import numpy as np
        INT4_QMAX = 7.0

        def simulate_quantize_int4(w):
            scale = jnp.max(jnp.abs(w)) / INT4_QMAX
            q = jnp.clip(jnp.round(w / scale), -8.0, 7.0)
            return q * scale
        key = jax.random.key(seed)
        k_x, k_w, k_bias, k_a, k_b = jax.random.split(key, 5)
        d_in, features, rank = (128, 128, 16)
        x = jax.random.normal(k_x, (4, 1024, d_in), dtype=jnp.float32)
        kernel = jax.random.normal(k_w, (d_in, features), dtype=jnp.float32)
        bias = jax.random.normal(k_bias, (features,), dtype=jnp.float32)
        a = jax.random.normal(k_a, (d_in, rank), dtype=jnp.float32) * (1.0 / np.sqrt(d_in))
        b = jax.random.normal(k_b, (rank, features), dtype=jnp.float32) * 0.01
        return {'x': x, 'kernel': kernel, 'bias': bias, 'a': a, 'b': b}
    _L0_ffn_all = _L0_ffn_setup()
    _L0_ffn_in = {k: v for k, v in _L0_ffn_all.items() if k in ('kernel', 'bias', 'a', 'b')}
    del _L0_ffn_all

    def _L1_xattn_setup():
        import jax, jax.numpy as jnp
        import numpy as np
        H, D, C1, C2, S, M, B, W = (16, 32, 128, 64, 256, 64, 2, 4)

        def _ln(x, g, b):
            m = jnp.mean(x, -1, keepdims=True)
            v = jnp.var(x, -1, keepdims=True)
            return (x - m) * jax.lax.rsqrt(v + 1e-05) * g + b

        def _mha(x, y, wq, wk, wv, li1_w, li1_b, lnx_g, lnx_b, lny_g, lny_b, ln3_g, ln3_b, li2_w, li2_b, li3_w, li3_b, causal):
            xn = _ln(x, lnx_g, lnx_b)
            yn = _ln(y, lny_g, lny_b)
            q = jnp.einsum('bsc,hcd->bhsd', xn, wq)
            k = jnp.einsum('btc,hcd->bhtd', yn, wk)
            v = jnp.einsum('btc,hcd->bhtd', yn, wv)
            a = jax.nn.softmax(jnp.einsum('bhsd,bhtd->bhst', q, k) * D ** (-0.5), axis=-1)
            if causal:
                s, t = (a.shape[-2], a.shape[-1])
                mask = (jnp.arange(t)[None, :] > jnp.arange(s)[:, None]).astype(a.dtype)
                a = a * mask
            o = jnp.einsum('bhst,bhtd->bhsd', a, v)
            o = o.transpose(0, 2, 1, 3).reshape(x.shape[0], x.shape[1], H * D)
            x_out = x + o @ li1_w + li1_b
            h = jax.nn.gelu(_ln(x_out, ln3_g, ln3_b) @ li2_w + li2_b, approximate=False)
            return x_out + h @ li3_w + li3_b
        key = jax.random.key(seed)
        ks = iter(jax.random.split(key, 64))

        def w(shape, scale=0.02):
            return jax.random.normal(next(ks), shape, jnp.float32) * scale
        inp = {'xx': jax.random.normal(next(ks), (B, S, C1), jnp.float32), 'ee': jax.random.normal(next(ks), (B, M, C2), jnp.float32), 'ln1_g': jnp.ones(C1, jnp.float32), 'ln1_b': jnp.zeros(C1, jnp.float32), 'ln2_g': jnp.ones(C1, jnp.float32), 'ln2_b': jnp.zeros(C1, jnp.float32)}
        for pfx, cy in (('a1', C1), ('a2', C2)):
            inp[pfx + '_wq'] = w((H, C1, D))
            inp[pfx + '_wk'] = w((H, cy, D))
            inp[pfx + '_wv'] = w((H, cy, D))
            inp[pfx + '_li1_w'] = w((H * D, C1))
            inp[pfx + '_li1_b'] = jnp.zeros(C1, jnp.float32)
            inp[pfx + '_lnx_g'] = jnp.ones(C1, jnp.float32)
            inp[pfx + '_lnx_b'] = jnp.zeros(C1, jnp.float32)
            inp[pfx + '_lny_g'] = jnp.ones(cy, jnp.float32)
            inp[pfx + '_lny_b'] = jnp.zeros(cy, jnp.float32)
            inp[pfx + '_ln3_g'] = jnp.ones(C1, jnp.float32)
            inp[pfx + '_ln3_b'] = jnp.zeros(C1, jnp.float32)
            inp[pfx + '_li2_w'] = w((C1, C1 * W))
            inp[pfx + '_li2_b'] = jnp.zeros(C1 * W, jnp.float32)
            inp[pfx + '_li3_w'] = w((C1 * W, C1))
            inp[pfx + '_li3_b'] = jnp.zeros(C1, jnp.float32)
        inp['training'] = 0
        return inp
    _L1_xattn_all = _L1_xattn_setup()
    _L1_xattn_in = {k: v for k, v in _L1_xattn_all.items() if k in ('ln1_g', 'ln1_b', 'ln2_g', 'ln2_b', 'a1_wq', 'a1_wk', 'a1_wv', 'a1_li1_w', 'a1_li1_b', 'a1_lnx_g', 'a1_lnx_b', 'a1_lny_g', 'a1_lny_b', 'a1_ln3_g', 'a1_ln3_b', 'a1_li2_w', 'a1_li2_b', 'a1_li3_w', 'a1_li3_b', 'a2_wq', 'a2_wk', 'a2_wv', 'a2_li1_w', 'a2_li1_b', 'a2_lnx_g', 'a2_lnx_b', 'a2_lny_g', 'a2_lny_b', 'a2_ln3_g', 'a2_ln3_b', 'a2_li2_w', 'a2_li2_b', 'a2_li3_w', 'a2_li3_b')}
    del _L1_xattn_all

    def _L1_ffn_setup():
        import jax, jax.numpy as jnp
        import numpy as np
        EPS = 1e-05

        def _quantize(W):
            gamma = jnp.mean(jnp.abs(W))
            return jnp.clip(jnp.round(W / (gamma + EPS)), -1.0, 1.0)
        key = jax.random.key(seed)
        k_x, k_w1, k_b1, k_w2, k_b2 = jax.random.split(key, 5)
        n_embd = 128
        d_ff = 4 * n_embd
        B, S = (4, 512)
        bound1 = 1.0 / np.sqrt(n_embd)
        bound2 = 1.0 / np.sqrt(d_ff)
        x = jax.random.normal(k_x, (B, S, n_embd), dtype=jnp.float32)
        W1 = jax.random.uniform(k_w1, (d_ff, n_embd), jnp.float32, -bound1, bound1)
        b1 = jax.random.uniform(k_b1, (d_ff,), jnp.float32, -bound1, bound1)
        W2 = jax.random.uniform(k_w2, (n_embd, d_ff), jnp.float32, -bound2, bound2)
        b2 = jax.random.uniform(k_b2, (n_embd,), jnp.float32, -bound2, bound2)
        return {'x': x, 'W1': W1, 'b1': b1, 'W2': W2, 'b2': b2}
    _L1_ffn_all = _L1_ffn_setup()
    _L1_ffn_in = {k: v for k, v in _L1_ffn_all.items() if k in ('W1', 'b1', 'W2', 'b2')}
    del _L1_ffn_all

    def _L2_xattn_setup():
        import jax, jax.numpy as jnp
        import numpy as np
        B, LQ, LK = (8, 256, 256)
        QD, KD, VD = (128, 64, 64)
        key = jax.random.key(seed)
        ks = jax.random.split(key, 9)
        s = 0.02
        return {'query': jax.random.normal(ks[0], (B, LQ, QD), jnp.float32), 'key': jax.random.normal(ks[1], (B, LK, KD), jnp.float32), 'value': jax.random.normal(ks[2], (B, LK, VD), jnp.float32), 'Wq': jax.random.normal(ks[3], (QD, QD), jnp.float32) * s, 'bq': jnp.zeros((QD,), jnp.float32), 'Wk': jax.random.normal(ks[4], (KD, QD), jnp.float32) * s, 'bk': jnp.zeros((QD,), jnp.float32), 'Wv': jax.random.normal(ks[5], (VD, QD), jnp.float32) * s, 'bv': jnp.zeros((QD,), jnp.float32)}
    _L2_xattn_all = _L2_xattn_setup()
    _L2_xattn_in = {k: v for k, v in _L2_xattn_all.items() if k in ('Wq', 'bq', 'Wk', 'bk', 'Wv', 'bv')}
    del _L2_xattn_all

    def _L2_ffn_setup():
        import jax, jax.numpy as jnp
        import numpy as np
        B, T, C, H, E, K = (4, 128, 128, 128, 8, 2)

        def _swiglu(x):
            a, b = jnp.split(x, 2, axis=-1)
            return jax.nn.silu(a) * b
        key = jax.random.key(seed)
        ks = jax.random.split(key, 6)
        s = 0.02
        x = jax.random.normal(ks[0], (B, T, C), jnp.float32)
        w_shared_in = jax.random.normal(ks[1], (C, 2 * H), jnp.float32) * s
        w_shared_out = jax.random.normal(ks[2], (H, C), jnp.float32) * s
        w1_shared = jax.random.normal(ks[3], (C, 2 * H), jnp.float32) * s
        w2 = jax.random.normal(ks[4], (E, H, C), jnp.float32) * s
        w_gate = jax.random.normal(ks[5], (C, E), jnp.float32) * s
        gate_bias = jnp.zeros((E,), jnp.float32)
        return {'x': x, 'w_shared_in': w_shared_in, 'w_shared_out': w_shared_out, 'w1_shared': w1_shared, 'w2': w2, 'w_gate': w_gate, 'gate_bias': gate_bias}
    _L2_ffn_all = _L2_ffn_setup()
    _L2_ffn_in = {k: v for k, v in _L2_ffn_all.items() if k in ('w_shared_in', 'w_shared_out', 'w1_shared', 'w2', 'w_gate', 'gate_bias')}
    del _L2_ffn_all

    def _L3_xattn_setup():
        import jax, jax.numpy as jnp
        import numpy as np
        DIM = 128
        LATENT_DIM = 64
        NUM_HEADS = 16
        HEAD_DIM = DIM // NUM_HEADS
        SCALE = HEAD_DIM ** (-0.5)
        key = jax.random.key(seed)
        k1, k2, k3, k4, k5 = jax.random.split(key, 5)
        B, xN, zN = (2, 256, 256)
        x = jax.random.normal(k1, (B, xN, DIM), dtype=jnp.float32)
        z = jax.random.normal(k2, (B, zN, LATENT_DIM), dtype=jnp.float32)
        Wq = jax.random.normal(k3, (DIM, DIM), dtype=jnp.float32) * DIM ** (-0.5)
        Wkv = jax.random.normal(k4, (2 * DIM, LATENT_DIM), dtype=jnp.float32) * LATENT_DIM ** (-0.5)
        Wo = jax.random.normal(k5, (DIM, DIM), dtype=jnp.float32) * DIM ** (-0.5)
        return {'x': x, 'z': z, 'Wq': Wq, 'Wkv': Wkv, 'Wo': Wo}
    _L3_xattn_all = _L3_xattn_setup()
    _L3_xattn_in = {k: v for k, v in _L3_xattn_all.items() if k in ('Wq', 'Wkv', 'Wo')}
    del _L3_xattn_all

    def _L3_ffn_setup():
        import jax, jax.numpy as jnp
        import numpy as np
        BLOCK = 16
        _GRID = jnp.array([0.0, 0.5, 1.0, 1.5, 2.0, 3.0, 4.0, 6.0], dtype=jnp.float32)
        _MID = jnp.array([0.25, 0.75, 1.25, 1.75, 2.5, 3.5, 5.0], dtype=jnp.float32)

        def fp4_quant_dequant(x):
            shape = x.shape
            xb = x.reshape(shape[:-1] + (shape[-1] // BLOCK, BLOCK))
            scale = jnp.max(jnp.abs(xb), axis=-1, keepdims=True) / 6.0
            scale = jnp.maximum(scale, jnp.float32(1e-12))
            xn = xb / scale
            idx = jnp.searchsorted(_MID, jnp.abs(xn))
            q = _GRID[idx] * jnp.sign(xn) * scale
            return q.reshape(shape)

        def fp4_linear(x, w):
            xq = fp4_quant_dequant(x)
            wq = fp4_quant_dequant(w)
            return jnp.einsum('bsk,nk->bsn', xq, wq)
        key = jax.random.key(seed)
        k1, k2, k3, k4 = jax.random.split(key, 4)
        H, I = (128, 352)
        x = jax.random.normal(k1, (4, 512, H), dtype=jnp.float32)
        w_gate = jax.random.normal(k2, (I, H), dtype=jnp.float32) * 0.02
        w_up = jax.random.normal(k3, (I, H), dtype=jnp.float32) * 0.02
        w_down = jax.random.normal(k4, (H, I), dtype=jnp.float32) * 0.02
        return {'x': x, 'w_gate': w_gate, 'w_up': w_up, 'w_down': w_down}
    _L3_ffn_all = _L3_ffn_setup()
    _L3_ffn_in = {k: v for k, v in _L3_ffn_all.items() if k in ('w_gate', 'w_up', 'w_down')}
    del _L3_ffn_all
    return {'x': x, 'ctx_512': ctx_512, 'L0_xattn_Wk': _L0_xattn_in['Wk'], 'L0_xattn_bk': _L0_xattn_in['bk'], 'L0_xattn_Wq': _L0_xattn_in['Wq'], 'L0_xattn_bq': _L0_xattn_in['bq'], 'L0_xattn_Wv': _L0_xattn_in['Wv'], 'L0_xattn_bv': _L0_xattn_in['bv'], 'L0_xattn_Wck': _L0_xattn_in['Wck'], 'L0_xattn_bck': _L0_xattn_in['bck'], 'L0_xattn_Wcq': _L0_xattn_in['Wcq'], 'L0_xattn_bcq': _L0_xattn_in['bcq'], 'L0_xattn_Wcv': _L0_xattn_in['Wcv'], 'L0_xattn_bcv': _L0_xattn_in['bcv'], 'L0_xattn_Wp': _L0_xattn_in['Wp'], 'L0_xattn_bp': _L0_xattn_in['bp'], 'L0_ffn_kernel': _L0_ffn_in['kernel'], 'L0_ffn_bias': _L0_ffn_in['bias'], 'L0_ffn_a': _L0_ffn_in['a'], 'L0_ffn_b': _L0_ffn_in['b'], 'L1_xattn_ln1_g': _L1_xattn_in['ln1_g'], 'L1_xattn_ln1_b': _L1_xattn_in['ln1_b'], 'L1_xattn_ln2_g': _L1_xattn_in['ln2_g'], 'L1_xattn_ln2_b': _L1_xattn_in['ln2_b'], 'L1_xattn_a1_wq': _L1_xattn_in['a1_wq'], 'L1_xattn_a1_wk': _L1_xattn_in['a1_wk'], 'L1_xattn_a1_wv': _L1_xattn_in['a1_wv'], 'L1_xattn_a1_li1_w': _L1_xattn_in['a1_li1_w'], 'L1_xattn_a1_li1_b': _L1_xattn_in['a1_li1_b'], 'L1_xattn_a1_lnx_g': _L1_xattn_in['a1_lnx_g'], 'L1_xattn_a1_lnx_b': _L1_xattn_in['a1_lnx_b'], 'L1_xattn_a1_lny_g': _L1_xattn_in['a1_lny_g'], 'L1_xattn_a1_lny_b': _L1_xattn_in['a1_lny_b'], 'L1_xattn_a1_ln3_g': _L1_xattn_in['a1_ln3_g'], 'L1_xattn_a1_ln3_b': _L1_xattn_in['a1_ln3_b'], 'L1_xattn_a1_li2_w': _L1_xattn_in['a1_li2_w'], 'L1_xattn_a1_li2_b': _L1_xattn_in['a1_li2_b'], 'L1_xattn_a1_li3_w': _L1_xattn_in['a1_li3_w'], 'L1_xattn_a1_li3_b': _L1_xattn_in['a1_li3_b'], 'L1_xattn_a2_wq': _L1_xattn_in['a2_wq'], 'L1_xattn_a2_wk': _L1_xattn_in['a2_wk'], 'L1_xattn_a2_wv': _L1_xattn_in['a2_wv'], 'L1_xattn_a2_li1_w': _L1_xattn_in['a2_li1_w'], 'L1_xattn_a2_li1_b': _L1_xattn_in['a2_li1_b'], 'L1_xattn_a2_lnx_g': _L1_xattn_in['a2_lnx_g'], 'L1_xattn_a2_lnx_b': _L1_xattn_in['a2_lnx_b'], 'L1_xattn_a2_lny_g': _L1_xattn_in['a2_lny_g'], 'L1_xattn_a2_lny_b': _L1_xattn_in['a2_lny_b'], 'L1_xattn_a2_ln3_g': _L1_xattn_in['a2_ln3_g'], 'L1_xattn_a2_ln3_b': _L1_xattn_in['a2_ln3_b'], 'L1_xattn_a2_li2_w': _L1_xattn_in['a2_li2_w'], 'L1_xattn_a2_li2_b': _L1_xattn_in['a2_li2_b'], 'L1_xattn_a2_li3_w': _L1_xattn_in['a2_li3_w'], 'L1_xattn_a2_li3_b': _L1_xattn_in['a2_li3_b'], 'L1_ffn_W1': _L1_ffn_in['W1'], 'L1_ffn_b1': _L1_ffn_in['b1'], 'L1_ffn_W2': _L1_ffn_in['W2'], 'L1_ffn_b2': _L1_ffn_in['b2'], 'L2_xattn_Wq': _L2_xattn_in['Wq'], 'L2_xattn_bq': _L2_xattn_in['bq'], 'L2_xattn_Wk': _L2_xattn_in['Wk'], 'L2_xattn_bk': _L2_xattn_in['bk'], 'L2_xattn_Wv': _L2_xattn_in['Wv'], 'L2_xattn_bv': _L2_xattn_in['bv'], 'L2_ffn_w_shared_in': _L2_ffn_in['w_shared_in'], 'L2_ffn_w_shared_out': _L2_ffn_in['w_shared_out'], 'L2_ffn_w1_shared': _L2_ffn_in['w1_shared'], 'L2_ffn_w2': _L2_ffn_in['w2'], 'L2_ffn_w_gate': _L2_ffn_in['w_gate'], 'L2_ffn_gate_bias': _L2_ffn_in['gate_bias'], 'L3_xattn_Wq': _L3_xattn_in['Wq'], 'L3_xattn_Wkv': _L3_xattn_in['Wkv'], 'L3_xattn_Wo': _L3_xattn_in['Wo'], 'L3_ffn_w_gate': _L3_ffn_in['w_gate'], 'L3_ffn_w_up': _L3_ffn_in['w_up'], 'L3_ffn_w_down': _L3_ffn_in['w_down']}

def reference(x, ctx_512, L0_xattn_Wk, L0_xattn_bk, L0_xattn_Wq, L0_xattn_bq, L0_xattn_Wv, L0_xattn_bv, L0_xattn_Wck, L0_xattn_bck, L0_xattn_Wcq, L0_xattn_bcq, L0_xattn_Wcv, L0_xattn_bcv, L0_xattn_Wp, L0_xattn_bp, L0_ffn_kernel, L0_ffn_bias, L0_ffn_a, L0_ffn_b, L1_xattn_ln1_g, L1_xattn_ln1_b, L1_xattn_ln2_g, L1_xattn_ln2_b, L1_xattn_a1_wq, L1_xattn_a1_wk, L1_xattn_a1_wv, L1_xattn_a1_li1_w, L1_xattn_a1_li1_b, L1_xattn_a1_lnx_g, L1_xattn_a1_lnx_b, L1_xattn_a1_lny_g, L1_xattn_a1_lny_b, L1_xattn_a1_ln3_g, L1_xattn_a1_ln3_b, L1_xattn_a1_li2_w, L1_xattn_a1_li2_b, L1_xattn_a1_li3_w, L1_xattn_a1_li3_b, L1_xattn_a2_wq, L1_xattn_a2_wk, L1_xattn_a2_wv, L1_xattn_a2_li1_w, L1_xattn_a2_li1_b, L1_xattn_a2_lnx_g, L1_xattn_a2_lnx_b, L1_xattn_a2_lny_g, L1_xattn_a2_lny_b, L1_xattn_a2_ln3_g, L1_xattn_a2_ln3_b, L1_xattn_a2_li2_w, L1_xattn_a2_li2_b, L1_xattn_a2_li3_w, L1_xattn_a2_li3_b, L1_ffn_W1, L1_ffn_b1, L1_ffn_W2, L1_ffn_b2, L2_xattn_Wq, L2_xattn_bq, L2_xattn_Wk, L2_xattn_bk, L2_xattn_Wv, L2_xattn_bv, L2_ffn_w_shared_in, L2_ffn_w_shared_out, L2_ffn_w1_shared, L2_ffn_w2, L2_ffn_w_gate, L2_ffn_gate_bias, L3_xattn_Wq, L3_xattn_Wkv, L3_xattn_Wo, L3_ffn_w_gate, L3_ffn_w_up, L3_ffn_w_down):
    import jax
    import jax.numpy as jnp

    def _L0_xattn_ref(x, cross_input, Wk, bk, Wq, bq, Wv, bv, Wck, bck, Wcq, bcq, Wcv, bcv, Wp, bp):
        import jax, jax.numpy as jnp
        import numpy as np
        B, T, TC, C, CC, H = (2, 256, 64, 128, 64, 16)
        D = C // H

        def _heads(t):
            b, l, _ = t.shape
            return t.reshape(b, l, H, D).transpose(0, 2, 1, 3)
        scale = np.float32(1.0 / np.sqrt(D))
        q = _heads(x @ Wq + bq)
        k = _heads(x @ Wk + bk)
        v = _heads(x @ Wv + bv)
        att = jnp.einsum('bhqd,bhkd->bhqk', q, k) * scale
        causal = jnp.tril(jnp.ones((T, T), bool))
        att = jnp.where(causal[None, None], att, -jnp.inf)
        y = jnp.einsum('bhqk,bhkd->bhqd', jax.nn.softmax(att, axis=-1), v)
        qc = _heads(x @ Wcq + bcq)
        kc = _heads(cross_input @ Wck + bck)
        vc = _heads(cross_input @ Wcv + bcv)
        attc = jnp.einsum('bhqd,bhkd->bhqk', qc, kc) * scale
        y = y + jnp.einsum('bhqk,bhkd->bhqd', jax.nn.softmax(attc, axis=-1), vc)
        y = y.transpose(0, 2, 1, 3).reshape(x.shape[0], T, C)
        return y @ Wp + bp

    def _L0_ffn_ref(x, kernel, bias, a, b):
        import jax, jax.numpy as jnp
        import numpy as np
        INT4_QMAX = 7.0

        def simulate_quantize_int4(w):
            scale = jnp.max(jnp.abs(w)) / INT4_QMAX
            q = jnp.clip(jnp.round(w / scale), -8.0, 7.0)
            return q * scale
        w = simulate_quantize_int4(kernel)
        y = jnp.einsum('bsd,df->bsf', x, w) + bias
        lora = jnp.einsum('bsr,rf->bsf', jnp.einsum('bsd,dr->bsr', x, a), b)
        return y + lora

    def _L1_xattn_ref(xx, ee, ln1_g, ln1_b, ln2_g, ln2_b, a1_wq, a1_wk, a1_wv, a1_li1_w, a1_li1_b, a1_lnx_g, a1_lnx_b, a1_lny_g, a1_lny_b, a1_ln3_g, a1_ln3_b, a1_li2_w, a1_li2_b, a1_li3_w, a1_li3_b, a2_wq, a2_wk, a2_wv, a2_li1_w, a2_li1_b, a2_lnx_g, a2_lnx_b, a2_lny_g, a2_lny_b, a2_ln3_g, a2_ln3_b, a2_li2_w, a2_li2_b, a2_li3_w, a2_li3_b, training):
        import jax, jax.numpy as jnp
        import numpy as np
        H, D, C1, C2, S, M, B, W = (16, 32, 128, 64, 256, 64, 2, 4)

        def _ln(x, g, b):
            m = jnp.mean(x, -1, keepdims=True)
            v = jnp.var(x, -1, keepdims=True)
            return (x - m) * jax.lax.rsqrt(v + 1e-05) * g + b

        def _mha(x, y, wq, wk, wv, li1_w, li1_b, lnx_g, lnx_b, lny_g, lny_b, ln3_g, ln3_b, li2_w, li2_b, li3_w, li3_b, causal):
            xn = _ln(x, lnx_g, lnx_b)
            yn = _ln(y, lny_g, lny_b)
            q = jnp.einsum('bsc,hcd->bhsd', xn, wq)
            k = jnp.einsum('btc,hcd->bhtd', yn, wk)
            v = jnp.einsum('btc,hcd->bhtd', yn, wv)
            a = jax.nn.softmax(jnp.einsum('bhsd,bhtd->bhst', q, k) * D ** (-0.5), axis=-1)
            if causal:
                s, t = (a.shape[-2], a.shape[-1])
                mask = (jnp.arange(t)[None, :] > jnp.arange(s)[:, None]).astype(a.dtype)
                a = a * mask
            o = jnp.einsum('bhst,bhtd->bhsd', a, v)
            o = o.transpose(0, 2, 1, 3).reshape(x.shape[0], x.shape[1], H * D)
            x_out = x + o @ li1_w + li1_b
            h = jax.nn.gelu(_ln(x_out, ln3_g, ln3_b) @ li2_w + li2_b, approximate=False)
            return x_out + h @ li3_w + li3_b
        x = _ln(xx, ln1_g, ln1_b)
        x = x + _mha(x, x, a1_wq, a1_wk, a1_wv, a1_li1_w, a1_li1_b, a1_lnx_g, a1_lnx_b, a1_lny_g, a1_lny_b, a1_ln3_g, a1_ln3_b, a1_li2_w, a1_li2_b, a1_li3_w, a1_li3_b, causal=True)
        x = _ln(x, ln2_g, ln2_b)
        return x + _mha(x, ee, a2_wq, a2_wk, a2_wv, a2_li1_w, a2_li1_b, a2_lnx_g, a2_lnx_b, a2_lny_g, a2_lny_b, a2_ln3_g, a2_ln3_b, a2_li2_w, a2_li2_b, a2_li3_w, a2_li3_b, causal=False)

    def _L1_ffn_ref(x, W1, b1, W2, b2):
        import jax, jax.numpy as jnp
        import numpy as np
        EPS = 1e-05

        def _quantize(W):
            gamma = jnp.mean(jnp.abs(W))
            return jnp.clip(jnp.round(W / (gamma + EPS)), -1.0, 1.0)
        Wq1 = _quantize(W1)
        Wq2 = _quantize(W2)
        h = jax.nn.relu(jnp.einsum('bsd,fd->bsf', x, Wq1) + b1)
        out = jnp.einsum('bsf,df->bsd', h, Wq2) + b2
        return out

    def _L2_xattn_ref(query, key, value, Wq, bq, Wk, bk, Wv, bv):
        import jax, jax.numpy as jnp
        import numpy as np
        B, LQ, LK = (8, 256, 256)
        QD, KD, VD = (128, 64, 64)
        q = jnp.einsum('bld,de->ble', query, Wq) + bq
        k = jnp.einsum('bld,de->ble', key, Wk) + bk
        v = jnp.einsum('bld,de->ble', value, Wv) + bv
        scores = jnp.einsum('bqe,bke->bqk', q, k)
        attn = jax.nn.softmax(scores, axis=-1)
        out = jnp.einsum('bqk,bke->bqe', attn, v)
        return out

    def _L2_ffn_ref(x, w_shared_in, w_shared_out, w1_shared, w2, w_gate, gate_bias):
        import jax, jax.numpy as jnp
        import numpy as np
        B, T, C, H, E, K = (4, 128, 128, 128, 8, 2)

        def _swiglu(x):
            a, b = jnp.split(x, 2, axis=-1)
            return jax.nn.silu(a) * b
        Bx, Tx, Cx = x.shape
        S = Bx * Tx
        fx = x.reshape(S, Cx)
        shared_out = _swiglu(fx @ w_shared_in) @ w_shared_out
        logits = fx @ w_gate + gate_bias
        probs = jax.nn.softmax(logits, axis=-1)
        top_val, top_idx = jax.lax.top_k(probs, K)
        wdense = jnp.zeros((S, E), probs.dtype).at[jnp.arange(S)[:, None], top_idx].add(top_val)
        hid = _swiglu(fx @ w1_shared)
        routed_out = jnp.zeros_like(shared_out)
        for e in range(E):
            routed_out = routed_out + wdense[:, e:e + 1] * (hid @ w2[e])
        return (shared_out + routed_out).reshape(Bx, Tx, Cx)

    def _L3_xattn_ref(x, z, Wq, Wkv, Wo):
        import jax, jax.numpy as jnp
        import numpy as np
        DIM = 128
        LATENT_DIM = 64
        NUM_HEADS = 16
        HEAD_DIM = DIM // NUM_HEADS
        SCALE = HEAD_DIM ** (-0.5)
        B, xN, _ = x.shape
        _, zN, _ = z.shape
        Q = (x @ Wq.T).reshape(B, xN, NUM_HEADS, HEAD_DIM)
        KV = (z @ Wkv.T).reshape(B, zN, 2, NUM_HEADS, HEAD_DIM)
        K = KV[:, :, 0]
        V = KV[:, :, 1]
        attn = jnp.einsum('bqhd,bkhd->bhqk', Q, K) * SCALE
        attn = jax.nn.softmax(attn, axis=-1)
        O = jnp.einsum('bhqk,bkhd->bqhd', attn, V).reshape(B, xN, DIM)
        return O @ Wo.T

    def _L3_ffn_ref(x, w_gate, w_up, w_down):
        import jax, jax.numpy as jnp
        import numpy as np
        BLOCK = 16
        _GRID = jnp.array([0.0, 0.5, 1.0, 1.5, 2.0, 3.0, 4.0, 6.0], dtype=jnp.float32)
        _MID = jnp.array([0.25, 0.75, 1.25, 1.75, 2.5, 3.5, 5.0], dtype=jnp.float32)

        def fp4_quant_dequant(x):
            shape = x.shape
            xb = x.reshape(shape[:-1] + (shape[-1] // BLOCK, BLOCK))
            scale = jnp.max(jnp.abs(xb), axis=-1, keepdims=True) / 6.0
            scale = jnp.maximum(scale, jnp.float32(1e-12))
            xn = xb / scale
            idx = jnp.searchsorted(_MID, jnp.abs(xn))
            q = _GRID[idx] * jnp.sign(xn) * scale
            return q.reshape(shape)

        def fp4_linear(x, w):
            xq = fp4_quant_dequant(x)
            wq = fp4_quant_dequant(w)
            return jnp.einsum('bsk,nk->bsn', xq, wq)
        gate = fp4_linear(x, w_gate)
        y = fp4_linear(x, w_up)
        h = jax.nn.silu(gate) * y
        return fp4_linear(h, w_down)
    x = x + _L0_xattn_ref(_layernorm(x, axis=-1), ctx_512, L0_xattn_Wk, L0_xattn_bk, L0_xattn_Wq, L0_xattn_bq, L0_xattn_Wv, L0_xattn_bv, L0_xattn_Wck, L0_xattn_bck, L0_xattn_Wcq, L0_xattn_bcq, L0_xattn_Wcv, L0_xattn_bcv, L0_xattn_Wp, L0_xattn_bp)
    x = x + _L0_ffn_ref(_layernorm(x, axis=-1), L0_ffn_kernel, L0_ffn_bias, L0_ffn_a, L0_ffn_b)
    x = x + _L1_xattn_ref(_layernorm(x, axis=-1), ctx_512, L1_xattn_ln1_g, L1_xattn_ln1_b, L1_xattn_ln2_g, L1_xattn_ln2_b, L1_xattn_a1_wq, L1_xattn_a1_wk, L1_xattn_a1_wv, L1_xattn_a1_li1_w, L1_xattn_a1_li1_b, L1_xattn_a1_lnx_g, L1_xattn_a1_lnx_b, L1_xattn_a1_lny_g, L1_xattn_a1_lny_b, L1_xattn_a1_ln3_g, L1_xattn_a1_ln3_b, L1_xattn_a1_li2_w, L1_xattn_a1_li2_b, L1_xattn_a1_li3_w, L1_xattn_a1_li3_b, L1_xattn_a2_wq, L1_xattn_a2_wk, L1_xattn_a2_wv, L1_xattn_a2_li1_w, L1_xattn_a2_li1_b, L1_xattn_a2_lnx_g, L1_xattn_a2_lnx_b, L1_xattn_a2_lny_g, L1_xattn_a2_lny_b, L1_xattn_a2_ln3_g, L1_xattn_a2_ln3_b, L1_xattn_a2_li2_w, L1_xattn_a2_li2_b, L1_xattn_a2_li3_w, L1_xattn_a2_li3_b, 0)
    x = x + _L1_ffn_ref(_layernorm(x, axis=-1), L1_ffn_W1, L1_ffn_b1, L1_ffn_W2, L1_ffn_b2)
    x = x + _L2_xattn_ref(_layernorm(x, axis=-1), ctx_512, ctx_512, L2_xattn_Wq, L2_xattn_bq, L2_xattn_Wk, L2_xattn_bk, L2_xattn_Wv, L2_xattn_bv)
    x = x + _L2_ffn_ref(_layernorm(x, axis=-1), L2_ffn_w_shared_in, L2_ffn_w_shared_out, L2_ffn_w1_shared, L2_ffn_w2, L2_ffn_w_gate, L2_ffn_gate_bias)
    x = x + _L3_xattn_ref(_layernorm(x, axis=-1), ctx_512, L3_xattn_Wq, L3_xattn_Wkv, L3_xattn_Wo)
    x = x + _L3_ffn_ref(_layernorm(x, axis=-1), L3_ffn_w_gate, L3_ffn_w_up, L3_ffn_w_down)
    return x

_drawn_inputs = setup_inputs


def setup_inputs(seed=0):
    import zlib

    import numpy as np

    out = dict(_drawn_inputs(seed))
    spreads = {'L0_xattn_bk': (0.0, 2.0),
     'L0_xattn_bq': (0.0, 0.444),
     'L0_xattn_bv': (0.0, 0.1),
     'L0_xattn_bck': (0.0, 2.0),
     'L0_xattn_bcq': (0.0, 0.383),
     'L0_xattn_bcv': (0.0, 0.1),
     'L0_xattn_bp': (0.0, 0.1),
     'L1_xattn_ln1_g': (1.0, 0.6),
     'L1_xattn_ln1_b': (0.0, 0.544),
     'L1_xattn_ln2_g': (1.0, 0.566),
     'L1_xattn_ln2_b': (0.0, 0.585),
     'L1_xattn_a1_li1_b': (0.0, 0.8),
     'L1_xattn_a1_lnx_g': (1.0, 0.6),
     'L1_xattn_a1_lnx_b': (0.0, 0.8),
     'L1_xattn_a1_lny_g': (1.0, 0.6),
     'L1_xattn_a1_lny_b': (0.0, 0.8),
     'L1_xattn_a1_ln3_g': (1.0, 0.6),
     'L1_xattn_a1_ln3_b': (0.0, 0.8),
     'L1_xattn_a1_li2_b': (0.0, 0.8),
     'L1_xattn_a1_li3_b': (0.0, 0.8),
     'L1_xattn_a2_li1_b': (0.0, 0.8),
     'L1_xattn_a2_lnx_g': (1.0, 0.6),
     'L1_xattn_a2_lnx_b': (0.0, 0.8),
     'L1_xattn_a2_lny_g': (1.0, 0.6),
     'L1_xattn_a2_lny_b': (0.0, 0.8),
     'L1_xattn_a2_ln3_g': (1.0, 0.6),
     'L1_xattn_a2_ln3_b': (0.0, 0.8),
     'L1_xattn_a2_li2_b': (0.0, 0.8),
     'L1_xattn_a2_li3_b': (0.0, 0.8),
     'L2_xattn_bq': (0.0, 2.0),
     'L2_xattn_bk': (0.0, 2.0),
     'L2_xattn_bv': (0.0, 2.0),
     'L2_ffn_gate_bias': (0.0, 0.8)}
    factors = {'L0_ffn_a': 8.0,
     'L0_ffn_b': 8.0,
     'L1_xattn_a1_wq': 8.0,
     'L1_xattn_a1_wk': 8.0,
     'L1_xattn_a1_wv': 8.0,
     'L1_xattn_a1_li1_w': 8.0,
     'L1_xattn_a1_li2_w': 8.0,
     'L1_xattn_a1_li3_w': 8.0,
     'L1_xattn_a2_wq': 8.0,
     'L1_xattn_a2_wk': 8.0,
     'L1_xattn_a2_wv': 8.0,
     'L1_xattn_a2_li1_w': 8.0,
     'L1_xattn_a2_li2_w': 8.0,
     'L1_xattn_a2_li3_w': 8.0,
     'L1_ffn_b1': 8.0,
     'L1_ffn_b2': 64.0,
     'L2_xattn_Wq': 8.0,
     'L2_xattn_Wk': 8.0,
     'L2_xattn_Wv': 8.0,
     'L2_ffn_w_shared_in': 8.0,
     'L2_ffn_w_shared_out': 8.0,
     'L2_ffn_w1_shared': 8.0,
     'L2_ffn_w2': 8.0,
     'L2_ffn_w_gate': 8.0,
     'L3_xattn_Wq': 8.0,
     'L3_xattn_Wkv': 8.0,
     'L3_xattn_Wo': 8.0,
     'L3_ffn_w_gate': 8.0,
     'L3_ffn_w_up': 8.0,
     'L3_ffn_w_down': 8.0}
    for name, (base, spread) in spreads.items():
        noise = np.random.default_rng([zlib.crc32(name.encode()), seed]).standard_normal(out[name].shape)
        drawn = base * np.exp(spread * noise) if base else spread * noise
        out[name] = jnp.asarray(drawn.astype(out[name].dtype))
    for name, factor in factors.items():
        out[name] = (out[name] * factor).astype(out[name].dtype)
    return out
```

```python
from contextlib import ExitStack

import numpy as np

import concourse.bass as bass
from concourse import mybir

F32 = mybir.dt.float32
BF16 = mybir.dt.bfloat16
ALU = mybir.AluOpType
ACT = mybir.ActivationFunctionType
AX_X = mybir.AxisListType.X
RMAX = bass.bass_isa.ReduceOp.max
RADD = bass.bass_isa.ReduceOp.add

P = 128
B = 8
S = 256
QT = S // P
NT = B * QT
TOK = B * S
C = 128
CC = 64
LC = 1601
KT = -(-LC // P)
LCP = KT * P
H = 16
EPS = 1e-5
MASKED = -1e30
BANK = 512
START = 1


class Chip:

    def __init__(self, nc, ctx):
        self.nc = nc
        self.ctx = ctx
        self.made = 0
        sb = self.sb
        self.x = sb("x_res", [P, NT, C])
        self.ps = ctx.enter_context(nc.psum_tensor("ps", [P, 8, BANK], F32))
        self.ident = sb("ident", [P, P])
        self.identb = sb("identb", [P, P], BF16)
        self.ones = sb("ones_row", [1, P])
        self.mhalf = sb("mhalf", [P, NT])
        self.stats = sb("bn_stats_t", [P, NT, 6])
        self.mv = sb("mean_var", [P, NT, 2])
        self.ve = sb("var_eps", [P, NT])
        self.rstd = sb("rstd", [P, NT])

    def sb(self, name, shape, dt=F32, ctx=None):
        self.made += 1
        return (ctx or self.ctx).enter_context(self.nc.sbuf_tensor(f"{name}_{self.made}", shape, dt))


def sems(nc, ctx, *names, start=0):
    made = [ctx.enter_context(nc.semaphore(n)) for n in names]
    if start:
        for s in made:
            nc.gpsimd.sem_inc(s, start)

    def clear_all():
        nums = sorted(s.num for s in made)
        while nums:
            n = 1
            while n < len(nums) and nums[n] == nums[0] + n:
                n += 1
            nc.gpsimd.sem_clear(range(nums[0], nums[0] + n))
            nums = nums[n:]

    ctx.callback(clear_all)
    return made




def load(nc, pairs):
    with ExitStack() as ctx:
        sp_loaded, act_loaded = sems(nc, ctx, "sp_loaded", "act_loaded")
        block = ctx.enter_context(nc.Block())
        sp_pairs, act_pairs = pairs[0::2], pairs[1::2]

        @block.sync
        def _(sp):
            for dst, src in sp_pairs:
                sp.dma_start(dst, src).then_inc(sp_loaded, 16)
            sp.wait_ge(sp_loaded, 16 * len(sp_pairs))

        @block.scalar
        def _(act):
            for dst, src in act_pairs:
                act.dma_start(dst, src).then_inc(act_loaded, 16)
            if act_pairs:
                act.wait_ge(act_loaded, 16 * len(act_pairs))


def step_past(eng, passed):
    eng.sem_inc(passed, 1)


def set_constants(nc, k):
    with ExitStack() as ctx:
        zeroed, done = sems(nc, ctx, "zeroed", "consts_done")
        block = ctx.enter_context(nc.Block())

        @block.gpsimd
        def _(pool):
            pool.memset(k.ident[:], 0.0).then_inc(zeroed, 1)
            pool.memset(k.ones[:], 1.0)
            pool.memset(k.mhalf[:], -0.5)
            pool.wait_ge(zeroed, 1)
            pool.affine_select(out=k.ident[:], in_=k.ident[:], compare_op=ALU.not_equal, fill=1.0,
                               base=0, pattern=[[-1, P]], channel_multiplier=1).then_inc(done, 1)
            pool.wait_ge(done, 1)
            pool.tensor_copy(k.identb[:], k.ident[:]).then_inc(done, 1)


def normalize(nc, k, src, dst, n=NT, c=C):
    with ExitStack() as ctx:
        stats_done, aggr_done, var_ready, rstd_ready, normed = sems(
            nc, ctx, "stats_done", "aggr_done", "var_ready", "rstd_ready", "normed")
        block = ctx.enter_context(nc.Block())

        @block.vector
        def _(dve):
            for t in range(n):
                dve.bn_stats(k.stats[:, t, :], src[:, t, 0:c]).then_inc(stats_done, 1)
            for t in range(n):
                dve.wait_ge(stats_done, t + 1)
                dve.bn_aggr(k.mv[:, t, :], k.stats[:, t, :]).then_inc(aggr_done, 1)
            dve.wait_ge(aggr_done, n)
            dve.tensor_scalar(k.ve[:, 0:n], k.mv[:, 0:n, 1], EPS, None, ALU.add).then_inc(var_ready, 1)
            dve.wait_ge(rstd_ready, 1)
            for t in range(n):
                dve.tensor_scalar(dst[:, t, 0:c], src[:, t, 0:c], k.mv[:, t, 0:1], k.rstd[:, t:t + 1],
                                  ALU.subtract, ALU.mult).then_inc(normed, 1)

        @block.gpsimd
        def _(pool):
            pool.wait_ge(var_ready, 1)
            pool.tensor_tensor(k.rstd[:, 0:n], k.ve[:, 0:n], k.mhalf[:, 0:n], ALU.pow).then_inc(rstd_ready, 1)


def transpose(nc, k, src, c, dsts):
    with ExitStack() as ctx:
        turned, taken = sems(nc, ctx, "turned", "taken")
        block = ctx.enter_context(nc.Block())

        @block.tensor
        def _(pe):
            for q in range(NT // 4):
                for i in range(4):
                    ins = pe.transpose(k.ps[0:c, q, P * i:P * i + P], src(4 * q + i), k.ident[:])
                ins.then_inc(turned, 1)

        @block.scalar
        def _(act):
            for q in range(NT // 4):
                act.wait_ge(turned, q + 1)
                for dst, g, b in dsts:
                    out = dst[0:c, BANK * q:BANK * q + BANK]
                    if g is None:
                        act.activation(out, k.ps[0:c, q, :], ACT.Copy).then_inc(taken, 1)
                    else:
                        act.activation(out, k.ps[0:c, q, :], ACT.Identity, scale=g, bias=b).then_inc(taken, 1)


def linear_tokens(nc, k, n, terms, bias, out, add=None):
    per = max(1, BANK // n) if n == C else 1
    groups = NT // per
    with ExitStack() as ctx:
        summed, drained = sems(nc, ctx, "summed", "drained")
        block = ctx.enter_context(nc.Block())

        @block.tensor
        def _(pe):
            for g in range(groups):
                if g >= 4:
                    pe.wait_ge(drained, g - 3)
                for i in range(per):
                    t = per * g + i
                    o = k.ps[:, g % 4, n * i:n * i + n]
                    for j, (lhs, rhs) in enumerate(terms):
                        ins = pe.matmul(o, lhs(t), rhs, start=(j == 0), stop=(bias is None and j == len(terms) - 1))
                    if bias is not None:
                        ins = pe.matmul(o, k.ones[:], bias, start=False, stop=True)
                ins.then_inc(summed, 1)

        @block.vector
        def _(dve):
            for g in range(groups):
                dve.wait_ge(summed, g + 1)
                src = k.ps[:, g % 4, 0:n * per].rearrange("p (t n) -> p t n", n=n)
                tiles = slice(per * g, per * g + per)
                if add is None:
                    dve.tensor_copy(out(tiles), src).then_inc(drained, 1)
                else:
                    dve.tensor_tensor(out(tiles), src, add(tiles), ALU.add).then_inc(drained, 1)


def linear_channels(nc, k, blocks, func):
    with ExitStack() as ctx:
        summed, drained = sems(nc, ctx, "summed", "drained")
        block = ctx.enter_context(nc.Block())

        @block.tensor
        def _(pe):
            for u in range(4 * len(blocks)):
                lhs, xt, _, _, rows = blocks[u // 4]
                if u >= 8:
                    pe.wait_ge(drained, u - 7)
                cols = slice(BANK * (u % 4), BANK * (u % 4) + BANK)
                pe.matmul(k.ps[0:rows, u % 8, :], lhs, xt[:, cols], start=True, stop=True).then_inc(summed, 1)

        @block.scalar
        def _(act):
            for u in range(4 * len(blocks)):
                _, _, out, bias, rows = blocks[u // 4]
                act.wait_ge(summed, u + 1)
                cols = slice(BANK * (u % 4), BANK * (u % 4) + BANK)
                if bias is None:
                    act.activation(out[:, cols], k.ps[0:rows, u % 8, :], func).then_inc(drained, 1)
                else:
                    act.activation(out[:, cols], k.ps[0:rows, u % 8, :], func, bias=bias).then_inc(drained, 1)


def affine_rows(nc, k, src, dst, g_row, b_row, gb):
    with ExitStack() as ctx:
        spread, copied, scaled, done = sems(nc, ctx, "spread", "copied", "scaled", "affine_done")
        block = ctx.enter_context(nc.Block())

        @block.tensor
        def _(pe):
            pe.matmul(k.ps[:, 0, 0:C], k.ones[:], g_row, start=True, stop=True)
            pe.matmul(k.ps[:, 0, C:2 * C], k.ones[:], b_row, start=True, stop=True).then_inc(spread, 1)

        @block.vector
        def _(dve):
            dve.wait_ge(spread, 1)
            dve.tensor_copy(gb[:], k.ps[:, 0, 0:2 * C]).then_inc(copied, 1)
            dve.wait_ge(copied, 1)
            g = gb[:, 0:C].rearrange("p (t c) -> p t c", t=1).broadcast_to([P, NT, C])
            b = gb[:, C:2 * C].rearrange("p (t c) -> p t c", t=1).broadcast_to([P, NT, C])
            dve.tensor_tensor(dst, src, g, ALU.mult).then_inc(scaled, 1)
            dve.wait_ge(scaled, 1)
            dve.tensor_tensor(dst, dst, b, ALU.add).then_inc(done, 1)


def add_tokens(nc, out, a, b):
    with ExitStack() as ctx:
        (done,) = sems(nc, ctx, "add_done")
        block = ctx.enter_context(nc.Block())

        @block.vector
        def _(dve):
            dve.tensor_tensor(out, a, b, ALU.add).then_inc(done, 1)




def self_attention(nc, k, d, w, causal, scale, xq, xk, wq, wk, wv, qb, kb, vb, y):
    hb = P // w
    nb = H // hb
    vw = d + 1
    half = H * vw // 2
    plan = []
    for u in range(4):
        plan.append(("values", u))
    late = []
    for s in range(nb + 2):
        if 1 <= s <= nb:
            plan.append(("max_turn", s - 1))
        if s < nb:
            plan.append(("project", s))
        for j in range(hb):
            h = (s - 2) * hb + j
            if s >= 2:
                plan.append(("scores", h))
            if s < nb:
                plan.append(("maxima", s * hb + j))
            if late:
                plan.append(late.pop(0))
            if s >= 2 and h >= 1:
                plan.append(("weigh", h - 1))
                if h % hb == 0:
                    plan.append(("take", h // hb - 1))
                    late = [("turn", h // hb - 1)]
    plan += late + [("weigh", H - 1), ("take", nb - 1), ("turn", nb - 1)]
    ring_steps = [s for s in plan if s[0] in ("project", "maxima", "max_turn")]
    use = {s: n for n, s in enumerate(ring_steps)}
    per = len(ring_steps)
    assert per % 2 == 0

    with ExitStack() as ctx:
        def sb(name, shape, dt=F32):
            return k.sb(name, shape, dt, ctx)

        xqb, xkb = sb("xqb", [P, S]), sb("xkb", [P, S])
        v = sb("v_cur", [P, 2, H * vw])
        q1, q2, kk = sb("q1", [P, nb, S]), sb("q2", [P, nb, S]), sb("kk", [P, nb, S])
        mpad = sb("mpad", [P, 2, 2, P])
        pr = sb("probs", [P, 2, 2 * S])
        pm = sb("probs_masked", [P, 2, 3 * P])
        ot = sb("ot", [P, S])
        rden = sb("rden", [P, 2, hb])
        mask = sb("mask", [P, 3 * P])
        maskb, maskb_t = sb("maskb", [P, P], BF16), sb("maskb_t", [P, P], BF16)
        ones_col = sb("ones_col", [P, vw])
        set_up, masks, batch_in, v_full, v_free, ring_full, free0, free1 = sems(
            nc, ctx, "set_up", "masks", "batch_in", "v_full", "v_free", "ring_full", "ring_free0", "ring_free1",
            start=START)
        s_full, exp_done, masked, pv_done, o_free, y_full, y_free, rden_ready, max_half, q_half, y_half, passed = sems(
            nc, ctx, "s_full", "exp_done", "masked", "pv_done", "o_free", "y_full", "y_free", "rden_ready",
            "max_half", "q_half", "y_half", "passed", start=START)
        ring_free = [free0, free1]

        def ring(step):
            return k.ps[:, use[step] % 2, :]

        def wait_ring_reuse(pe, b, step):
            u = use[step]
            pe.wait_ge(ring_free[u % 2], START + b * (per // 2) + u // 2)

        def wait_consumed(eng, b, step):
            u = use[step]
            eng.wait_ge(ring_free[u % 2], START + b * (per // 2) + u // 2 + 1)

        def wait_produced(eng, b, step):
            eng.wait_ge(ring_full, START + b * per + use[step] + 1)

        obank, ybank = k.ps[:, 4, 0:S], k.ps[:, 5, 0:S]
        keys = S + P if causal else 2 * S
        block = ctx.enter_context(nc.Block())

        @block.gpsimd
        def _(pool):
            pool.memset(mpad[:], 0.0).then_inc(set_up, 1)
            pool.memset(ones_col[:], 0.0).then_inc(set_up, 1)
            pool.memset(mask[:], 1.0).then_inc(set_up, 1)
            pool.memset(maskb[:], 0.0).then_inc(set_up, 1)
            pool.memset(maskb_t[:], 0.0).then_inc(set_up, 1)
            pool.wait_ge(set_up, START + 5)
            pool.memset(ones_col[:, d:d + 1], 1.0).then_inc(masks, 1)
            pool.affine_select(out=maskb[:], in_=maskb[:], compare_op=ALU.is_ge, fill=MASKED, base=0,
                               pattern=[[-1, P]], channel_multiplier=1).then_inc(masks, 1)
            pool.affine_select(out=maskb_t[:], in_=maskb_t[:], compare_op=ALU.is_ge, fill=MASKED, base=0,
                               pattern=[[1, P]], channel_multiplier=-1).then_inc(masks, 1)
            for sq in (mask[:, 0:P], mask[:, 2 * P:3 * P]):
                pool.affine_select(out=sq, in_=sq, compare_op=ALU.is_gt, fill=0.0, base=0,
                                   pattern=[[-1, P]], channel_multiplier=1).then_inc(masks, 1)
            with pool.Fori(0, B) as b:
                pool.wait_ge(ring_full, START + b * per)
                step_past(pool, passed)
                pool.tensor_copy(xqb[:], xq[:, bass.ds(S * b, S)]).then_inc(batch_in, 1)
                pool.tensor_copy(xkb[:], xk[:, bass.ds(S * b, S)]).then_inc(batch_in, 1)

        @block.tensor
        def _(pe):
            pe.wait_ge(masks, START + 5)
            pe.wait_ge(o_free, START + 1)
            with pe.Fori(0, B) as b:
                for step in plan:
                    kind, n = step
                    if kind == "values":
                        kt, hf = n // 2, n % 2
                        pe.wait_ge(batch_in, START + 2 * b + 2)
                        pe.wait_ge(v_free, START + 4 * b + max(n - 1, 0))
                        o = k.ps[:, 6 + n % 2, 0:half]
                        pe.matmul(o, xkb[:, P * kt:P * kt + P], wv[:, half * hf:half * hf + half],
                                  start=True, stop=False)
                        pe.matmul(o, k.ones[:], vb[:, half * hf:half * hf + half],
                                  start=False, stop=True).then_inc(v_full, 1)
                    elif kind == "project":
                        wait_ring_reuse(pe, b, step)
                        pe.matmul(ring(step)[:, 0:S], wq[:, P * n:P * n + P], xqb[:], start=True, stop=True)
                        pe.matmul(ring(step)[:, S:2 * S], wk[:, P * n:P * n + P], xkb[:],
                                  start=True, stop=True).then_inc(ring_full, 1)
                    elif kind == "maxima":
                        g, r = n // hb, w * (n % hb)
                        wait_ring_reuse(pe, b, step)
                        wait_consumed(pe, b, ("project", g))
                        for qt in range(2):
                            nk = P * (qt + 1) if causal else S
                            ins = pe.matmul(ring(step)[:, S * qt:S * qt + nk], q1[r:r + w, g, P * qt:P * qt + P],
                                            kk[r:r + w, g, 0:nk], start=True, stop=True)
                            if causal:
                                ins = pe.matmul(ring(step)[:, S * qt + nk - P:S * qt + nk], k.identb[:],
                                                maskb[:], start=False, stop=True, skip_group_check=True)
                        ins.then_inc(ring_full, 1)
                    elif kind == "max_turn":
                        wait_ring_reuse(pe, b, step)
                        wait_consumed(pe, b, ("maxima", hb * n + hb - 2))
                        wait_consumed(pe, b, ("maxima", hb * n + hb - 1))
                        for qt in range(2):
                            ins = pe.transpose(ring(step)[:, P * qt:P * qt + P], mpad[:, n % 2, qt, :], k.ident[:])
                        ins.then_inc(ring_full, 1)
                    elif kind == "scores":
                        g, r = n // hb, w * (n % hb)
                        wait_consumed(pe, b, ("max_turn", g))
                        pe.wait_ge(exp_done, START + H * b + max(n - 1, 0))
                        o = k.ps[:, 2 + n % 2, :]
                        pe.matmul(o[:, 0:S], kk[r:r + w, g, 0:P], q2[r:r + w, g, :], start=True, stop=True)
                        if causal:
                            pe.matmul(o[:, 0:P], k.identb[:], maskb_t[:], start=False, stop=True, skip_group_check=True)
                            pe.matmul(o[:, S:S + P], kk[r:r + w, g, P:S], q2[r:r + w, g, P:S],
                                      start=True, stop=True)
                            pe.matmul(o[:, S:S + P], k.identb[:], maskb_t[:],
                                      start=False, stop=True, skip_group_check=True).then_inc(s_full, 1)
                        else:
                            pe.matmul(o[:, S:2 * S], kk[r:r + w, g, P:S], q2[r:r + w, g, :],
                                      start=True, stop=True).then_inc(s_full, 1)
                    elif kind == "weigh":
                        r, i = w * (n % hb), n % 2
                        if n == 0:
                            pe.wait_ge(v_free, START + 4 * b + 4)
                        if n % hb == 0:
                            pe.wait_ge(o_free, START + nb * b + n // hb + 1)
                        pe.wait_ge(exp_done, START + H * b + n + 1)
                        o = obank[r:r + vw, :]
                        vh = slice(vw * n, vw * n + vw)
                        if causal:
                            pe.matmul(o, v[:, 0, vh], pr[:, i, 0:S], start=True, stop=True)
                            pe.matmul(o[:, P:S], v[:, 1, vh], pr[:, i, S:S + P],
                                      start=False, stop=True, skip_group_check=True).then_inc(pv_done, 1)
                        else:
                            pe.matmul(o, ones_col[:], pr[:, i, 0:S], start=True, stop=True)
                            pe.matmul(o, ones_col[:], pr[:, i, S:2 * S], start=False, stop=True, skip_group_check=True)
                            pe.wait_ge(masked, START + 2 * (H * b + n + 1))
                            pe.matmul(o[:, 0:P], v[:, 0, vh], pm[:, i, 0:P], start=False, stop=True,
                                      skip_group_check=True)
                            pe.matmul(o, v[:, 1, vh], pm[:, i, P:3 * P], start=False, stop=True,
                                      skip_group_check=True).then_inc(pv_done, 1)
                    elif kind == "turn":
                        pe.wait_ge(o_free, START + nb * b + n + 2)
                        pe.wait_ge(y_free, START + nb * b + n)
                        for qt in range(2):
                            ins = pe.transpose(ybank[:, P * qt:P * qt + P], ot[:, P * qt:P * qt + P], k.ident[:])
                        ins.then_inc(y_full, 1)

        @block.scalar
        def _(act):
            with act.Fori(0, B) as b:
                for step in plan:
                    kind, n = step
                    if kind == "values":
                        kt, hf = n // 2, n % 2
                        act.wait_ge(v_full, START + 4 * b + n + 1)
                        act.activation(v[:, kt, half * hf:half * hf + half], k.ps[:, 6 + n % 2, 0:half],
                                       ACT.Copy).then_inc(v_free, 1)
                    elif kind == "project":
                        wait_produced(act, b, step)
                        act.activation(q1[:, n, :], ring(step)[:, 0:S], ACT.Identity,
                                       bias=qb[:, n:n + 1]).then_inc(q_half, 1)
                        act.activation(kk[:, n, :], ring(step)[:, S:2 * S], ACT.Identity,
                                       bias=kb[:, n:n + 1]).then_inc(ring_free[use[step] % 2], 1)
                    elif kind == "scores":
                        act.wait_ge(s_full, START + H * b + n + 1)
                        act.wait_ge(pv_done, START + H * b + max(n - 1, 0))
                        act.activation(pr[:, n % 2, 0:keys], k.ps[:, 2 + n % 2, 0:keys], ACT.Exp,
                                       scale=scale).then_inc(exp_done, 1)

        @block.vector
        def _(dve):
            dve.memset(obank, 0.0).then_inc(o_free, 1)
            with dve.Fori(0, B) as b:
                for step in plan:
                    kind, n = step
                    if kind == "maxima":
                        g, col = n // hb, w * (n % hb) + d
                        wait_produced(dve, b, step)
                        free = ring_free[use[step] % 2]
                        if causal:
                            dve.tensor_reduce(mpad[:, g % 2, 0, col:col + 1], ring(step)[:, 0:P], AX_X, ALU.max,
                                              negate=True).then_inc(max_half, 1)
                            dve.tensor_reduce(mpad[:, g % 2, 1, col:col + 1], ring(step)[:, S:2 * S], AX_X,
                                              ALU.max, negate=True).then_inc(free, 1)
                        else:
                            dve.tensor_reduce(mpad[:, g % 2, :, col], ring(step).rearrange("p (q n) -> p q n", q=2), AX_X, ALU.max,
                                              negate=True).then_inc(free, 1)
                    elif kind == "max_turn":
                        wait_produced(dve, b, step)
                        dve.tensor_tensor(q2[:, n, :], ring(step)[:, 0:S], q1[:, n, :],
                                          ALU.add).then_inc(ring_free[use[step] % 2], 1)
                    elif kind == "weigh" and not causal:
                        i = n % 2
                        dve.wait_ge(exp_done, START + H * b + n + 1)
                        dve.wait_ge(pv_done, START + H * b + max(n - 1, 0))
                        dve.tensor_tensor(pm[:, i, 0:P], pr[:, i, 0:P], mask[:, 0:P], ALU.mult).then_inc(masked, 1)
                        dve.tensor_tensor(pm[:, i, P:3 * P], pr[:, i, S:2 * S], mask[:, P:3 * P],
                                          ALU.mult).then_inc(masked, 1)
                    elif kind == "take":
                        dve.wait_ge(pv_done, START + H * b + hb * (n + 1))
                        dve.wait_ge(y_full, START + nb * b + n)
                        dve.tensor_copy(ot[:], obank).then_inc(o_free, 1)
                    elif kind == "turn":
                        dve.wait_ge(y_full, START + nb * b + n + 1)
                        yb = ybank.rearrange("p (q j n) -> p q j n", q=2, j=hb)
                        dve.reciprocal(rden[:], yb[:, :, :, d]).then_inc(rden_ready, 1)
                        dve.wait_ge(rden_ready, START + nb * b + n + 1)
                        for qt in range(2):
                            out = y[:, bass.ds(2 * b + qt, 1), d * hb * n:d * hb * (n + 1)]
                            ins = dve.tensor_tensor(
                                out.rearrange("p t (j n) -> p (t j) n", n=d), yb[:, qt, :, 0:d],
                                rden[:, qt, :].rearrange("p (j n) -> p j n", n=1).broadcast_to([P, hb, d]),
                                ALU.mult)
                            ins.then_inc(y_half if qt == 0 else y_free, 1)



R = CC + 1
CH = -(-LC // 4)
CHUNKS = [(CH * c, min(CH * c + CH, LC)) for c in range(4)]
GROUPS = [range(4 * c, min(4 * c + 4, KT)) for c in range(4)]
SLOT = 64
PAIRS = 6


def cross_attention(nc, k, split, nh, d, scale, ctx_t, q_in, wq, wk, wv, y, ctx_tokens=None):
    hb = 2 if nh > 1 else 1
    nb = nh // hb
    vw = d + 1
    pitch = 32 if vw <= 32 else 64 if vw <= 64 else P
    og = min(P // pitch, nh)
    no = nh // og
    common = not split and wq.shape[1] == R
    ns = 4 * nh
    if wv is None:
        vuses = []
    elif split:
        vuses = [[(t, 0, nh * vw) for t in g] for g in GROUPS]
    else:
        half = nh * vw // 2
        vuses = [[(t, 0, half), (t, half, 2 * half)] for t in range(KT - 1)]
        vuses += [[(KT - 1, 0, half)], [(KT - 1, half, 2 * half)]]
    nv = len(vuses)
    quses = [] if split else [(qt, n) for qt in range(QT) for n in range(0, wq.shape[1], BANK)]
    msteps = 4 if split else 2 if common else 1

    first = [("keys", n) for n in range(4)] if split else [("queries", n) for n in range(len(quses))]
    turns = lambda g: [("q_turn", g)] + ([("k_turn", g, 0), ("k_turn", g, 1)] if split else [])
    npm = 8 * hb

    def plan(search, attend):
        out = [("values", n) for n in range(nv)] if attend else []
        late = []
        for s in range(nb + 1):
            maxima = []
            if search and s == 0:
                out += first + [("split", 0)]
            if search and s >= 1:
                out += turns(s - 1)
                maxima = [("maxima", s - 1, n) for n in range(npm)]
            for i in range(4 * hb):
                n = 4 * hb * s + i
                if attend and s < nb:
                    out.append(("scores", n))
                out += maxima[2 * i:2 * i + 2] + late
                late = []
                if search and s >= 2 and i == min(3, 4 * hb - 1):
                    out.append(("max_turn", s - 2))
                if attend and s < nb and n >= 1:
                    out.append(("weigh", n - 1))
                    if n % (4 * og) == 0:
                        out.append(("take", n // (4 * og) - 1))
                        late = [("turn", n // (4 * og) - 1)]
                if attend and s == nb and i == 0:
                    out += [("weigh", ns - 1), ("take", no - 1)]
                    late = [("turn", no - 1)]
            if maxima:
                out.append(("place_max", s - 1))
        if search:
            out.append(("max_turn", nb - 1))
        return out + late

    ring_steps = [s for s in plan(True, False) if s[0] in ("keys", "queries", "q_turn", "k_turn", "maxima", "max_turn")]
    use = {s: n for n, s in enumerate(ring_steps)}
    per = len(ring_steps)
    nsu = nv + ns
    assert per % 2 == 0 and nsu % 2 == 0
    assert [s for s in plan(True, True) if s in use] == ring_steps
    KDT = BF16 if split else F32

    with ExitStack() as ctx:
        def sb(name, shape, dt=F32):
            return k.sb(name, shape, dt, ctx)

        ctx_a, ctx_b = sb("ctx_a", [R, LCP]), sb("ctx_b", [R, LCP])
        v = sb("v_cur", [P, KT, nh * vw])
        pr = sb("probs", [P, 2, 4 * S])
        ot = sb("ot", [P, S])
        rden = sb("rden", [P, QT, og])
        mx, negm = sb("mx", [P, 2, QT * hb, 4]), sb("negm", [P, nb, QT * hb])
        mr = sb("max_rest", [P, QT, hb])
        if split:
            kf = sb("kf", [P, KT, C])
            ktok = sb("ktok", [P, KT, H * SLOT], BF16)
            kparts = ktok[:].rearrange("p t (h s) -> p (t h) s", s=SLOT)
            kt = sb("kt", [P, nb, LC], BF16)
            qtok = sb("qtok", [P, QT, H * SLOT], BF16)
            q1, q2 = sb("q1", [P, nb, S], BF16), sb("q2", [P, nb, S], BF16)
        else:
            xq = sb("xq_cur", [P, S])
            qtok = sb("qtok", [P, QT, nh, R])
            qhh, qlo = sb("qhh", [P, QT, nh, 2 * CC], BF16), sb("qlo", [P, QT, nh, CC], BF16)
            yhl = sb("yhl", [P, LCP], BF16)
            qhh_t, qlo_t = sb("qhh_t", [P, 2, hb * S], BF16), sb("qlo_t", [CC, 2, hb * S], BF16)
            q2 = sb("q2", [R, nb, hb * S])
            cmn = sb("common", [P, QT])
        a_in, b_in, set_up, q_in_place, parts, copies, ring_full, free0, free1 = sems(
            nc, ctx, "ctx_a_in", "ctx_b_in", "set_up", "q_in_place", "parts", "copies", "ring_full",
            "ring_free0", "ring_free1",
            start=START)
        s_full, s_free, pv_done, o_free, y_full, y_free, rden_ready, y_half, neg_ready, max_placed, q_half, passed = sems(
            nc, ctx, "s_full", "s_free", "pv_done", "o_free", "y_full", "y_free", "rden_ready", "y_half",
            "neg_ready", "max_placed", "q_half", "passed", start=START)
        ring_free = [free0, free1]

        def ring(step, dt=F32):
            bank = k.ps[:, use[step] % 2, :]
            return bank if dt == F32 else bank.bitcast(dt)

        def wait_ring_reuse(pe, b, step):
            u = use[step]
            pe.wait_ge(ring_free[u % 2], START + b * (per // 2) + u // 2)

        def wait_consumed(eng, b, step):
            u = use[step]
            eng.wait_ge(ring_free[u % 2], START + b * (per // 2) + u // 2 + 1)

        def wait_produced(eng, b, step):
            eng.wait_ge(ring_full, START + b * per + use[step] + 1)

        def pair(u):
            return k.ps[:, 2 + 2 * (u % 2):4 + 2 * (u % 2), :].rearrange("p a n -> p (a n)")

        obank, ybank = k.ps[:, 6, 0:S], k.ps[:, 7, 0:S]
        block = ctx.enter_context(nc.Block())

        def iterations(eng, emit):
            emit(0, None, plan(True, False))
            with eng.Fori(0, B - 1) as i:
                emit(i + 1, i, plan(True, True))
            emit(None, B - 1, plan(False, True))

        @block.sync
        def _(sp):
            def load_a(b):
                if split:
                    sp.wait_ge(ring_full, START + (b * per if isinstance(b, int) else (b - 1) * per + 4))
                else:
                    sp.wait_ge(parts, START + 4 * b)
                sp.dma_start(ctx_a[0:CC, 0:LC], ctx_t[b]).then_inc(a_in, 16)

            def load_b(b):
                if split:
                    sp.wait_ge(s_full, START + (b * nsu if isinstance(b, int) and b == 0 else (b - 1) * nsu + nv))
                else:
                    sp.wait_ge(s_full, START + b * nsu)
                sp.dma_start(ctx_b[0:CC, 0:LC], ctx_t[b]).then_inc(b_in, 16)
                if wv is None:
                    sp.wait_ge(pv_done, START + b * ns)
                    sp.dma_start(v[:, 0:KT - 1, 0:CC], ctx_tokens[b][0:LCP - P, :].rearrange(
                        "(t p) c -> p t c", p=P)).then_inc(b_in, 16)
                    sp.dma_start(v[0:LC - LCP + P, KT - 1, 0:CC], ctx_tokens[b][LCP - P:LC, :]).then_inc(b_in, 16)

            sp.wait_ge(set_up, START + 4)
            load_a(0)
            load_b(0)
            with sp.Fori(0, B - 1) as i:
                load_a(i + 1)
                load_b(i + 1)

        nload = 16 if wv is not None else 48

        @block.gpsimd
        def _(pool):
            pool.memset(ctx_a[:], 0.0).then_inc(set_up, 1)
            pool.memset(ctx_b[:], 0.0).then_inc(set_up, 1)
            pool.wait_ge(set_up, START + 2)
            pool.memset(ctx_a[CC:R, :], 1.0).then_inc(set_up, 1)
            pool.memset(ctx_b[CC:R, :], 1.0).then_inc(set_up, 1)
            pool.wait_ge(set_up, START + 4)
            if split:
                kslots = ktok[:].rearrange("p t (h s) -> p (t h) s", s=SLOT)
                pool.memset(kslots[:, :, 8 * PAIRS:8 * PAIRS + 3], 1.0).then_inc(set_up, 1)
                pool.memset(kslots[:, :, 8 * PAIRS + 3:SLOT], 0.0).then_inc(set_up, 1)
            elif wv is None:
                pool.memset(v[:, :, CC:R], 1.0).then_inc(set_up, 1)

            def emit(ba, bb, steps):
                for step in steps:
                    kind, g = step[0], step[1]
                    if kind == "split":
                        if split:
                            pool.wait_ge(parts, START + 4 * ba + 1)
                            step_past(pool, passed)
                            pool.tensor_copy(kparts[:, :, 24:32], kparts[:, :, 0:8]).then_inc(copies, 1)
                            pool.tensor_copy(kparts[:, :, 40:48], kparts[:, :, 0:8]).then_inc(copies, 1)
                            pool.wait_ge(parts, START + 4 * ba + 3)
                            step_past(pool, passed)
                            pool.tensor_copy(kparts[:, :, 32:40], kparts[:, :, 8:16]).then_inc(copies, 1)
                        else:
                            pool.wait_ge(parts, START + 4 * ba + 1)
                            step_past(pool, passed)
                            pool.tensor_copy(qhh[:, :, :, CC:2 * CC], qhh[:, :, :, 0:CC]).then_inc(copies, 1)
                    elif kind == "place_max":
                        n = nb * ba + g
                        pool.wait_ge(neg_ready, START + n + 1)
                        step_past(pool, passed)
                        neg = negm[:, g, :].rearrange("p (q h) -> p q h", q=QT)
                        if split:
                            qs = qtok[:].rearrange("p q (h s) -> p q h s", s=SLOT)[:, :, hb * g:hb * g + hb, :]
                            cut = [qs[:, :, :, 8 * PAIRS + i] for i in range(3)]
                            pool.tensor_copy(cut[0], neg).then_inc(max_placed, 1)
                            pool.wait_ge(max_placed, START + 4 * n + 1)
                            pool.tensor_tensor(mr[:], neg, cut[0], ALU.subtract).then_inc(max_placed, 1)
                            pool.wait_ge(max_placed, START + 4 * n + 2)
                            step_past(pool, passed)
                            pool.tensor_copy(cut[1], mr[:]).then_inc(max_placed, 1)
                            pool.wait_ge(max_placed, START + 4 * n + 3)
                            pool.tensor_tensor(cut[2], mr[:], cut[1], ALU.subtract).then_inc(max_placed, 1)
                        elif common:
                            cm = cmn[:].rearrange("p (q h) -> p q h", h=1)
                            pool.tensor_tensor(mr[:], cm, neg, ALU.subtract).then_inc(max_placed, 1)
                            pool.wait_ge(max_placed, START + 2 * n + 1)
                            pool.tensor_tensor(qtok[:, :, :, CC], cm, mr[:], ALU.subtract).then_inc(max_placed, 1)
                        else:
                            pool.tensor_copy(qtok[:, :, hb * g:hb * g + hb, CC], neg).then_inc(max_placed, 1)

            def bring_q(b):
                pool.wait_ge(ring_full, START + b * per)
                step_past(pool, passed)
                if split:
                    pool.tensor_copy(qtok[:], q_in[:, bass.ds(QT * b, QT), :]).then_inc(q_in_place, 1)
                else:
                    pool.tensor_copy(xq[:], q_in[:, bass.ds(S * b, S)]).then_inc(q_in_place, 1)

            bring_q(0)
            emit(0, None, plan(True, False))
            with pool.Fori(0, B - 1) as i:
                bring_q(i + 1)
                emit(i + 1, i, plan(True, True))

        nset = 4 + (2 if split else 1 if wv is None else 0)

        @block.tensor
        def _(pe):
            def emit(ba, bb, steps):
                for step in steps:
                    kind, g = step[0], step[1]
                    if step in use:
                        wait_ring_reuse(pe, ba, step)
                    if kind == "keys":
                        pe.wait_ge(a_in, START + 16 * ba + 16)
                        for i, t in enumerate(GROUPS[g]):
                            ins = pe.matmul(ring(step)[:, C * i:C * i + C], ctx_a[:, P * t:P * t + P], wk,
                                            start=True, stop=True)
                        ins.then_inc(ring_full, 1)
                    elif kind == "queries":
                        pe.wait_ge(q_in_place, START + ba + 1)
                        qt, n = quses[g]
                        m = min(BANK, wq.shape[1] - n)
                        pe.matmul(ring(step)[:, 0:m], xq[:, P * qt:P * qt + P], wq[:, n:n + m],
                                  start=True, stop=True).then_inc(ring_full, 1)
                    elif kind == "q_turn" and split:
                        pe.wait_ge(q_in_place, START + ba + 1)
                        for qt in range(QT):
                            ins = pe.transpose(ring(step, BF16)[:, P * qt:P * qt + P],
                                               qtok[:, qt, P * g:P * g + P], k.identb[:])
                        ins.then_inc(ring_full, 1)
                    elif kind == "q_turn":
                        pe.wait_ge(parts, START + 4 * ba + 2)
                        pe.wait_ge(copies, START + ba + 1)
                        for j in range(hb):
                            for qt in range(QT):
                                c = S * j + P * qt
                                pe.transpose(ring(step, BF16)[:, c:c + P], qhh[:, qt, hb * g + j, :], k.identb[:])
                                c += hb * S
                                ins = pe.transpose(ring(step, BF16)[0:CC, c:c + P], qlo[:, qt, hb * g + j, :],
                                                   k.identb[:])
                        ins.then_inc(ring_full, 1)
                    elif kind == "k_turn":
                        pe.wait_ge(parts, START + 4 * ba + 4)
                        pe.wait_ge(copies, START + 3 * ba + 3)
                        for i, t in enumerate(range(8 * step[2], min(8 * step[2] + 8, KT))):
                            ins = pe.transpose(ring(step, BF16)[:, P * i:P * i + P], ktok[:, t, P * g:P * g + P],
                                               k.identb[:])
                        ins.then_inc(ring_full, 1)
                    elif kind == "maxima":
                        n = step[2]
                        j, qt, (lo, hi) = n // 8, n // 4 % 2, CHUNKS[n % 4]
                        wait_consumed(pe, ba, turns(g)[-1])
                        if split:
                            wait_consumed(pe, ba, turns(g)[-2])
                            r = SLOT * j
                            pe.matmul(ring(step)[:, 0:hi - lo], q1[r:r + SLOT - 16, g, P * qt:P * qt + P],
                                      kt[r:r + SLOT - 16, g, lo:hi], start=True, stop=True).then_inc(ring_full, 1)
                        else:
                            c = S * j + P * qt
                            pe.wait_ge(parts, START + 4 * ba + 4)
                            pe.matmul(ring(step)[:, 0:hi - lo], qhh_t[:, g % 2, c:c + P], yhl[:, lo:hi],
                                      start=True, stop=False)
                            pe.matmul(ring(step)[:, 0:hi - lo], qlo_t[:, g % 2, c:c + P], yhl[0:CC, lo:hi],
                                      start=False, stop=True).then_inc(ring_full, 1)
                    elif kind == "max_turn":
                        pe.wait_ge(max_placed, START + msteps * (nb * ba + g + 1))
                        if split:
                            for qt in range(QT):
                                ins = pe.transpose(ring(step, BF16)[:, P * qt:P * qt + P],
                                                   qtok[:, qt, P * g:P * g + P], k.identb[:])
                        else:
                            for j in range(hb):
                                for qt in range(QT):
                                    c = S * j + P * qt
                                    ins = pe.transpose(ring(step)[0:R, c:c + P], qtok[:, qt, hb * g + j, :],
                                                       k.ident[:])
                        ins.then_inc(ring_full, 1)
                    elif kind == "values":
                        pe.wait_ge(b_in, START + nload * bb + nload)
                        pe.wait_ge(s_free, START + nsu * bb + max(g - 1, 0))
                        for i, (t, lo, hi) in enumerate(vuses[g]):
                            c = P * 2 * i if split else BANK * i
                            ins = pe.matmul(pair(g)[:, c:c + hi - lo], ctx_b[:, P * t:P * t + P], wv[:, lo:hi],
                                            start=True, stop=True)
                        ins.then_inc(s_full, 1)
                    elif kind == "scores":
                        u, h = nv + g, g // 4
                        pe.wait_ge(s_free, START + nsu * bb + max(u - 1, 0))
                        if wv is None and g == 0:
                            pe.wait_ge(b_in, START + nload * bb + nload)
                        if g % (4 * hb) == 0:
                            wait_consumed(pe, bb, ("max_turn", h // hb))
                        for i, t in enumerate(GROUPS[g % 4]):
                            m = min(P, LC - P * t)
                            o = pair(u)[0:m, S * i:S * i + S]
                            if split:
                                r = SLOT * (h % 2)
                                ins = pe.matmul(o, kt[r:r + SLOT, h // 2, P * t:P * t + m],
                                                q2[r:r + SLOT, h // 2, :], start=True, stop=True)
                            else:
                                ins = pe.matmul(o, ctx_b[:, P * t:P * t + m],
                                                q2[:, h // hb, S * (h % hb):S * (h % hb) + S],
                                                start=True, stop=True)
                        ins.then_inc(s_full, 1)
                    elif kind == "weigh":
                        h = g // 4
                        r = pitch * (h % og)
                        if g == 0 and nv:
                            pe.wait_ge(s_free, START + nsu * bb + nv)
                        if g % (4 * og) == 0:
                            pe.wait_ge(o_free, START + no * bb + g // (4 * og) + 1)
                        pe.wait_ge(s_free, START + nsu * bb + nv + g + 1)
                        for i, t in enumerate(GROUPS[g % 4]):
                            m = min(P, LC - P * t)
                            ins = pe.matmul(obank[r:r + vw, :], v[0:m, t, vw * h:vw * h + vw],
                                            pr[0:m, g % 2, S * i:S * i + S], start=(t == 0), stop=(t == KT - 1))
                        ins.then_inc(pv_done, 1)
                    elif kind == "turn":
                        pe.wait_ge(o_free, START + no * bb + g + 2)
                        pe.wait_ge(y_free, START + no * bb + g)
                        for qt in range(QT):
                            ins = pe.transpose(ybank[:, P * qt:P * qt + P], ot[:, P * qt:P * qt + P], k.ident[:])
                        ins.then_inc(y_full, 1)

            pe.wait_ge(set_up, START + nset)
            pe.wait_ge(o_free, START + 1)
            iterations(pe, emit)

        @block.scalar
        def _(act):
            def emit(ba, bb, steps):
                for step in steps:
                    kind, g = step[0], step[1]
                    if step in use and kind != "maxima":
                        wait_produced(act, ba, step)
                        free = ring_free[use[step] % 2]
                    if kind == "keys":
                        if g == 0:
                            act.wait_ge(parts, START + 4 * ba)
                        n = len(GROUPS[g])
                        act.activation(kf[:, 4 * g:4 * g + n, :], ring(step)[:, 0:C * n].rearrange(
                            "p (t c) -> p t c", c=C), ACT.Copy).then_inc(free, 1)
                    elif kind == "queries":
                        qt, n = quses[g]
                        if common:
                            act.activation(qtok[:, qt, 0, :], ring(step)[:, 0:R], ACT.Copy).then_inc(free, 1)
                        else:
                            act.activation(qtok[:, qt, n // CC:n // CC + BANK // CC, 0:CC],
                                           ring(step).rearrange("p (h c) -> p h c", c=CC),
                                           ACT.Copy).then_inc(free, 1)
                    elif kind == "q_turn" and split:
                        act.activation(q1[:, g, :], ring(step, BF16)[:, 0:S], ACT.Copy).then_inc(free, 1)
                    elif kind == "q_turn":
                        act.activation(qhh_t[:, g % 2, :], ring(step, BF16)[:, 0:hb * S],
                                       ACT.Copy).then_inc(q_half, 1)
                        act.activation(qlo_t[:, g % 2, :], ring(step, BF16)[0:CC, hb * S:2 * hb * S],
                                       ACT.Copy).then_inc(free, 1)
                    elif kind == "k_turn":
                        lo, hi = 8 * P * step[2], min(8 * P * step[2] + 8 * P, LC)
                        act.activation(kt[:, g, lo:hi], ring(step, BF16)[:, 0:hi - lo], ACT.Copy).then_inc(free, 1)
                    elif kind == "max_turn":
                        if split:
                            act.activation(q2[:, g, :], ring(step, BF16)[:, 0:S], ACT.Copy).then_inc(free, 1)
                        else:
                            act.activation(q2[:, g, :], ring(step)[0:R, 0:hb * S], ACT.Copy).then_inc(free, 1)
                    elif kind == "values":
                        act.wait_ge(s_full, START + nsu * bb + g + 1)
                        t, lo, _ = vuses[g][0]
                        n = len(vuses[g])
                        if split:
                            src = pair(g)[:, 0:2 * P * n].rearrange("p (t c) -> p t c", c=2 * P)[:, :, 0:nh * vw]
                            dst = v[:, t:t + n, :]
                        else:
                            src = pair(g)[:, 0:BANK * n].rearrange("p (t c) -> p t c", c=BANK)[:, :, 0:half]
                            dst = v[:, t, lo:lo + n * half].rearrange("p (t c) -> p t c", c=half)
                        act.activation(dst, src, ACT.Copy).then_inc(s_free, 1)
                    elif kind == "scores":
                        u = nv + g
                        act.wait_ge(s_full, START + nsu * bb + u + 1)
                        act.wait_ge(pv_done, START + ns * bb + max(g - 1, 0))
                        n = S * len(GROUPS[g % 4])
                        m = P if g % 4 < 3 else LC - LCP + P
                        act.activation(pr[0:m, g % 2, 0:n], pair(u)[0:m, 0:n], ACT.Exp,
                                       scale=scale).then_inc(s_free, 1)

            iterations(act, emit)

        @block.vector
        def _(dve):
            def emit(ba, bb, steps):
                for step in steps:
                    kind, g = step[0], step[1]
                    if kind == "split" and split:
                        kv = kf[:].rearrange("p t (h c) -> p (t h) c", c=8)
                        wait_consumed(dve, ba, ("keys", 2))
                        wait_consumed(dve, ba, ("keys", 3))
                        dve.tensor_copy(kparts[:, :, 0:8], kv).then_inc(parts, 1)
                        dve.wait_ge(parts, START + 4 * ba + 1)
                        dve.tensor_tensor(kv, kv, kparts[:, :, 0:8], ALU.subtract).then_inc(parts, 1)
                        dve.wait_ge(parts, START + 4 * ba + 2)
                        dve.tensor_copy(kparts[:, :, 8:16], kv).then_inc(parts, 1)
                        dve.wait_ge(parts, START + 4 * ba + 3)
                        dve.tensor_tensor(kparts[:, :, 16:24], kv, kparts[:, :, 8:16],
                                          ALU.subtract).then_inc(parts, 1)
                    elif kind == "split":
                        wait_consumed(dve, ba, first[-1])
                        wait_consumed(dve, ba, first[-2])
                        q = qtok[:, :, :, 0:CC]
                        dve.tensor_copy(qhh[:, :, :, 0:CC], q).then_inc(parts, 1)
                        dve.wait_ge(parts, START + 4 * ba + 1)
                        dve.tensor_tensor(qlo[:], q, qhh[:, :, :, 0:CC], ALU.subtract).then_inc(parts, 1)
                        dve.wait_ge(a_in, START + 16 * ba + 16)
                        dve.tensor_copy(yhl[0:CC, 0:LC], ctx_a[0:CC, 0:LC]).then_inc(parts, 1)
                        dve.wait_ge(parts, START + 4 * ba + 3)
                        dve.tensor_tensor(yhl[CC:P, 0:LC], ctx_a[0:CC, 0:LC], yhl[0:CC, 0:LC],
                                          ALU.subtract).then_inc(parts, 1)
                        if common:
                            dve.tensor_copy(cmn[:], qtok[:, :, 0, CC]).then_inc(q_half, 1)
                    elif kind == "maxima":
                        n = step[2]
                        j, qt, (lo, hi) = n // 8, n // 4 % 2, CHUNKS[n % 4]
                        if n == 0:
                            dve.wait_ge(neg_ready, START + nb * ba + max(g - 1, 0))
                        wait_produced(dve, ba, step)
                        i = hb * qt + j
                        dve.tensor_reduce(mx[:, g % 2, i, n % 4:n % 4 + 1], ring(step)[:, 0:hi - lo], AX_X,
                                          ALU.max).then_inc(ring_free[use[step] % 2], 1)
                    elif kind == "place_max":
                        wait_consumed(dve, ba, ("maxima", g, npm - 1))
                        wait_consumed(dve, ba, ("maxima", g, npm - 2))
                        dve.tensor_reduce(negm[:, g, :], mx[:, g % 2, :, :], AX_X, ALU.max,
                                          negate=True).then_inc(neg_ready, 1)
                    elif kind == "take":
                        dve.wait_ge(pv_done, START + ns * bb + 4 * og * (g + 1))
                        dve.wait_ge(y_full, START + no * bb + g)
                        dve.tensor_copy(ot[:], obank).then_inc(o_free, 1)
                    elif kind == "turn":
                        dve.wait_ge(y_full, START + no * bb + g + 1)
                        yb = ybank.rearrange("p (q j n) -> p q j n", q=QT, j=og)
                        dve.reciprocal(rden[:], yb[:, :, :, d]).then_inc(rden_ready, 1)
                        dve.wait_ge(rden_ready, START + no * bb + g + 1)
                        for qt in range(QT):
                            o = y[:, bass.ds(QT * bb + qt, 1), d * og * g:d * og * (g + 1)]
                            dve.tensor_tensor(
                                o.rearrange("p t (j n) -> p (t j) n", n=d), yb[:, qt, :, 0:d],
                                rden[:, qt, :].rearrange("p (j n) -> p j n", n=1).broadcast_to([P, og, d]),
                                ALU.mult).then_inc(y_half if qt == 0 else y_free, 1)

            dve.memset(obank, 0.0).then_inc(o_free, 1)
            iterations(dve, emit)


def split_queries(nc, k, q, qtok):
    with ExitStack() as ctx:
        rest = k.sb("q_rest", [P, NT, C], F32, ctx)
        (cut,) = sems(nc, ctx, "cut")
        block = ctx.enter_context(nc.Block())
        qv = q.rearrange("p t (h c) -> p (t h) c", c=8)
        rv = rest[:].rearrange("p t (h c) -> p (t h) c", c=8)
        o = qtok[:].rearrange("p t (h s) -> p (t h) s", s=SLOT)

        @block.vector
        def _(dve):
            steps = [
                lambda: dve.tensor_copy(o[:, :, 0:8], qv),
                lambda: dve.tensor_tensor(rv, qv, o[:, :, 0:8], ALU.subtract),
                lambda: dve.tensor_copy(o[:, :, 24:32], rv),
                lambda: dve.tensor_tensor(o[:, :, 40:48], rv, o[:, :, 24:32], ALU.subtract),
                lambda: dve.tensor_copy(o[:, :, 8:16], o[:, :, 0:8]),
                lambda: dve.tensor_copy(o[:, :, 16:24], o[:, :, 0:8]),
                lambda: dve.tensor_copy(o[:, :, 32:40], o[:, :, 24:32]),
                lambda: dve.memset(o[:, :, 48:SLOT], 0.0),
            ]
            for n, step in enumerate(steps):
                step().then_inc(cut, 1)
                dve.wait_ge(cut, n + 1)




def vec_row(ap):
    return ap.rearrange("(a n) -> a n", a=1)


def vec_col(ap):
    return ap.rearrange("(n a) -> n a", a=1)


def clear(nc, *tiles):
    with ExitStack() as ctx:
        (cleared,) = sems(nc, ctx, "cleared")
        block = ctx.enter_context(nc.Block())

        @block.gpsimd
        def _(pool):
            for t, value in tiles:
                pool.memset(t, value).then_inc(cleared, 1)


def quantize_weight(nc, k, w, add, factor, floor, lo, hi, rescale):
    rounder = 1.5 * 2.0 ** 23
    with ExitStack() as ctx:
        m, ma, s, r = (k.sb(n, [P, 1], F32, ctx) for n in ("qm", "qma", "qs", "qr"))
        dve_step, reduced = sems(nc, ctx, "dve_step", "reduced")
        block = ctx.enter_context(nc.Block())

        @block.vector
        def _(dve):
            dve.tensor_reduce(m[:], w, AX_X, ALU.add if add else ALU.max,
                              apply_absolute_value=True).then_inc(dve_step, 1)
            dve.wait_ge(reduced, 1)
            dve.tensor_scalar(s[:], ma[:], factor, floor, ALU.mult, ALU.add).then_inc(dve_step, 1)
            dve.wait_ge(dve_step, 2)
            dve.reciprocal(r[:], s[:]).then_inc(dve_step, 1)
            dve.wait_ge(dve_step, 3)
            dve.tensor_scalar(w, w, r[:], rounder, ALU.mult, ALU.add).then_inc(dve_step, 1)
            dve.wait_ge(dve_step, 4)
            dve.tensor_scalar(w, w, rounder, hi, ALU.subtract, ALU.min).then_inc(dve_step, 1)
            dve.wait_ge(dve_step, 5)
            if rescale:
                dve.tensor_scalar(w, w, lo, s[:], ALU.max, ALU.mult).then_inc(dve_step, 1)
            else:
                dve.tensor_scalar(w, w, lo, None, ALU.max).then_inc(dve_step, 1)

        @block.gpsimd
        def _(pool):
            pool.wait_ge(dve_step, 1)
            pool.partition_all_reduce(ma[:], m[:], P, RADD if add else RMAX).then_inc(reduced, 1)


def quantize_fp4(nc, k, x, n):
    with ExitStack() as ctx:
        sb = lambda name, shape: k.sb(name, shape, F32, ctx)
        am, sc, rs = sb("fam", [P, n]), sb("fsc", [P, n]), sb("frs", [P, n])
        a, c, big = sb("fabs", [P, n, 16]), sb("fcount", [P, n, 16]), sb("fbig", [P, n, 16])
        dve_step, abs_ready, sign_ready = sems(nc, ctx, "dve_step", "abs_ready", "sign_ready")
        spread = lambda t: t[:].rearrange("p (n a) -> p n a", a=1).broadcast_to([P, n, 16])
        block = ctx.enter_context(nc.Block())

        @block.vector
        def _(dve):
            def above(out, v, rest):
                return dve.scalar_tensor_tensor(out=out[:], in0=a[:], scalar=v, in1=rest[:], op0=ALU.is_gt, op1=ALU.add)

            steps = [
                lambda: dve.tensor_reduce(am[:], x, AX_X, ALU.max, apply_absolute_value=True),
                lambda: dve.tensor_scalar(sc[:], am[:], 1.0 / 6.0, 1e-12, ALU.mult, ALU.max),
                lambda: dve.reciprocal(rs[:], sc[:]),
                lambda: dve.tensor_tensor(a[:], x, spread(rs), ALU.mult),
                lambda: dve.tensor_scalar(big[:], a[:], 5.0, 2.0, ALU.is_gt, ALU.mult),
                lambda: above(big, 3.5, big),
                lambda: above(big, 2.5, big),
                lambda: dve.tensor_scalar(c[:], a[:], 1.75, None, ALU.is_gt),
                lambda: dve.scalar_tensor_tensor(out=c[:], in0=big[:], scalar=2.0, in1=c[:], op0=ALU.mult, op1=ALU.add),
                lambda: above(c, 1.25, c),
                lambda: above(c, 0.75, c),
                lambda: above(c, 0.25, c),
                lambda: dve.scalar_tensor_tensor(out=c[:], in0=c[:], scalar=0.5, in1=x, op0=ALU.mult, op1=ALU.mult),
                lambda: dve.tensor_tensor(x, c[:], spread(sc), ALU.mult),
            ]
            for i, step in enumerate(steps):
                if i == 4:
                    dve.wait_ge(abs_ready, 1)
                if i == 12:
                    dve.wait_ge(sign_ready, 1)
                step().then_inc(dve_step, 1)
                dve.wait_ge(dve_step, i + 1)

        @block.scalar
        def _(act):
            act.wait_ge(dve_step, 4)
            act.activation(a[:], a[:], ACT.Abs).then_inc(abs_ready, 1)
            act.activation(x, x, ACT.Sign).then_inc(sign_ready, 1)


def transpose_weight(nc, k, pieces):
    with ExitStack() as ctx:
        turned, taken = sems(nc, ctx, "turned", "taken")
        block = ctx.enter_context(nc.Block())
        sizes = [(src.shape[0], src.shape[1]) for src, _ in pieces]

        @block.tensor
        def _(pe):
            for n, (src, _) in enumerate(pieces):
                r, c = sizes[n]
                if n >= 8:
                    pe.wait_ge(taken, n - 7)
                pe.transpose(k.ps[0:c, n % 8, 0:r], src, k.ident[0:r, 0:r]).then_inc(turned, 1)

        @block.vector
        def _(dve):
            for n, (_, dst) in enumerate(pieces):
                r, c = sizes[n]
                dve.wait_ge(turned, n + 1)
                dve.tensor_copy(dst, k.ps[0:c, n % 8, 0:r]).then_inc(taken, 1)


def gated(nc, k, n, lhs_a, lhs_b, rhs_a, rhs_b, out):
    count = len(out)
    with ExitStack() as ctx:
        s = k.sb("silu", [P, 2, n], F32, ctx)
        summed, silu_done, mult_done = sems(nc, ctx, "summed", "silu_done", "mult_done")
        block = ctx.enter_context(nc.Block())

        @block.tensor
        def _(pe):
            for i in range(count):
                if i >= 4:
                    pe.wait_ge(mult_done, i - 3)
                pe.matmul(k.ps[:, 2 * (i % 4), 0:n], lhs_a(i), rhs_a(i), start=True, stop=True)
                pe.matmul(k.ps[:, 2 * (i % 4) + 1, 0:n], lhs_b(i), rhs_b(i), start=True, stop=True).then_inc(summed, 1)

        @block.scalar
        def _(act):
            for i in range(count):
                act.wait_ge(summed, i + 1)
                if i >= 2:
                    act.wait_ge(mult_done, i - 1)
                act.activation(s[:, i % 2, :], k.ps[:, 2 * (i % 4), 0:n], ACT.Silu).then_inc(silu_done, 1)

        @block.vector
        def _(dve):
            for i in range(count):
                dve.wait_ge(silu_done, i + 1)
                dve.tensor_tensor(out[i], k.ps[:, 2 * (i % 4) + 1, 0:n], s[:, i % 2, :], ALU.mult).then_inc(mult_done, 1)


def normalize_context(nc, k, ctx_tokens, g_col, b_col, out_t):
    with ExitStack() as ctx:
        sb = lambda name, shape: k.sb(name, shape, F32, ctx)
        c, st, mv = sb("ctx_tok", [P, KT, CC]), sb("cst", [P, KT, 6]), sb("cmv", [P, KT, 2])
        ve, rstd, mhalf = sb("cve", [P, KT]), sb("crstd", [P, KT]), sb("cmhalf", [P, KT])
        ct = sb("ctx_norm_t", [CC, LC])
        padded, c_in, stats_done, aggr_done, var_ready, rstd_ready, normed, turned, taken, stored, passed = sems(
            nc, ctx, "padded", "c_in", "stats_done", "aggr_done", "var_ready", "rstd_ready", "normed", "turned",
            "taken", "stored", "passed", start=START)
        last = LC - LCP + P
        block = ctx.enter_context(nc.Block())

        @block.sync
        def _(sp):
            sp.wait_ge(padded, START + 2)
            with sp.Fori(0, B) as b:
                sp.wait_ge(turned, START + 4 * b)
                sp.dma_start(c[:, 0:KT - 1, :], ctx_tokens[b][0:LCP - P, :].rearrange(
                    "(t p) c -> p t c", p=P)).then_inc(c_in, 16)
                sp.dma_start(c[0:last, KT - 1, :], ctx_tokens[b][LCP - P:LC, :]).then_inc(c_in, 16)
                sp.wait_ge(taken, START + 4 * b + 4)
                sp.dma_start(out_t[b], ct[:]).then_inc(stored, 16)
            sp.wait_ge(stored, START + 16 * B)

        @block.gpsimd
        def _(pool):
            pool.memset(c[:], 0.0).then_inc(padded, 1)
            pool.memset(mhalf[:], -0.5).then_inc(padded, 1)
            pool.wait_ge(padded, START + 2)
            with pool.Fori(0, B) as b:
                pool.wait_ge(var_ready, START + b + 1)
                pool.tensor_tensor(rstd[:], ve[:], mhalf[:], ALU.pow).then_inc(rstd_ready, 1)

        @block.vector
        def _(dve):
            with dve.Fori(0, B) as b:
                dve.wait_ge(c_in, START + 32 * b + 32)
                for t in range(KT):
                    dve.bn_stats(st[:, t, :], c[:, t, :]).then_inc(stats_done, 1)
                dve.wait_ge(stats_done, START + KT * b + KT)
                step_past(dve, passed)
                for t in range(KT):
                    dve.bn_aggr(mv[:, t, :], st[:, t, :]).then_inc(aggr_done, 1)
                dve.wait_ge(aggr_done, START + KT * b + KT)
                dve.tensor_scalar(ve[:], mv[:, :, 1], EPS, None, ALU.add).then_inc(var_ready, 1)
                dve.wait_ge(rstd_ready, START + b + 1)
                for t in range(KT):
                    dve.tensor_scalar(c[:, t, :], c[:, t, :], mv[:, t, 0:1], rstd[:, t:t + 1],
                                      ALU.subtract, ALU.mult).then_inc(normed, 1)

        @block.tensor
        def _(pe):
            with pe.Fori(0, B) as b:
                for q in range(4):
                    pe.wait_ge(normed, START + KT * b + min(4 * q + 4, KT))
                    pe.wait_ge(taken, START + 4 * b)
                    step_past(pe, passed)
                    for i, t in enumerate(GROUPS[q]):
                        ins = pe.transpose(k.ps[0:CC, q, P * i:P * i + P], c[:, t, :], k.ident[:])
                    ins.then_inc(turned, 1)

        @block.scalar
        def _(act):
            with act.Fori(0, B) as b:
                act.wait_ge(stored, START + 16 * b)
                for q in range(4):
                    lo, hi = BANK * q, min(BANK * q + BANK, LC)
                    act.wait_ge(turned, START + 4 * b + q + 1)
                    act.activation(ct[:, lo:hi], k.ps[0:CC, q, 0:hi - lo], ACT.Identity, scale=g_col,
                                   bias=b_col).then_inc(taken, 1)


def fold_keys(nc, k, wq_t, wk_t, out):
    with ExitStack() as ctx:
        folded, taken = sems(nc, ctx, "folded", "taken")
        block = ctx.enter_context(nc.Block())

        @block.tensor
        def _(pe):
            for j in range(4):
                for g in range(4):
                    ins = pe.matmul(k.ps[:, j, CC * g:CC * g + CC], wq_t[32 * j:32 * j + 32, g, :],
                                    wk_t[32 * j:32 * j + 32, g, :], start=True, stop=True)
                ins.then_inc(folded, 1)

        @block.vector
        def _(dve):
            for j in range(4):
                dve.wait_ge(folded, j + 1)
                dve.tensor_copy(out.rearrange("p (g j c) -> p j g c", j=4, c=CC)[:, j, :, :],
                                k.ps[:, j, 0:4 * CC].rearrange("p (g c) -> p g c", c=CC)).then_inc(taken, 1)


def route(nc, k, logits, w):
    E = 8
    with ExitStack() as ctx:
        sb = lambda name, shape: k.sb(name, shape, F32, ctx)
        m, p, s, r = sb("rm", [P, NT]), sb("rp", [P, NT, E]), sb("rs", [P, NT]), sb("rr", [P, NT])
        beat, rank = sb("beat", [P, NT, E]), sb("rank", [P, NT, E])
        dve_step, exped = sems(nc, ctx, "dve_step", "exped")
        wide = lambda ap, n: ap.rearrange("p (t a) -> p t a", a=1).broadcast_to([P, NT, n])
        block = ctx.enter_context(nc.Block())

        @block.vector
        def _(dve):
            steps = [
                lambda: dve.tensor_reduce(m[:], logits, AX_X, ALU.max),
                lambda: dve.tensor_tensor(p[:], logits, wide(m[:], E), ALU.subtract),
                lambda: dve.tensor_reduce(s[:], p[:], AX_X, ALU.add),
                lambda: dve.reciprocal(r[:], s[:]),
                lambda: dve.tensor_tensor(p[:], p[:], wide(r[:], E), ALU.mult),
                lambda: dve.memset(rank[:], 0.0),
            ]
            for j in range(E):
                if j:
                    steps.append(lambda j=j: dve.tensor_tensor(
                        beat[:, :, 0:j], p[:, :, j:j + 1].broadcast_to([P, NT, j]), p[:, :, 0:j], ALU.is_gt))
                if j < E - 1:
                    steps.append(lambda j=j: dve.tensor_tensor(
                        beat[:, :, j + 1:E], p[:, :, j:j + 1].broadcast_to([P, NT, E - 1 - j]), p[:, :, j + 1:E],
                        ALU.is_ge))
                steps.append(lambda j=j: dve.memset(beat[:, :, j:j + 1], 0.0))
                steps.append(lambda: dve.tensor_tensor(rank[:], rank[:], beat[:], ALU.add))
            steps.append(lambda: dve.scalar_tensor_tensor(out=w, in0=rank[:], scalar=2.0, in1=p[:], op0=ALU.is_lt,
                                                          op1=ALU.mult))
            for i, step in enumerate(steps):
                if i == 2:
                    dve.wait_ge(exped, 1)
                step().then_inc(dve_step, 1)
                dve.wait_ge(dve_step, i + 1)

        @block.scalar
        def _(act):
            act.wait_ge(dve_step, 2)
            act.activation(p[:], p[:], ACT.Exp).then_inc(exped, 1)


def experts(nc, k, hid_t, w2, w):
    with ExitStack() as ctx:
        summed, added = sems(nc, ctx, "summed", "added")
        block = ctx.enter_context(nc.Block())

        @block.tensor
        def _(pe):
            for t in range(NT):
                if t >= 4:
                    pe.wait_ge(added, 8 * (t - 3))
                for f in range(2):
                    ins = pe.matmul(k.ps[:, 2 * (t % 4) + f, :], hid_t[:, P * t:P * t + P],
                                    w2[:, 4 * f:4 * f + 4, :].rearrange("p e c -> p (e c)"), start=True, stop=True)
                ins.then_inc(summed, 1)

        @block.vector
        def _(dve):
            for t in range(NT):
                dve.wait_ge(summed, t + 1)
                for e in range(8):
                    if e:
                        dve.wait_ge(added, 8 * t + e)
                    dve.scalar_tensor_tensor(
                        out=k.x[:, t, :], in0=k.ps[:, 2 * (t % 4) + e // 4, C * (e % 4):C * (e % 4) + C],
                        scalar=w[:, t, e:e + 1], in1=k.x[:, t, :], op0=ALU.mult, op1=ALU.add).then_inc(added, 1)


def residual(k):
    return dict(out=lambda ts: k.x[:, ts, :], add=lambda ts: k.x[:, ts, :])


def normalized_t(nc, k, src, xn, dsts):
    normalize(nc, k, src, xn)
    transpose(nc, k, lambda t: xn[:, t, :], C, dsts)


def tile_of(xt):
    return lambda t: xt[:, P * t:P * t + P]


def layer0(nc, k, a, xn):
    with ExitStack() as c0:
        sb = lambda name, shape, dt=F32: k.sb(name, shape, dt, c0)
        xt, y, y2 = sb("xt", [P, TOK]), sb("y", [P, NT, C]), sb("y2", [P, NT, C])
        normalized_t(nc, k, k.x, xn, [(xt, None, None)])
        with ExitStack() as ctx:
            sb1 = lambda name, shape, dt=F32: k.sb(name, shape, dt, ctx)
            wq, wk, wv = sb1("wq_pad", [P, H * 32]), sb1("wk_pad", [P, H * 32]), sb1("wv_pad", [P, H * 9])
            qb, kb, vb = sb1("qb", [P, 4]), sb1("kb", [P, 4]), sb1("vb", [1, H * 9])
            load(nc, [(wq[:], a["l0_wq"]), (wk[:], a["l0_wk"]), (wv[:], a["l0_wv"]), (qb[:], a["l0_bq"]),
                      (kb[:], a["l0_bk"]), (vb[:], a["l0_bv"])])
            self_attention(nc, k, 8, 32, True, float(1.0 / np.sqrt(8)), xt, xt, wq[:], wk[:], wv[:], qb, kb, vb[:], y)
        with ExitStack() as ctx:
            sb1 = lambda name, shape, dt=F32: k.sb(name, shape, dt, ctx)
            w0, wk, wv = sb1("wcq", [P, C]), sb1("wck", [R, C]), sb1("wcv", [R, H * 9])
            bcq = sb1("bcq", [1, C])
            qtok = sb1("qtok_all", [P, NT, H * SLOT], BF16)
            load(nc, [(w0[:], a["L0_xattn_Wcq"]), (wk[:], a["l0_wck"]), (wv[:], a["l0_wcv"]),
                      (bcq[:], vec_row(a["L0_xattn_bcq"]))])
            linear_tokens(nc, k, C, [(tile_of(xt), w0[:])], bcq[:], lambda ts: y2[:, ts, :])
            split_queries(nc, k, y2[:], qtok)
            cross_attention(nc, k, True, H, 8, float(1.0 / np.sqrt(8)), a["ctx_t"], qtok, None, wk[:], wv[:], y2)
        w, b = sb("wp", [P, C]), sb("bp", [1, C])
        load(nc, [(w[:], a["L0_xattn_Wp"]), (b[:], vec_row(a["L0_xattn_bp"]))])
        add_tokens(nc, y[:], y[:], y2[:])
        transpose(nc, k, lambda t: y[:, t, :], C, [(xt, None, None)])
        linear_tokens(nc, k, C, [(tile_of(xt), w[:])], b[:], **residual(k))
        wa, wb, wf, bf = sb("lora_a", [P, 16]), sb("lora_b", [16, C]), sb("w_int4", [P, C]), sb("bf", [1, C])
        at = sb("xa_t", [16, TOK])
        load(nc, [(wa[:], a["L0_ffn_a"]), (wb[:], a["L0_ffn_b"]), (wf[:], a["L0_ffn_kernel"]),
                  (bf[:], vec_row(a["L0_ffn_bias"]))])
        quantize_weight(nc, k, wf[:], False, 1.0 / 7.0, 0.0, -8.0, 7.0, True)
        normalized_t(nc, k, k.x, xn, [(xt, None, None)])
        linear_channels(nc, k, [(wa[:], xt, at, None, 16)], ACT.Copy)
        linear_tokens(nc, k, C, [(tile_of(xt), wf[:]), (tile_of(at), wb[:])], bf[:], **residual(k))


def mha_end(nc, k, a, p, x, y, xn, xt, big, xo):
    with ExitStack() as ctx:
        sb = lambda name, shape: k.sb(name, shape, F32, ctx)
        w1, w2, w3 = sb("li1", [P, 4, C]), sb("li2", [P, 4 * C]), sb("li3", [P, 4, C])
        b1, b2, b3, g, b = sb("b1", [1, C]), sb("b2", [P, 4]), sb("b3", [1, C]), sb("g", [P, 1]), sb("b", [P, 1])
        load(nc, [(w1[:], a[p + "li1_w"].rearrange("(j p) c -> p j c", p=P)), (w2[:], a[p + "li2_w"]),
                  (w3[:], a[p + "li3_w"].rearrange("(j p) c -> p j c", p=P)), (b1[:], vec_row(a[p + "li1_b"])),
                  (b2[:], a[p + "li2_b_cols"]), (b3[:], vec_row(a[p + "li3_b"])), (g[:], vec_col(a[p + "ln3_g"])),
                  (b[:], vec_col(a[p + "ln3_b"]))])
        for j in range(4):
            transpose(nc, k, lambda t: y[:, t, C * j:C * j + C], C, [(big[:, j, :], None, None)])
        linear_tokens(nc, k, C, [(tile_of(big[:, j, :]), w1[:, j, :]) for j in range(4)], b1[:],
                      lambda ts: xo[:, ts, :], lambda ts: x[:, ts, :])
        normalized_t(nc, k, xo, xn, [(xt, g[:], b[:])])
        linear_channels(nc, k, [(w2[:, C * j:C * j + C], xt, big[:, j, :], b2[:, j:j + 1], P) for j in range(4)],
                        ACT.Gelu)
        linear_tokens(nc, k, C, [(tile_of(big[:, j, :]), w3[:, j, :]) for j in range(4)], b3[:],
                      lambda ts: xo[:, ts, :], lambda ts: xo[:, ts, :])


def layer1(nc, k, a, xn):
    p = "L1_xattn_"
    d = 32
    scale = float(d ** -0.5)
    with ExitStack() as c0:
        sb = lambda name, shape, dt=F32: k.sb(name, shape, dt, c0)
        x1, x2 = sb("x1", [P, NT, C]), sb("x2", [P, NT, C])
        xt, y, gb = sb("xt", [P, TOK]), sb("y", [P, NT, H * d]), sb("gb", [P, 2 * C])
        rows, cols = sb("ln_rows", [1, 4, C]), sb("ln_cols", [P, 6])
        ccols = sb("ctx_cols", [CC, 2])
        load(nc, [(rows[:, i, :], vec_row(a[p + n])) for i, n in enumerate(("ln1_g", "ln1_b", "ln2_g", "ln2_b"))] +
             [(cols[:, i:i + 1], vec_col(a[p + n])) for i, n in enumerate(
                 ("a1_lnx_g", "a1_lnx_b", "a1_lny_g", "a1_lny_b", "a2_lnx_g", "a2_lnx_b"))] +
             [(ccols[:, i:i + 1], vec_col(a[p + n])) for i, n in enumerate(("a2_lny_g", "a2_lny_b"))])
        normalize(nc, k, k.x, xn)
        normalize(nc, k, xn, xn)
        affine_rows(nc, k, xn[:], x1[:], rows[:, 0, :], rows[:, 1, :], gb)
        with ExitStack() as ctx:
            sb1 = lambda name, shape, dt=F32: k.sb(name, shape, dt, ctx)
            xkt = sb1("xkt", [P, TOK])
            wq, wk, wv = sb1("wq_pad", [P, H * 64]), sb1("wk_pad", [P, H * 64]), sb1("wv_pad", [P, H * 33])
            qb, kb, vb = sb1("qb", [P, 8]), sb1("kb", [P, 8]), sb1("vb", [1, H * 33])
            load(nc, [(wq[:], a["l1_wq"]), (wk[:], a["l1_wk"]), (wv[:], a["l1_wv"]), (qb[:], a["l1_qb"]),
                      (kb[:], a["l1_kb"])])
            clear(nc, (vb[:], 0.0))
            normalized_t(nc, k, x1, xn, [(xt, cols[:, 0:1], cols[:, 1:2]), (xkt, cols[:, 2:3], cols[:, 3:4])])
            self_attention(nc, k, d, 64, False, scale, xt, xkt, wq[:], wk[:], wv[:], qb, kb, vb[:], y)
        with ExitStack() as ctx:
            big = k.sb("big", [P, 4, TOK], F32, ctx)
            mha_end(nc, k, a, p + "a1_", x1, y, xn, xt, big, x2)
        add_tokens(nc, x2[:], x2[:], x1[:])
        normalize(nc, k, x2, xn)
        affine_rows(nc, k, xn[:], x1[:], rows[:, 2, :], rows[:, 3, :], gb)
        ctx_norm_t = nc.dram_tensor("ctx_norm_t", (B, CC, LC), F32, kind="Internal").ap()
        normalize_context(nc, k, a["ctx_512"], ccols[:, 0:1], ccols[:, 1:2], ctx_norm_t)
        normalized_t(nc, k, x1, xn, [(xt, cols[:, 4:5], cols[:, 5:6])])
        with ExitStack() as ctx:
            sb1 = lambda name, shape, dt=F32: k.sb(name, shape, dt, ctx)
            wqk, wv = sb1("wqk", [P, H * CC]), sb1("wv2", [R, H * 33])
            wq_t, wk_t = sb1("wq_t", [P, 4, C]), sb1("wk_t", [P, 4, CC])
            load(nc, [(wq_t[:], a["l1_wq2_t"]), (wk_t[:], a["l1_wk2_t"]), (wv[:], a["l1_wv2"])])
            fold_keys(nc, k, wq_t, wk_t, wqk[:])
            cross_attention(nc, k, False, H, d, scale, ctx_norm_t, xt, wqk[:], None, wv[:], y)
        with ExitStack() as ctx:
            big = k.sb("big", [P, 4, TOK], F32, ctx)
            mha_end(nc, k, a, p + "a2_", x1, y, xn, xt, big, x2)
        add_tokens(nc, x2[:], x2[:], x1[:])
        add_tokens(nc, k.x[:], k.x[:], x2[:])
    with ExitStack() as c0:
        sb = lambda name, shape, dt=F32: k.sb(name, shape, dt, c0)
        xt, ht = sb("xt", [P, TOK]), sb("ht", [P, 4, TOK])
        w1, w2, b1, b2 = sb("w1", [P, 4 * C]), sb("w2", [P, 4 * C]), sb("b1", [P, 4]), sb("b2", [1, C])
        load(nc, [(w1[:], a["l1_w1_t"]), (w2[:].rearrange("p (j c) -> p j c", c=C),
                                          a["l1_w2_t"].rearrange("(j p) c -> p j c", p=P)),
                  (b1[:], a["l1_b1"]), (b2[:], vec_row(a["L1_ffn_b2"]))])
        for w in (w1, w2):
            quantize_weight(nc, k, w[:], True, 1.0 / (4 * C * C), EPS, -1.0, 1.0, False)
        normalized_t(nc, k, k.x, xn, [(xt, None, None)])
        linear_channels(nc, k, [(w1[:, C * j:C * j + C], xt, ht[:, j, :], b1[:, j:j + 1], P) for j in range(4)],
                        ACT.Relu)
        linear_tokens(nc, k, C, [(tile_of(ht[:, j, :]), w2[:, C * j:C * j + C]) for j in range(4)], b2[:],
                      **residual(k))


def layer2(nc, k, a, xn):
    with ExitStack() as c0:
        sb = lambda name, shape, dt=F32: k.sb(name, shape, dt, c0)
        xt, qt, yc = sb("xt", [P, TOK]), sb("qt", [P, TOK]), sb("yc", [P, NT, CC])
        wq, bq, wk, wv, bv = sb("wq", [P, C]), sb("bq", [P, 1]), sb("wk", [P, R]), sb("wv", [CC, C]), sb("bv", [1, C])
        load(nc, [(wq[:], a["L2_xattn_Wq"]), (bq[:], vec_col(a["L2_xattn_bq"])), (wk[:], a["l2_wk_t"]),
                  (wv[:], a["L2_xattn_Wv"]), (bv[:], vec_row(a["L2_xattn_bv"]))])
        normalized_t(nc, k, k.x, xn, [(xt, None, None)])
        linear_channels(nc, k, [(wq[:], xt, qt, bq[:], P)], ACT.Identity)
        cross_attention(nc, k, False, 1, CC, 1.0, a["ctx_t"], qt, wk[:], None, None, yc, a["ctx_512"])
        transpose(nc, k, lambda t: yc[:, t, :], CC, [(xt, None, None)])
        linear_tokens(nc, k, C, [(tile_of(xt[0:CC, :]), wv[:])], bv[:], **residual(k))
    with ExitStack() as c0:
        sb = lambda name, shape, dt=F32: k.sb(name, shape, dt, c0)
        xt, st, ht = sb("xt", [P, TOK]), sb("shared_t", [P, TOK]), sb("hid_t", [P, TOK])
        wi, wo, w1, w2 = sb("w_in", [P, 2 * C]), sb("w_out", [P, C]), sb("w1", [P, 2 * C]), sb("w2", [P, 8, C])
        wg, bg, lg, wd = sb("wg", [P, 8]), sb("bg", [1, 8]), sb("logits", [P, NT, 8]), sb("wdense", [P, NT, 8])
        load(nc, [(wi[:], a["L2_ffn_w_shared_in"]), (wo[:], a["L2_ffn_w_shared_out"]), (w1[:], a["L2_ffn_w1_shared"]),
                  (w2[:], a["L2_ffn_w2"].rearrange("e p c -> p e c")), (wg[:], a["L2_ffn_w_gate"]),
                  (bg[:], vec_row(a["L2_ffn_gate_bias"]))])
        normalized_t(nc, k, k.x, xn, [(xt, None, None)])
        linear_tokens(nc, k, 8, [(tile_of(xt), wg[:])], bg[:], lambda ts: lg[:, ts, :])
        route(nc, k, lg[:], wd[:])
        for w, o in ((wi, st), (w1, ht)):
            chunk = lambda i: xt[:, BANK * i:BANK * i + BANK]
            gated(nc, k, BANK, lambda i: w[:, 0:C], lambda i: w[:, C:2 * C], chunk, chunk,
                  [o[:, BANK * i:BANK * i + BANK] for i in range(4)])
        linear_tokens(nc, k, C, [(tile_of(st), wo[:])], None, **residual(k))
        experts(nc, k, ht, w2, wd)


def layer3(nc, k, a, xn):
    with ExitStack() as c0:
        sb = lambda name, shape, dt=F32: k.sb(name, shape, dt, c0)
        xt, y = sb("xt", [P, TOK]), sb("y", [P, NT, C])
        wq, wk, wv, wo = sb("wq", [P, C]), sb("wk", [R, C]), sb("wv", [R, H * 9]), sb("wo", [P, C])
        load(nc, [(wq[:], a["l3_wq_t"]), (wk[:], a["l3_wk_t"]), (wv[:], a["l3_wv_t"]), (wo[:], a["l3_wo_t"])])
        normalized_t(nc, k, k.x, xn, [(xt, None, None)])
        with ExitStack() as ctx:
            qtok = k.sb("qtok_all", [P, NT, H * SLOT], BF16, ctx)
            linear_tokens(nc, k, C, [(tile_of(xt), wq[:])], None, lambda ts: y[:, ts, :])
            split_queries(nc, k, y[:], qtok)
            cross_attention(nc, k, True, H, 8, float(8 ** -0.5), a["ctx_t"], qtok, None, wk[:], wv[:], y)
        transpose(nc, k, lambda t: y[:, t, :], C, [(xt, None, None)])
        linear_tokens(nc, k, C, [(tile_of(xt), wo[:])], None, **residual(k))
    with ExitStack() as c0:
        sb = lambda name, shape, dt=F32: k.sb(name, shape, dt, c0)
        I = 352
        rows = [(0, P), (P, 2 * P), (2 * P, I)]
        xt, h = sb("xt", [P, TOK]), sb("h", [P, NT, I])
        wg, wu, wd = sb("wg", [P, 3, C]), sb("wu", [P, 3, C]), sb("wd", [P, I])
        wgt, wut, wdt = sb("wgt", [P, I]), sb("wut", [P, I]), sb("wdt", [P, 3, C])
        clear(nc, (wg[:], 0.0), (wu[:], 0.0))
        load(nc, [(w[0:hi - lo, j, :], a[n][lo:hi, :]) for w, n in ((wg, "L3_ffn_w_gate"), (wu, "L3_ffn_w_up"))
                  for j, (lo, hi) in enumerate(rows)] + [(wd[:], a["L3_ffn_w_down"])])
        quantize_fp4(nc, k, wg[:].rearrange("p j (n e) -> p (j n) e", e=16), 24)
        quantize_fp4(nc, k, wu[:].rearrange("p j (n e) -> p (j n) e", e=16), 24)
        quantize_fp4(nc, k, wd[:].rearrange("p (n e) -> p n e", e=16), 22)
        transpose_weight(nc, k, [(w[0:hi - lo, j, :], wt[:, lo:hi]) for w, wt in ((wg, wgt), (wu, wut))
                                 for j, (lo, hi) in enumerate(rows)] +
                         [(wd[:, lo:hi], wdt[0:hi - lo, j, :]) for j, (lo, hi) in enumerate(rows)])
        normalize(nc, k, k.x, xn)
        quantize_fp4(nc, k, xn[:].rearrange("p t (n e) -> p (t n) e", e=16), NT * 8)
        transpose(nc, k, lambda t: xn[:, t, :], C, [(xt, None, None)])
        gated(nc, k, I, tile_of(xt), tile_of(xt), lambda i: wgt[:], lambda i: wut[:], [h[:, t, :] for t in range(NT)])
        quantize_fp4(nc, k, h[:].rearrange("p t (n e) -> p (t n) e", e=16), NT * 22)
        ht = sb("ht", [P, 3, TOK])
        for j, (lo, hi) in enumerate(rows):
            transpose(nc, k, lambda t: h[:, t, lo:hi], hi - lo, [(ht[:, j, :], None, None)])
        linear_tokens(nc, k, C, [(tile_of(ht[0:hi - lo, j, :]), wdt[0:hi - lo, j, :])
                                 for j, (lo, hi) in enumerate(rows)], None, **residual(k))


def network(nc, a, out):
    with ExitStack() as ctx:
        k = Chip(nc, ctx)
        tokens = lambda ap: ap.rearrange("b (t p) c -> p (b t) c", p=P)
        set_constants(nc, k)
        load(nc, [(k.x[:], tokens(a["x"]))])
        xn = k.sb("xn", [P, NT, C])
        for layer in (layer0, layer1, layer2, layer3):
            layer(nc, k, a, xn)
        load(nc, [(tokens(out), k.x[:])])


NATURAL = """x ctx_512 L0_xattn_Wcq L0_xattn_bcq L0_xattn_Wp L0_xattn_bp L0_ffn_kernel L0_ffn_bias L0_ffn_a L0_ffn_b
L1_xattn_ln1_g L1_xattn_ln1_b L1_xattn_ln2_g L1_xattn_ln2_b L1_xattn_a1_li1_w L1_xattn_a1_li1_b L1_xattn_a1_lnx_g
L1_xattn_a1_lnx_b L1_xattn_a1_lny_g L1_xattn_a1_lny_b L1_xattn_a1_ln3_g L1_xattn_a1_ln3_b L1_xattn_a1_li2_w
L1_xattn_a1_li3_w L1_xattn_a1_li3_b L1_xattn_a2_li1_w L1_xattn_a2_li1_b L1_xattn_a2_lnx_g L1_xattn_a2_lnx_b
L1_xattn_a2_lny_g L1_xattn_a2_lny_b L1_xattn_a2_ln3_g L1_xattn_a2_ln3_b L1_xattn_a2_li2_w L1_xattn_a2_li3_w
L1_xattn_a2_li3_b L1_ffn_b2 L2_xattn_Wq L2_xattn_bq L2_xattn_Wv L2_xattn_bv L2_ffn_w_shared_in
L2_ffn_w_shared_out L2_ffn_w1_shared L2_ffn_w2 L2_ffn_w_gate L2_ffn_gate_bias L3_ffn_w_gate L3_ffn_w_up
L3_ffn_w_down""".split()


def spaced(w, d, width, fill=0.0):
    w = np.asarray(w)
    w = w.reshape(w.shape[:-1] + (H, d))
    out = np.zeros(w.shape[:-1] + (width,), w.dtype)
    out[..., 0:d] = w
    if fill:
        out[..., d] = fill
    return out.reshape(w.shape[:-2] + (H * width,))


def columns(v):
    return np.asarray(v).reshape(-1, P).T


def with_row(w, row):
    return np.concatenate([np.asarray(w), np.asarray(row)[None]], 0)


def laid_out(inputs):
    i = {n: np.asarray(v) for n, v in inputs.items()}
    a = {n: i[n] for n in NATURAL}
    p = "L0_xattn_"
    a["l0_wq"], a["l0_wk"] = spaced(i[p + "Wq"], 8, 32), spaced(i[p + "Wk"], 8, 32)
    a["l0_bq"], a["l0_bk"] = columns(spaced(i[p + "bq"], 8, 32)), columns(spaced(i[p + "bk"], 8, 32, 1.0))
    a["l0_wv"], a["l0_bv"] = spaced(i[p + "Wv"], 8, 9), spaced(i[p + "bv"], 8, 9, 1.0)[None]
    a["ctx_t"] = i["ctx_512"].transpose(0, 2, 1)
    a["l0_wck"] = with_row(i[p + "Wck"], i[p + "bck"])
    a["l0_wcv"] = with_row(spaced(i[p + "Wcv"], 8, 9), spaced(i[p + "bcv"], 8, 9, 1.0))
    p = "L1_xattn_"
    heads = lambda w: i[p + w].transpose(1, 0, 2).reshape(i[p + w].shape[1], -1)
    none = np.zeros(H * 32, np.float32)
    a["l1_wq"], a["l1_wk"] = spaced(heads("a1_wq"), 32, 64), spaced(heads("a1_wk"), 32, 64)
    a["l1_qb"], a["l1_kb"] = columns(spaced(none, 32, 64)), columns(spaced(none, 32, 64, 1.0))
    a["l1_wv"] = spaced(heads("a1_wv"), 32, 33)
    a["l1_wv2"] = with_row(spaced(heads("a2_wv"), 32, 33), spaced(none, 32, 33, 1.0))
    a["l1_wq2_t"] = i[p + "a2_wq"].reshape(4, 4, C, 32).transpose(1, 3, 0, 2).reshape(P, 4, C)
    a["l1_wk2_t"] = i[p + "a2_wk"].reshape(4, 4, CC, 32).transpose(1, 3, 0, 2).reshape(P, 4, CC)
    for m in ("a1_", "a2_"):
        a[p + m + "li2_b_cols"] = columns(i[p + m + "li2_b"])
    a["l1_w1_t"], a["l1_w2_t"], a["l1_b1"] = i["L1_ffn_W1"].T, i["L1_ffn_W2"].T, columns(i["L1_ffn_b1"])
    a["l2_wk_t"] = np.concatenate([i["L2_xattn_Wk"].T, i["L2_xattn_bk"][:, None]], 1)
    kv = i["L3_xattn_Wkv"].T
    a["l3_wq_t"], a["l3_wo_t"] = i["L3_xattn_Wq"].T, i["L3_xattn_Wo"].T
    a["l3_wk_t"] = with_row(kv[:, 0:C], np.zeros(C, np.float32))
    a["l3_wv_t"] = with_row(spaced(kv[:, C:], 8, 9), spaced(np.zeros(C, np.float32), 8, 9, 1.0))
    return {n: np.ascontiguousarray(v) for n, v in a.items()}


def kernel(**inputs):
    import concourse.bacc as bacc
    from concourse.bass_utils import run_bass_kernel_spmd

    nc = bacc.Bacc("TRN2", target_bir_lowering=False, num_devices=1)
    arrays = laid_out(inputs)
    args = {n: nc.dram_tensor("in_" + n, v.shape, F32, kind="ExternalInput").ap() for n, v in arrays.items()}
    out = nc.dram_tensor("out_0_dram", (B, S, C), F32, kind="ExternalOutput").ap()
    network(nc, args, out)
    result = run_bass_kernel_spmd(nc, [{"in_" + n: v for n, v in arrays.items()}], core_ids=[0])
    return result.results[0]["out_0_dram"]
```

```python
from contextlib import ExitStack

import numpy as np

import concourse.bass as bass
from concourse import mybir

F32 = mybir.dt.float32
BF16 = mybir.dt.bfloat16
ALU = mybir.AluOpType
ACT = mybir.ActivationFunctionType
AX_X = mybir.AxisListType.X
RMAX = bass.bass_isa.ReduceOp.max
RADD = bass.bass_isa.ReduceOp.add

P = 128
B = 8
S = 256
QT = S // P
NT = B * QT
TOK = B * S
C = 128
CC = 64
LC = 1601
KT = -(-LC // P)
LCP = KT * P
H = 16
EPS = 1e-5
MASKED = -1e30
BANK = 512
START = 1


class Chip:

    def __init__(self, nc, ctx):
        self.nc = nc
        self.ctx = ctx
        self.made = 0
        sb = self.sb
        self.x = sb("x_res", [P, NT, C])
        self.ps = ctx.enter_context(nc.psum_tensor("ps", [P, 8, BANK], F32))
        self.ident = sb("ident", [P, P])
        self.identb = sb("identb", [P, P], BF16)
        self.ones = sb("ones_row", [1, P])
        self.mhalf = sb("mhalf", [P, NT])
        self.stats = sb("bn_stats_t", [P, NT, 6])
        self.mv = sb("mean_var", [P, NT, 2])
        self.ve = sb("var_eps", [P, NT])
        self.rstd = sb("rstd", [P, NT])

    def sb(self, name, shape, dt=F32, ctx=None):
        self.made += 1
        return (ctx or self.ctx).enter_context(self.nc.sbuf_tensor(f"{name}_{self.made}", shape, dt))


def sems(nc, ctx, *names, start=0):
    made = [ctx.enter_context(nc.semaphore(n)) for n in names]
    if start:
        for s in made:
            nc.gpsimd.sem_inc(s, start)

    def clear_all():
        nums = sorted(s.num for s in made)
        while nums:
            n = 1
            while n < len(nums) and nums[n] == nums[0] + n:
                n += 1
            nc.gpsimd.sem_clear(range(nums[0], nums[0] + n))
            nums = nums[n:]

    ctx.callback(clear_all)
    return made




def load(nc, pairs):
    with ExitStack() as ctx:
        sp_loaded, act_loaded = sems(nc, ctx, "sp_loaded", "act_loaded")
        block = ctx.enter_context(nc.Block())
        sp_pairs, act_pairs = pairs[0::2], pairs[1::2]

        @block.sync
        def _(sp):
            for dst, src in sp_pairs:
                sp.dma_start(dst, src).then_inc(sp_loaded, 16)
            sp.wait_ge(sp_loaded, 16 * len(sp_pairs))

        @block.scalar
        def _(act):
            for dst, src in act_pairs:
                act.dma_start(dst, src).then_inc(act_loaded, 16)
            if act_pairs:
                act.wait_ge(act_loaded, 16 * len(act_pairs))


def step_past(eng, passed):
    eng.sem_inc(passed, 1)


def set_constants(nc, k):
    with ExitStack() as ctx:
        zeroed, done = sems(nc, ctx, "zeroed", "consts_done")
        block = ctx.enter_context(nc.Block())

        @block.gpsimd
        def _(pool):
            pool.memset(k.ident[:], 0.0).then_inc(zeroed, 1)
            pool.memset(k.ones[:], 1.0)
            pool.memset(k.mhalf[:], -0.5)
            pool.wait_ge(zeroed, 1)
            pool.affine_select(out=k.ident[:], in_=k.ident[:], compare_op=ALU.not_equal, fill=1.0,
                               base=0, pattern=[[-1, P]], channel_multiplier=1).then_inc(done, 1)
            pool.wait_ge(done, 1)
            pool.tensor_copy(k.identb[:], k.ident[:]).then_inc(done, 1)


def normalize(nc, k, src, dst, turns=()):
    n, c = NT, C
    with ExitStack() as ctx:
        stats_done, aggr_done, var_ready, rstd_ready, normed, turned, taken = sems(
            nc, ctx, "stats_done", "aggr_done", "var_ready", "rstd_ready", "normed", "turned", "taken")
        block = ctx.enter_context(nc.Block())

        @block.vector
        def _(dve):
            for t in range(n):
                dve.bn_stats(k.stats[:, t, :], src[:, t, 0:c]).then_inc(stats_done, 1)
            for t in range(n):
                dve.wait_ge(stats_done, t + 1)
                dve.bn_aggr(k.mv[:, t, :], k.stats[:, t, :]).then_inc(aggr_done, 1)
            dve.wait_ge(aggr_done, n)
            dve.tensor_scalar(k.ve[:, 0:n], k.mv[:, 0:n, 1], EPS, None, ALU.add).then_inc(var_ready, 1)
            dve.wait_ge(rstd_ready, 1)
            for t in range(n):
                dve.tensor_scalar(dst[:, t, 0:c], src[:, t, 0:c], k.mv[:, t, 0:1], k.rstd[:, t:t + 1],
                                  ALU.subtract, ALU.mult).then_inc(normed, 1)

        @block.gpsimd
        def _(pool):
            pool.wait_ge(var_ready, 1)
            pool.tensor_tensor(k.rstd[:, 0:n], k.ve[:, 0:n], k.mhalf[:, 0:n], ALU.pow).then_inc(rstd_ready, 1)

        if turns:
            @block.tensor
            def _(pe):
                for q in range(NT // 4):
                    pe.wait_ge(normed, 4 * q + 4)
                    for i in range(4):
                        ins = pe.transpose(k.ps[:, q, P * i:P * i + P], dst[:, 4 * q + i, :], k.ident[:])
                    ins.then_inc(turned, 1)

            @block.scalar
            def _(act):
                for q in range(NT // 4):
                    act.wait_ge(turned, q + 1)
                    for out, g, b in turns:
                        o = out[:, BANK * q:BANK * q + BANK]
                        if g is None:
                            act.activation(o, k.ps[:, q, :], ACT.Copy).then_inc(taken, 1)
                        else:
                            act.activation(o, k.ps[:, q, :], ACT.Identity, scale=g, bias=b).then_inc(taken, 1)


def transpose(nc, k, src, c, dsts):
    with ExitStack() as ctx:
        turned, taken = sems(nc, ctx, "turned", "taken")
        block = ctx.enter_context(nc.Block())

        @block.tensor
        def _(pe):
            for q in range(NT // 4):
                for i in range(4):
                    ins = pe.transpose(k.ps[0:c, q, P * i:P * i + P], src(4 * q + i), k.ident[:])
                ins.then_inc(turned, 1)

        @block.scalar
        def _(act):
            for q in range(NT // 4):
                act.wait_ge(turned, q + 1)
                for dst, g, b in dsts:
                    out = dst[0:c, BANK * q:BANK * q + BANK]
                    if g is None:
                        act.activation(out, k.ps[0:c, q, :], ACT.Copy).then_inc(taken, 1)
                    else:
                        act.activation(out, k.ps[0:c, q, :], ACT.Identity, scale=g, bias=b).then_inc(taken, 1)


def linear_tokens(nc, k, n, terms, bias, out, add=None):
    per = max(1, BANK // n) if n == C else 1
    groups = NT // per
    with ExitStack() as ctx:
        summed, drained = sems(nc, ctx, "summed", "drained")
        block = ctx.enter_context(nc.Block())

        @block.tensor
        def _(pe):
            for g in range(groups):
                if g >= 4:
                    pe.wait_ge(drained, g - 3)
                for i in range(per):
                    t = per * g + i
                    o = k.ps[:, g % 4, n * i:n * i + n]
                    for j, (lhs, rhs) in enumerate(terms):
                        ins = pe.matmul(o, lhs(t), rhs, start=(j == 0), stop=(bias is None and j == len(terms) - 1))
                    if bias is not None:
                        ins = pe.matmul(o, k.ones[:], bias, start=False, stop=True)
                ins.then_inc(summed, 1)

        @block.vector
        def _(dve):
            for g in range(groups):
                dve.wait_ge(summed, g + 1)
                src = k.ps[:, g % 4, 0:n * per].rearrange("p (t n) -> p t n", n=n)
                tiles = slice(per * g, per * g + per)
                if add is None:
                    dve.tensor_copy(out(tiles), src).then_inc(drained, 1)
                else:
                    dve.tensor_tensor(out(tiles), src, add(tiles), ALU.add).then_inc(drained, 1)


def linear_channels(nc, k, blocks, func):
    with ExitStack() as ctx:
        summed, drained = sems(nc, ctx, "summed", "drained")
        block = ctx.enter_context(nc.Block())

        @block.tensor
        def _(pe):
            for u in range(4 * len(blocks)):
                lhs, xt, _, _, rows = blocks[u // 4]
                if u >= 8:
                    pe.wait_ge(drained, u - 7)
                cols = slice(BANK * (u % 4), BANK * (u % 4) + BANK)
                pe.matmul(k.ps[0:rows, u % 8, :], lhs, xt[:, cols], start=True, stop=True).then_inc(summed, 1)

        @block.scalar
        def _(act):
            for u in range(4 * len(blocks)):
                _, _, out, bias, rows = blocks[u // 4]
                act.wait_ge(summed, u + 1)
                cols = slice(BANK * (u % 4), BANK * (u % 4) + BANK)
                if bias is None:
                    act.activation(out[:, cols], k.ps[0:rows, u % 8, :], func).then_inc(drained, 1)
                else:
                    act.activation(out[:, cols], k.ps[0:rows, u % 8, :], func, bias=bias).then_inc(drained, 1)


def affine_rows(nc, k, src, dst, g_row, b_row, gb):
    with ExitStack() as ctx:
        spread, copied, scaled, done = sems(nc, ctx, "spread", "copied", "scaled", "affine_done")
        block = ctx.enter_context(nc.Block())

        @block.tensor
        def _(pe):
            pe.matmul(k.ps[:, 0, 0:C], k.ones[:], g_row, start=True, stop=True)
            pe.matmul(k.ps[:, 0, C:2 * C], k.ones[:], b_row, start=True, stop=True).then_inc(spread, 1)

        @block.vector
        def _(dve):
            dve.wait_ge(spread, 1)
            dve.tensor_copy(gb[:], k.ps[:, 0, 0:2 * C]).then_inc(copied, 1)
            dve.wait_ge(copied, 1)
            g = gb[:, 0:C].rearrange("p (t c) -> p t c", t=1).broadcast_to([P, NT, C])
            b = gb[:, C:2 * C].rearrange("p (t c) -> p t c", t=1).broadcast_to([P, NT, C])
            dve.tensor_tensor(dst, src, g, ALU.mult).then_inc(scaled, 1)
            dve.wait_ge(scaled, 1)
            dve.tensor_tensor(dst, dst, b, ALU.add).then_inc(done, 1)


def add_tokens(nc, out, a, b):
    with ExitStack() as ctx:
        (done,) = sems(nc, ctx, "add_done")
        block = ctx.enter_context(nc.Block())

        @block.vector
        def _(dve):
            dve.tensor_tensor(out, a, b, ALU.add).then_inc(done, 1)




def self_attention(nc, k, d, w, causal, scale, xq, xk, wq, wk, wv, qb, kb, vb, y):
    hb = P // w
    nb = H // hb
    vw = d + 1
    half = H * vw // 2
    keys = S + P if causal else 2 * S
    plan = [("project", 0)]
    for u in range(4):
        plan.append(("values", u))
    late = []
    for s in range(nb + 2):
        for j in range(hb):
            h = (s - 2) * hb + j
            if j == 1:
                if 1 <= s <= nb:
                    plan.append(("max_turn", s - 1))
                if s < nb - 1:
                    plan.append(("project", s + 1))
            if s >= 2:
                plan.append(("scores", h))
            if s < nb:
                plan.append(("maxima", s * hb + j))
            if late:
                plan.append(late.pop(0))
            if s >= 2 and h >= 1:
                plan.append(("mask", h - 1))
                if h % hb == 0:
                    plan += [("weigh", h // hb - 1), ("take", h // hb - 1)]
                    late = [("turn", h // hb - 1)]
    plan += late + [("mask", H - 1), ("weigh", nb - 1), ("take", nb - 1), ("turn", nb - 1)]
    ring_steps = [s for s in plan if s[0] in ("project", "maxima", "max_turn")]
    use = {s: n for n, s in enumerate(ring_steps)}
    per = len(ring_steps)
    assert per % 2 == 0

    with ExitStack() as ctx:
        def sb(name, shape, dt=F32):
            return k.sb(name, shape, dt, ctx)

        xqb, xkb = sb("xqb", [P, S]), sb("xkb", [P, S])
        v = sb("v_cur", [P, 2, H * vw])
        q1, q2, kk = sb("q1", [P, nb, hb, S]), sb("q2", [P, nb, hb, S]), sb("kk", [P, nb, S])
        mpad = sb("mpad", [P, 2, 2, P])
        pr = sb("probs", [P, 2 * hb, keys])
        pm = None if causal else sb("probs_masked", [P, 2 * hb, 3 * P])
        ot = sb("ot", [P, S])
        rden = sb("rden", [P, 2, hb])
        mask = sb("mask", [P, 3 * P])
        maskb, maskb_t = sb("maskb", [P, P], BF16), sb("maskb_t", [P, P], BF16)
        ones_col = sb("ones_col", [P, vw])
        cleared, set_up, masks, batch_in, v_full, v_free, ring_full, free0, free1 = sems(
            nc, ctx, "cleared", "set_up", "masks", "batch_in", "v_full", "v_free", "ring_full", "ring_free0",
            "ring_free1",
            start=START)
        s_full, exp_done, masked, pv_done, o_free, y_full, y_free, rden_ready, max_half, q_half, q2_part, y_half, \
            passed = sems(
            nc, ctx, "s_full", "exp_done", "masked", "pv_done", "o_free", "y_full", "y_free", "rden_ready",
            "max_half", "q_half", "q2_part", "y_half", "passed", start=START)
        ring_free = [free0, free1]

        def ring(step):
            return k.ps[:, use[step] % 2, :]

        def wait_ring_reuse(pe, b, step):
            u = use[step]
            pe.wait_ge(ring_free[u % 2], START + b * (per // 2) + u // 2)

        def wait_consumed(eng, b, step):
            u = use[step]
            eng.wait_ge(ring_free[u % 2], START + b * (per // 2) + u // 2 + 1)

        def wait_ring(pe, b, step, *consumed):
            wait_ring_reuse(pe, b, step)
            for other in consumed:
                if use[other] % 2 != use[step] % 2:
                    wait_consumed(pe, b, other)

        def wait_produced(eng, b, step):
            eng.wait_ge(ring_full, START + b * per + use[step] + 1)

        obank, ybank = k.ps[:, 4, 0:S], k.ps[:, 5, 0:S]
        block = ctx.enter_context(nc.Block())

        @block.gpsimd
        def _(pool):
            pool.memset(mpad[:], 0.0).then_inc(set_up, 1)
            pool.memset(ones_col[:], 0.0).then_inc(set_up, 1)
            pool.memset(mask[:], 1.0).then_inc(set_up, 1)
            pool.memset(maskb[:], 0.0).then_inc(set_up, 1)
            pool.memset(maskb_t[:], 0.0).then_inc(set_up, 1)
            pool.wait_ge(set_up, START + 5)
            pool.memset(ones_col[:, d:d + 1], 1.0).then_inc(masks, 1)
            pool.affine_select(out=maskb[:], in_=maskb[:], compare_op=ALU.is_ge, fill=MASKED, base=0,
                               pattern=[[-1, P]], channel_multiplier=1).then_inc(masks, 1)
            pool.affine_select(out=maskb_t[:], in_=maskb_t[:], compare_op=ALU.is_ge, fill=MASKED, base=0,
                               pattern=[[1, P]], channel_multiplier=-1).then_inc(masks, 1)
            for sq in (mask[:, 0:P], mask[:, 2 * P:3 * P]):
                pool.affine_select(out=sq, in_=sq, compare_op=ALU.is_gt, fill=0.0, base=0,
                                   pattern=[[-1, P]], channel_multiplier=1).then_inc(masks, 1)

            def bring(b):
                pool.tensor_copy(xqb[:], xq[:, bass.ds(S * b, S)]).then_inc(batch_in, 1)
                pool.tensor_copy(xkb[:], xk[:, bass.ds(S * b, S)]).then_inc(batch_in, 1)

            bring(0)
            with pool.Fori(1, B) as b:
                pool.wait_ge(ring_full, START + (b - 1) * per + use[("project", nb - 1)] + 1)
                step_past(pool, passed)
                bring(b)

        @block.tensor
        def _(pe):
            pe.wait_ge(masks, START + 5)
            pe.wait_ge(cleared, START + 2)
            pe.wait_ge(o_free, START + 1)
            with pe.Fori(0, B) as b:
                for step in plan:
                    kind, n = step
                    if kind == "values":
                        kt, hf = n // 2, n % 2
                        pe.wait_ge(batch_in, START + 2 * b + 2)
                        pe.wait_ge(v_free, START + 4 * b + max(n - 1, 0))
                        o = k.ps[:, 6 + n % 2, 0:half]
                        pe.matmul(o, xkb[:, P * kt:P * kt + P], wv[:, half * hf:half * hf + half],
                                  start=True, stop=False)
                        pe.matmul(o, k.ones[:], vb[:, half * hf:half * hf + half],
                                  start=False, stop=True).then_inc(v_full, 1)
                    elif kind == "project":
                        pe.wait_ge(batch_in, START + 2 * b + 2)
                        wait_ring_reuse(pe, b, step)
                        pe.matmul(ring(step)[:, 0:S], wq[:, P * n:P * n + P], xqb[:], start=True, stop=True)
                        pe.matmul(ring(step)[:, S:2 * S], wk[:, P * n:P * n + P], xkb[:],
                                  start=True, stop=True).then_inc(ring_full, 1)
                    elif kind == "maxima":
                        g, j = n // hb, n % hb
                        wait_ring(pe, b, step, ("project", g))
                        for qt in range(2):
                            nk = P * (qt + 1) if causal else S
                            ins = pe.matmul(ring(step)[:, S * qt:S * qt + nk], q1[:, g, j, P * qt:P * qt + P],
                                            kk[:, g, 0:nk], start=True, stop=True)
                            if causal:
                                ins = pe.matmul(ring(step)[:, S * qt + nk - P:S * qt + nk], k.identb[:],
                                                maskb[:], start=False, stop=True, skip_group_check=True)
                        ins.then_inc(ring_full, 1)
                    elif kind == "max_turn":
                        wait_ring(pe, b, step, ("maxima", hb * n + hb - 2), ("maxima", hb * n + hb - 1))
                        for qt in range(2):
                            ins = pe.transpose(ring(step)[:, P * qt:P * qt + P], mpad[:, n % 2, qt, :], k.ident[:])
                        ins.then_inc(ring_full, 1)
                    elif kind == "scores":
                        g, j = n // hb, n % hb
                        wait_consumed(pe, b, ("max_turn", g))
                        pe.wait_ge(exp_done, START + H * b + max(n - 1, 0))
                        o = k.ps[:, 2 + n % 2, :]
                        pe.matmul(o[:, 0:S], kk[:, g, 0:P], q2[:, g, j, :], start=True, stop=True)
                        if causal:
                            pe.matmul(o[:, 0:P], k.identb[:], maskb_t[:], start=False, stop=True, skip_group_check=True)
                            pe.matmul(o[:, S:S + P], kk[:, g, P:S], q2[:, g, j, P:S],
                                      start=True, stop=True)
                            pe.matmul(o[:, S:S + P], k.identb[:], maskb_t[:],
                                      start=False, stop=True, skip_group_check=True).then_inc(s_full, 1)
                        else:
                            pe.matmul(o[:, S:2 * S], kk[:, g, P:S], q2[:, g, j, :],
                                      start=True, stop=True).then_inc(s_full, 1)
                    elif kind == "weigh":
                        if n == 0:
                            pe.wait_ge(v_free, START + 4 * b + 4)
                        pe.wait_ge(o_free, START + nb * b + n + 1)
                        pe.wait_ge(exp_done, START + H * b + hb * (n + 1))
                        heads = [(obank[w * j:w * j + vw, :], slice(vw * h, vw * h + vw), h % (2 * hb))
                                 for j, h in enumerate(range(hb * n, hb * n + hb))]
                        if causal:
                            for o, vh, i in heads:
                                pe.matmul(o, v[:, 0, vh], pr[:, i, 0:S], start=True, stop=True)
                            for o, vh, i in heads:
                                ins = pe.matmul(o[:, P:S], v[:, 1, vh], pr[:, i, S:S + P],
                                                start=False, stop=True, skip_group_check=True)
                        else:
                            for o, vh, i in heads:
                                pe.matmul(o, ones_col[:], pr[:, i, 0:S], start=True, stop=True)
                            for o, vh, i in heads:
                                pe.matmul(o, ones_col[:], pr[:, i, S:2 * S], start=False, stop=True,
                                          skip_group_check=True)
                            pe.wait_ge(masked, START + 2 * (H * b + hb * (n + 1)))
                            for o, vh, i in heads:
                                pe.matmul(o[:, 0:P], v[:, 0, vh], pm[:, i, 0:P], start=False, stop=True,
                                          skip_group_check=True)
                            for o, vh, i in heads:
                                ins = pe.matmul(o, v[:, 1, vh], pm[:, i, P:3 * P], start=False, stop=True,
                                                skip_group_check=True)
                        ins.then_inc(pv_done, 1)
                    elif kind == "turn":
                        pe.wait_ge(o_free, START + nb * b + n + 2)
                        pe.wait_ge(y_free, START + nb * b + n)
                        for qt in range(2):
                            ins = pe.transpose(ybank[:, P * qt:P * qt + P], ot[:, P * qt:P * qt + P], k.ident[:])
                        ins.then_inc(y_full, 1)

        @block.scalar
        def _(act):
            act.wait_ge(cleared, START + 2)
            with act.Fori(0, B) as b:
                for step in plan:
                    kind, n = step
                    if kind == "values":
                        kt, hf = n // 2, n % 2
                        act.wait_ge(v_full, START + 4 * b + n + 1)
                        act.activation(v[:, kt, half * hf:half * hf + half], k.ps[:, 6 + n % 2, 0:half],
                                       ACT.Copy).then_inc(v_free, 1)
                    elif kind == "project":
                        wait_produced(act, b, step)
                        for j in range(hb):
                            r = slice(w * j, w * j + w)
                            act.activation(q1[r, n, j, :], ring(step)[r, 0:S], ACT.Identity,
                                           bias=qb[r, n:n + 1]).then_inc(q_half, 1)
                        act.activation(kk[:, n, :], ring(step)[:, S:2 * S], ACT.Identity,
                                       bias=kb[:, n:n + 1]).then_inc(ring_free[use[step] % 2], 1)
                    elif kind == "scores":
                        act.wait_ge(s_full, START + H * b + n + 1)
                        act.wait_ge(pv_done, START + nb * b + max(n // hb - 1, 0))
                        act.activation(pr[:, n % (2 * hb), :], k.ps[:, 2 + n % 2, 0:keys], ACT.Exp,
                                       scale=scale).then_inc(exp_done, 1)

        @block.vector
        def _(dve):
            dve.memset(q1[:], 0.0).then_inc(cleared, 1)
            dve.memset(q2[:], 0.0).then_inc(cleared, 1)
            dve.memset(obank, 0.0).then_inc(o_free, 1)
            with dve.Fori(0, B) as b:
                for step in plan:
                    kind, n = step
                    if kind == "maxima":
                        g, col = n // hb, w * (n % hb) + d
                        wait_produced(dve, b, step)
                        free = ring_free[use[step] % 2]
                        if causal:
                            dve.tensor_reduce(mpad[:, g % 2, 0, col:col + 1], ring(step)[:, 0:P], AX_X, ALU.max,
                                              negate=True).then_inc(max_half, 1)
                            dve.tensor_reduce(mpad[:, g % 2, 1, col:col + 1], ring(step)[:, S:2 * S], AX_X,
                                              ALU.max, negate=True).then_inc(free, 1)
                        else:
                            dve.tensor_reduce(mpad[:, g % 2, :, col], ring(step).rearrange("p (q n) -> p q n", q=2),
                                              AX_X, ALU.max, negate=True).then_inc(free, 1)
                    elif kind == "max_turn":
                        wait_produced(dve, b, step)
                        for j in range(hb):
                            r = slice(w * j, w * j + w)
                            done = q2_part if j < hb - 1 else ring_free[use[step] % 2]
                            dve.tensor_tensor(q2[r, n, j, :], ring(step)[r, 0:S], q1[r, n, j, :],
                                              ALU.add).then_inc(done, 1)
                    elif kind == "mask" and not causal:
                        i = n % (2 * hb)
                        dve.wait_ge(exp_done, START + H * b + n + 1)
                        dve.wait_ge(pv_done, START + nb * b + max(n // hb - 1, 0))
                        dve.tensor_tensor(pm[:, i, 0:P], pr[:, i, 0:P], mask[:, 0:P], ALU.mult).then_inc(masked, 1)
                        dve.tensor_tensor(pm[:, i, P:3 * P], pr[:, i, S:2 * S], mask[:, P:3 * P],
                                          ALU.mult).then_inc(masked, 1)
                    elif kind == "take":
                        dve.wait_ge(pv_done, START + nb * b + n + 1)
                        dve.wait_ge(y_full, START + nb * b + n)
                        dve.tensor_copy(ot[:], obank).then_inc(o_free, 1)
                    elif kind == "turn":
                        dve.wait_ge(y_full, START + nb * b + n + 1)
                        yb = ybank.rearrange("p (q j n) -> p q j n", q=2, j=hb)
                        dve.reciprocal(rden[:], yb[:, :, :, d]).then_inc(rden_ready, 1)
                        dve.wait_ge(rden_ready, START + nb * b + n + 1)
                        for qt in range(2):
                            out = y[:, bass.ds(2 * b + qt, 1), d * hb * n:d * hb * (n + 1)]
                            ins = dve.tensor_tensor(
                                out.rearrange("p t (j n) -> p (t j) n", n=d), yb[:, qt, :, 0:d],
                                rden[:, qt, :].rearrange("p (j n) -> p j n", n=1).broadcast_to([P, hb, d]),
                                ALU.mult)
                            ins.then_inc(y_half if qt == 0 else y_free, 1)



R = CC + 1
CH = -(-LC // 4)
CHUNKS = [(CH * c, min(CH * c + CH, LC)) for c in range(4)]
GROUPS = [range(4 * c, min(4 * c + 4, KT)) for c in range(4)]
SLOT = 64
PAIRS = 6


def cross_attention(nc, k, split, nh, d, scale, ctx_t, q_in, wq, wk, wv, y, ctx_tokens=None):
    hb = 2 if nh > 1 else 1
    nb = nh // hb
    apart = not split and nh > 1
    vw = d if apart else d + 1
    pitch = 32 if vw <= 32 else P
    og = min(P // pitch, nh)
    no = nh // og
    common = not split and wq.shape[1] == R
    tg = 4 // og
    gps = -(-KT // tg)
    ns = no * gps
    bps = og // hb

    def group(g):
        a, t0 = g // gps, tg * (g % gps)
        tiles = range(t0, min(t0 + tg, KT))
        return a, tiles, [(og * i + j, t, og * a + j) for i, t in enumerate(tiles) for j in range(og)]

    if wv is None:
        vuses = []
    elif split:
        vuses = [[(t, 0, nh * vw) for t in g] for g in GROUPS]
    else:
        vuses = [[(t, 0, nh * vw), (t + 1, 0, nh * vw)] for t in range(0, KT - 3, 2)]
        vuses += [[(t, 0, nh * vw)] for t in range(KT - 3, KT)]
    nv = len(vuses)
    quses = [] if split else [(qt, n) for qt in range(QT) for n in range(0, wq.shape[1], BANK)]
    msteps = 4 if split else 2 if common else 1

    first = [("keys", n) for n in range(4)] if split else [("queries", n) for n in range(len(quses))]
    turns = lambda g: [("q_turn", g)] + ([("k_turn", g, 0), ("k_turn", g, 1)] if split else [])
    nsplit = 7 if split else 5
    npm = 8 * hb

    def schedule():
        out = []

        def block(g, off, lo, hi):
            for s in turns(g):
                out.append((lo - 1, off, s))
            for n in range(npm):
                out.append((lo + (n + 0.5) * (hi - lo) / npm, off, ("maxima", g, n)))
            out.append((hi, off, ("place_max", g)))
            out.append((hi + 1, off, ("max_turn", g)))

        def queries(at, step):
            out.extend((at + 0.25 * n, 1, s) for n, s in enumerate(first))
            out.extend((at + 1 + step * n, 1, ("split", n)) for n in range(nsplit))

        if no == 1:
            queries(-2, 0.25)
            block(0, 1, 1, gps)
            return sorted(out, key=lambda e: e[0])
        wide = (0.55 * gps + 1.6) / bps
        for j in range(bps):
            block(nb - bps + j, 0, wide * j - 1.6, wide * (j + 1) - 1.6)
        out = [(p + ns + 2, 1, s) if p < -1 else (p, off, s) for p, off, s in out]
        queries(0.55 * gps + 1.01, 0.3 if split else 0.25)
        for a in range(1, no):
            lo, hi = gps * a, gps * (a + 1)
            if a == 1:
                lo += 2
            for j in range(bps):
                block(bps * (a - 1) + j, 1, lo + (hi - lo) * j / bps, lo + (hi - lo) * (j + 1) / bps)
        return sorted(out, key=lambda e: e[0])

    def plan(last, attend, search):
        out = [(-1 + (n + 1) / (nv + 1), 0, ("values", n)) for n in range(nv)]
        for n in range(ns + 1):
            if n < ns:
                out.append((n, 0, ("scores", n)))
            if n >= 1:
                out.append((n + (0.6 if apart else 0.45), 0, ("weigh", n - 1)))
                if n % gps == 0:
                    if apart:
                        out.append((n + 0.85, 0, ("sum", n // gps - 1)))
                    out.append((n + 0.9, 0, ("take", n // gps - 1)))
                    if n < ns:
                        out.append((n + 1.5, 0, ("turn", n // gps - 1)))
        out.append((0.5, -1, ("turn", no - 1)))
        out = sorted(out + schedule(), key=lambda e: e[0])
        return [(off, s) for _, off, s in out if (last, attend, search)[off + 1]]

    ringed = ("keys", "queries", "q_turn", "k_turn", "maxima", "max_turn")
    by_batch = sorted(schedule(), key=lambda e: -e[1])
    ring_steps = [s for _, _, s in by_batch if s[0] in ringed]
    use = {s: n for n, s in enumerate(ring_steps)}
    per = len(ring_steps)
    nsu = nv + ns
    assert per % 2 == 0 and nsu % 2 == 0
    ow = 2 * S if apart else S
    offs = [off for off, s in plan(True, True, True) if s in use]
    assert offs == sorted(offs)
    KDT = BF16 if split else F32

    with ExitStack() as ctx:
        def sb(name, shape, dt=F32):
            return k.sb(name, shape, dt, ctx)

        ctx_a, ctx_b = sb("ctx_a", [P, LCP]), sb("ctx_b", [P, LCP])
        v = sb("v_cur", [P, KT, nh * vw])
        pr = sb("probs", [P, 2, 4 * S])
        ot = sb("ot", [P, ow])
        if apart:
            acc, ones_col = sb("prob_sums", [P, 2, 4 * S]), sb("ones_col", [P, 1])
        rden = sb("rden", [P, QT, og])
        mx, negm = sb("mx", [P, 2, QT * hb, 4]), sb("negm", [P, nb, QT * hb])
        mr = sb("max_rest", [P, QT, hb])
        if split:
            kf = sb("kf", [P, KT, C])
            ktok = sb("ktok", [P, KT, H * SLOT], BF16)
            kparts = ktok[:].rearrange("p t (h s) -> p (t h) s", s=SLOT)
            kt = sb("kt", [P, nb, LC], BF16)
            qtok = sb("qtok", [P, QT, H * SLOT], BF16)
            q1, q2 = sb("q1", [P, nb, hb, S], BF16), sb("q2", [P, nb, hb, S], BF16)
        else:
            xq = sb("xq_cur", [P, S])
            qtok = sb("qtok", [P, QT, nh, R])
            qhh, qlo = sb("qhh", [P, QT, nh, 2 * CC], BF16), sb("qlo", [P, QT, nh, CC], BF16)
            yhl = sb("yhl", [P, LCP], BF16)
            qhh_t, qlo_t = sb("qhh_t", [P, 2, hb * S], BF16), sb("qlo_t", [P, 2, hb * S], BF16)
            q2 = sb("q2", [P, nb, hb * S])
            cmn = sb("common", [P, QT])
        a_in, b_in, cleared, set_up, q_in_place, parts, ring_full, free0, free1 = sems(
            nc, ctx, "ctx_a_in", "ctx_b_in", "cleared", "set_up", "q_in_place", "parts", "ring_full",
            "ring_free0", "ring_free1",
            start=START)
        s_full, s_free, pv_done, o_free, y_full, y_free, rden_ready, y_half, neg_ready, max_placed, q_half, added, \
            summed, passed = sems(
            nc, ctx, "s_full", "s_free", "pv_done", "o_free", "y_full", "y_free", "rden_ready", "y_half",
            "neg_ready", "max_placed", "q_half", "added", "summed", "passed", start=START)
        ring_free = [free0, free1]

        def ring(step, dt=F32):
            bank = k.ps[:, use[step] % 2, :]
            return bank if dt == F32 else bank.bitcast(dt)

        def wait_ring_reuse(pe, b, step):
            u = use[step]
            pe.wait_ge(ring_free[u % 2], START + b * (per // 2) + u // 2)

        def wait_consumed(eng, b, step):
            u = use[step]
            eng.wait_ge(ring_free[u % 2], START + b * (per // 2) + u // 2 + 1)

        def wait_others(pe, b, step, *consumed):
            others = [o for o in consumed if use[o] % 2 != use[step] % 2]
            if others:
                wait_consumed(pe, b, max(others, key=use.get))

        def wait_produced(eng, b, step):
            eng.wait_ge(ring_full, START + b * per + use[step] + 1)

        def pair(u):
            return k.ps[:, 2 + 2 * (u % 2):4 + 2 * (u % 2), :].rearrange("p a n -> p (a n)")

        obank, ybank = k.ps[:, 6, 0:ow], k.ps[:, 7, 0:ow]
        block = ctx.enter_context(nc.Block())

        def iterations(eng, emit):
            emit(-1, plan(False, False, True))
            emit(0, plan(False, True, True))
            with eng.Fori(1, B - 1) as i:
                emit(i, plan(True, True, True))
            emit(B - 1, plan(True, True, False))
            emit(B, plan(True, False, False))

        @block.sync
        def _(sp):
            def load_a(b):
                if split:
                    sp.wait_ge(ring_full, START + (0 if isinstance(b, int) and b == 0 else (b - 1) * per + 4))
                else:
                    sp.wait_ge(parts, START + nsplit * b)
                    if apart and not (isinstance(b, int) and b == 0):
                        sp.wait_ge(s_full, START + (b - 1) * nsu + nv)
                sp.dma_start(ctx_a[0:CC, 0:LC], ctx_t[b]).then_inc(a_in, 16)

            def load_b(b):
                if split:
                    sp.wait_ge(s_full, START + (0 if isinstance(b, int) and b == 0 else (b - 1) * nsu + nv))
                else:
                    sp.wait_ge(s_full, START + b * nsu)
                sp.dma_start(ctx_b[0:CC, 0:LC], ctx_t[b]).then_inc(b_in, 16)
                if wv is None:
                    sp.wait_ge(pv_done, START + b * ns)
                    sp.dma_start(v[:, 0:KT - 1, 0:CC], ctx_tokens[b][0:LCP - P, :].rearrange(
                        "(t p) c -> p t c", p=P)).then_inc(b_in, 16)
                    sp.dma_start(v[0:LC - LCP + P, KT - 1, 0:CC], ctx_tokens[b][LCP - P:LC, :]).then_inc(b_in, 16)

            load_a(0)
            load_b(0)
            load_a(1)
            load_b(1)
            with sp.Fori(1, B - 1) as i:
                load_a(i + 1)
                load_b(i + 1)

        nload = 16 if wv is not None else 48

        @block.gpsimd
        def _(pool):
            for t in (ctx_a, ctx_b):
                pool.memset(t[0:CC, LC:LCP], 0.0).then_inc(set_up, 1)
                pool.memset(t[CC:P, :], 0.0).then_inc(set_up, 1)
            pool.wait_ge(set_up, START + 4)
            pool.memset(ctx_a[CC:R, :], 1.0).then_inc(set_up, 1)
            pool.memset(ctx_b[CC:R, :], 1.0).then_inc(set_up, 1)
            pool.wait_ge(set_up, START + 6)
            if split:
                kslots = ktok[:].rearrange("p t (h s) -> p (t h) s", s=SLOT)
                pool.memset(kslots[:, :, 8 * PAIRS:8 * PAIRS + 3], 1.0).then_inc(set_up, 1)
                pool.memset(kslots[:, :, 8 * PAIRS + 3:SLOT], 0.0).then_inc(set_up, 1)
            elif wv is None:
                pool.memset(v[:, :, CC:R], 1.0).then_inc(set_up, 1)
            else:
                pool.memset(ones_col[:], 1.0).then_inc(set_up, 1)

            def emit(i0, steps):
                for off, step in steps:
                    kind, g = step[0], step[1]
                    b = i0 + off
                    if apart and step == ("q_turn", nb - 1) and not (isinstance(b, int) and b == B - 1):
                        pool.wait_ge(ring_full, START + b * per + len(first))
                        step_past(pool, passed)
                        pool.tensor_copy(xq[:], q_in[:, bass.ds(S * (b + 1), S)]).then_inc(q_in_place, 1)
                    elif not apart and step == first[0]:
                        pool.wait_ge(ring_full, START + b * per)
                        step_past(pool, passed)
                        if split:
                            pool.tensor_copy(qtok[:], q_in[:, bass.ds(QT * b, QT), :]).then_inc(q_in_place, 1)
                        else:
                            pool.tensor_copy(xq[:], q_in[:, bass.ds(S * b, S)]).then_inc(q_in_place, 1)
                    elif kind == "place_max":
                        n = nb * b + g
                        pool.wait_ge(neg_ready, START + n + 1)
                        step_past(pool, passed)
                        neg = negm[:, g, :].rearrange("p (q h) -> p q h", q=QT)
                        if split:
                            qs = qtok[:].rearrange("p q (h s) -> p q h s", s=SLOT)[:, :, hb * g:hb * g + hb, :]
                            cut = [qs[:, :, :, 8 * PAIRS + i] for i in range(3)]
                            pool.tensor_copy(cut[0], neg).then_inc(max_placed, 1)
                            pool.wait_ge(max_placed, START + 4 * n + 1)
                            pool.tensor_tensor(mr[:], neg, cut[0], ALU.subtract).then_inc(max_placed, 1)
                            pool.wait_ge(max_placed, START + 4 * n + 2)
                            step_past(pool, passed)
                            pool.tensor_copy(cut[1], mr[:]).then_inc(max_placed, 1)
                            pool.wait_ge(max_placed, START + 4 * n + 3)
                            pool.tensor_tensor(cut[2], mr[:], cut[1], ALU.subtract).then_inc(max_placed, 1)
                        elif common:
                            cm = cmn[:].rearrange("p (q h) -> p q h", h=1)
                            pool.tensor_tensor(mr[:], cm, neg, ALU.subtract).then_inc(max_placed, 1)
                            pool.wait_ge(max_placed, START + 2 * n + 1)
                            pool.tensor_tensor(qtok[:, :, :, CC], cm, mr[:], ALU.subtract).then_inc(max_placed, 1)
                        else:
                            pool.tensor_copy(qtok[:, :, hb * g:hb * g + hb, CC], neg).then_inc(max_placed, 1)

            if apart:
                pool.tensor_copy(xq[:], q_in[:, 0:S]).then_inc(q_in_place, 1)
            iterations(pool, emit)

        nset = 6 + (2 if split else 1)

        @block.tensor
        def _(pe):
            def emit(i0, steps):
                for off, step in steps:
                    kind, g = step[0], step[1]
                    b = i0 + off
                    if step in use:
                        wait_ring_reuse(pe, b, step)
                    if kind == "keys":
                        pe.wait_ge(a_in, START + 16 * b + 16)
                        for i, t in enumerate(GROUPS[g]):
                            ins = pe.matmul(ring(step)[:, C * i:C * i + C], ctx_a[:, P * t:P * t + P], wk,
                                            start=True, stop=True)
                        ins.then_inc(ring_full, 1)
                    elif kind == "queries":
                        pe.wait_ge(q_in_place, START + b + 1)
                        qt, n = quses[g]
                        m = min(BANK, wq.shape[1] - n)
                        pe.matmul(ring(step)[:, 0:m], xq[:, P * qt:P * qt + P], wq[:, n:n + m],
                                  start=True, stop=True).then_inc(ring_full, 1)
                    elif kind == "q_turn" and split:
                        pe.wait_ge(q_in_place, START + b + 1)
                        for qt in range(QT):
                            ins = pe.transpose(ring(step, BF16)[:, P * qt:P * qt + P],
                                               qtok[:, qt, P * g:P * g + P], k.identb[:])
                        ins.then_inc(ring_full, 1)
                    elif kind == "q_turn":
                        pe.wait_ge(parts, START + nsplit * b + 3)
                        for j in range(hb):
                            for qt in range(QT):
                                c = S * j + P * qt
                                pe.transpose(ring(step, BF16)[:, c:c + P], qhh[:, qt, hb * g + j, :], k.identb[:])
                                c += hb * S
                                ins = pe.transpose(ring(step, BF16)[0:CC, c:c + P], qlo[:, qt, hb * g + j, :],
                                                   k.identb[:])
                        ins.then_inc(ring_full, 1)
                    elif kind == "k_turn":
                        pe.wait_ge(parts, START + nsplit * b + nsplit)
                        for i, t in enumerate(range(8 * step[2], min(8 * step[2] + 8, KT))):
                            ins = pe.transpose(ring(step, BF16)[:, P * i:P * i + P], ktok[:, t, P * g:P * g + P],
                                               k.identb[:])
                        ins.then_inc(ring_full, 1)
                    elif kind == "maxima":
                        n = step[2]
                        j, qt, (lo, hi) = n // 8, n // 4 % 2, CHUNKS[n % 4]
                        wait_others(pe, b, step, *turns(g))
                        if split:
                            pe.matmul(ring(step)[:, 0:hi - lo], q1[:, g, j, P * qt:P * qt + P],
                                      kt[:, g, lo:hi], start=True, stop=True).then_inc(ring_full, 1)
                        else:
                            c = S * j + P * qt
                            pe.wait_ge(parts, START + nsplit * b + nsplit)
                            pe.matmul(ring(step)[:, 0:hi - lo], qhh_t[:, g % 2, c:c + P], yhl[:, lo:hi],
                                      start=True, stop=False)
                            pe.matmul(ring(step)[:, 0:hi - lo], qlo_t[:, g % 2, c:c + P], yhl[:, lo:hi],
                                      start=False, stop=True).then_inc(ring_full, 1)
                    elif kind == "max_turn":
                        pe.wait_ge(max_placed, START + msteps * (nb * b + g + 1))
                        if split:
                            for qt in range(QT):
                                ins = pe.transpose(ring(step, BF16)[:, P * qt:P * qt + P],
                                                   qtok[:, qt, P * g:P * g + P], k.identb[:])
                        else:
                            for j in range(hb):
                                for qt in range(QT):
                                    c = S * j + P * qt
                                    ins = pe.transpose(ring(step)[0:R, c:c + P], qtok[:, qt, hb * g + j, :],
                                                       k.ident[:])
                        ins.then_inc(ring_full, 1)
                    elif kind == "values":
                        if apart:
                            pe.wait_ge(a_in, START + 16 * b + 16)
                        else:
                            pe.wait_ge(b_in, START + nload * b + nload)
                        pe.wait_ge(s_free, START + nsu * b + max(g - 1, 0))
                        tokens = ctx_a if apart else ctx_b
                        for i, (t, lo, hi) in enumerate(vuses[g]):
                            c = P * 2 * i if split else BANK * i
                            ins = pe.matmul(pair(g)[:, c:c + hi - lo], tokens[:, P * t:P * t + P], wv[:, lo:hi],
                                            start=True, stop=True)
                        ins.then_inc(s_full, 1)
                    elif kind == "scores":
                        u = nv + g
                        a, _, squares = group(g)
                        pe.wait_ge(s_free, START + nsu * b + max(u - 1, 0))
                        if not split and g == 0:
                            pe.wait_ge(b_in, START + nload * b + nload)
                        if g % gps == 0:
                            for n in range(bps * a, bps * a + bps):
                                wait_consumed(pe, b, ("max_turn", n))
                        for i, t, h in squares:
                            m = min(P, LC - P * t)
                            o = pair(u)[0:m, S * i:S * i + S]
                            if split:
                                if h % 2 == 0:
                                    o = pair(u)[0:m, S * i:S * i + 2 * S].rearrange("p (j n) -> p j n", n=S)
                                    ins = pe.matmul(o, kt[:, h // 2, P * t:P * t + m], q2[:, h // 2, :, :],
                                                    start=True, stop=True)
                            else:
                                ins = pe.matmul(o, ctx_b[:, P * t:P * t + m],
                                                q2[:, h // hb, S * (h % hb):S * (h % hb) + S],
                                                start=True, stop=True)
                        ins.then_inc(s_full, 1)
                    elif kind == "weigh":
                        a, _, squares = group(g)
                        if g == 0 and nv:
                            pe.wait_ge(s_free, START + nsu * b + nv)
                        if g % gps == 0:
                            pe.wait_ge(o_free, START + no * b + a + 1)
                        pe.wait_ge(s_free, START + nsu * b + nv + g + 1)
                        for i, t, h in squares:
                            m = min(P, LC - P * t)
                            r = pitch * (h % og)
                            ins = pe.matmul(obank[r:r + vw, 0:S], v[0:m, t, vw * h:vw * h + vw],
                                            pr[0:m, g % 2, S * i:S * i + S], start=(t == 0), stop=(t == KT - 1))
                        ins.then_inc(pv_done, 1)
                    elif kind == "sum":
                        pe.wait_ge(added, START + ns * b + gps * (g + 1))
                        for j in range(og):
                            ins = pe.matmul(obank[pitch * j:pitch * j + 1, S:2 * S], ones_col[:],
                                            acc[:, g % 2, S * j:S * j + S], start=True, stop=True)
                        ins.then_inc(summed, 1)
                    elif kind == "turn":
                        pe.wait_ge(o_free, START + no * b + g + 2)
                        pe.wait_ge(y_free, START + no * b + g)
                        for i in range(ow // P):
                            ins = pe.transpose(ybank[:, P * i:P * i + P], ot[:, P * i:P * i + P], k.ident[:])
                        ins.then_inc(y_full, 1)

            pe.wait_ge(set_up, START + nset)
            pe.wait_ge(cleared, START + 2)
            pe.wait_ge(o_free, START + 1)
            iterations(pe, emit)

        @block.scalar
        def _(act):
            def emit(i0, steps):
                for off, step in steps:
                    kind, g = step[0], step[1]
                    b = i0 + off
                    if step in use and kind != "maxima" and not (split and kind in ("q_turn", "max_turn")):
                        wait_produced(act, b, step)
                        free = ring_free[use[step] % 2]
                    if kind == "keys":
                        if g == 0:
                            act.wait_ge(parts, START + nsplit * b)
                        n = len(GROUPS[g])
                        act.activation(kf[:, 4 * g:4 * g + n, :], ring(step)[:, 0:C * n].rearrange(
                            "p (t c) -> p t c", c=C), ACT.Copy).then_inc(free, 1)
                    elif kind == "queries":
                        qt, n = quses[g]
                        if common:
                            act.activation(qtok[:, qt, 0, :], ring(step)[:, 0:R], ACT.Copy).then_inc(free, 1)
                        else:
                            act.activation(qtok[:, qt, n // CC:n // CC + BANK // CC, 0:CC],
                                           ring(step).rearrange("p (h c) -> p h c", c=CC),
                                           ACT.Copy).then_inc(free, 1)
                    elif kind == "q_turn" and not split:
                        act.activation(qhh_t[:, g % 2, :], ring(step, BF16)[:, 0:hb * S],
                                       ACT.Copy).then_inc(q_half, 1)
                        act.activation(qlo_t[0:CC, g % 2, :], ring(step, BF16)[0:CC, hb * S:2 * hb * S],
                                       ACT.Copy).then_inc(free, 1)
                    elif kind == "k_turn":
                        lo, hi = 8 * P * step[2], min(8 * P * step[2] + 8 * P, LC)
                        act.activation(kt[:, g, lo:hi], ring(step, BF16)[:, 0:hi - lo], ACT.Copy).then_inc(free, 1)
                    elif kind == "max_turn" and not split:
                        act.activation(q2[0:R, g, :], ring(step)[0:R, 0:hb * S], ACT.Copy).then_inc(free, 1)
                    elif kind == "values":
                        act.wait_ge(s_full, START + nsu * b + g + 1)
                        t, lo, _ = vuses[g][0]
                        n = len(vuses[g])
                        if split:
                            src = pair(g)[:, 0:2 * P * n].rearrange("p (t c) -> p t c", c=2 * P)[:, :, 0:nh * vw]
                            dst = v[:, t:t + n, :]
                        else:
                            src = pair(g)[:, 0:BANK * n].rearrange("p (t c) -> p t c", c=BANK)[:, :, 0:nh * vw]
                            dst = v[:, t:t + n, :]
                        act.activation(dst, src, ACT.Copy).then_inc(s_free, 1)
                    elif kind == "scores":
                        u = nv + g
                        act.wait_ge(s_full, START + nsu * b + u + 1)
                        act.wait_ge(pv_done, START + ns * b + max(g - 1, 0))
                        if apart:
                            act.wait_ge(added, START + ns * b + max(g - 1, 0))
                        _, tiles, squares = group(g)
                        n = S * len(squares)
                        m = min(P, LC - P * tiles[-1])
                        act.activation(pr[0:m, g % 2, 0:n], pair(u)[0:m, 0:n], ACT.Exp,
                                       scale=scale).then_inc(s_free, 1)

            act.wait_ge(cleared, START + 2)
            iterations(act, emit)

        @block.vector
        def _(dve):
            def emit(i0, steps):
                for off, step in steps:
                    kind, g = step[0], step[1]
                    b = i0 + off
                    if kind == "split" and split:
                        kv = kf[:].rearrange("p t (h c) -> p (t h) c", c=8)
                        if g == 0:
                            wait_consumed(dve, b, ("keys", 2))
                            wait_consumed(dve, b, ("keys", 3))
                        elif g not in (2, 6):
                            dve.wait_ge(parts, START + nsplit * b + g)
                        k1, k2 = kparts[:, :, 0:8], kparts[:, :, 8:16]
                        if g in (1, 2, 5):
                            dst, src = ((24, 32), k1) if g == 1 else ((40, 48), k1) if g == 2 else ((32, 40), k2)
                            dve.tensor_copy(kparts[:, :, dst[0]:dst[1]], src).then_inc(parts, 1)
                        elif g == 0:
                            dve.tensor_copy(k1, kv).then_inc(parts, 1)
                        elif g == 3:
                            dve.tensor_tensor(kv, kv, k1, ALU.subtract).then_inc(parts, 1)
                        elif g == 4:
                            dve.tensor_copy(k2, kv).then_inc(parts, 1)
                        else:
                            dve.tensor_tensor(kparts[:, :, 16:24], kv, k2, ALU.subtract).then_inc(parts, 1)
                    elif kind == "split":
                        q = qtok[:, :, :, 0:CC]
                        if g == 0:
                            wait_consumed(dve, b, first[-1])
                            wait_consumed(dve, b, first[-2])
                            dve.tensor_copy(qhh[:, :, :, 0:CC], q).then_inc(parts, 1)
                        elif g == 1:
                            dve.wait_ge(parts, START + nsplit * b + 1)
                            dve.tensor_tensor(qlo[:], q, qhh[:, :, :, 0:CC], ALU.subtract).then_inc(parts, 1)
                        elif g == 2:
                            dve.tensor_copy(qhh[:, :, :, CC:2 * CC], qhh[:, :, :, 0:CC]).then_inc(parts, 1)
                        elif g == 3:
                            dve.wait_ge(a_in, START + 16 * b + 16)
                            dve.tensor_copy(yhl[0:CC, 0:LC], ctx_a[0:CC, 0:LC]).then_inc(parts, 1)
                        else:
                            dve.wait_ge(parts, START + nsplit * b + 4)
                            dve.tensor_tensor(yhl[CC:P, 0:LC], ctx_a[0:CC, 0:LC], yhl[0:CC, 0:LC],
                                              ALU.subtract).then_inc(parts, 1)
                        if common and g == 4:
                            dve.tensor_copy(cmn[:], qtok[:, :, 0, CC]).then_inc(q_half, 1)
                    elif split and kind in ("q_turn", "max_turn"):
                        wait_produced(dve, b, step)
                        q = q1 if kind == "q_turn" else q2
                        for j, done in ((0, q_half), (1, ring_free[use[step] % 2])):
                            rows = slice(SLOT * j, SLOT * j + SLOT)
                            dve.tensor_copy(q[rows, g, j, :], ring(step, BF16)[rows, 0:S]).then_inc(done, 1)
                    elif kind == "maxima":
                        n = step[2]
                        j, qt, (lo, hi) = n // 8, n // 4 % 2, CHUNKS[n % 4]
                        if n == 0:
                            dve.wait_ge(neg_ready, START + nb * b + max(g - 1, 0))
                        wait_produced(dve, b, step)
                        i = hb * qt + j
                        dve.tensor_reduce(mx[:, g % 2, i, n % 4:n % 4 + 1], ring(step)[:, 0:hi - lo], AX_X,
                                          ALU.max).then_inc(ring_free[use[step] % 2], 1)
                    elif kind == "place_max":
                        wait_consumed(dve, b, ("maxima", g, npm - 1))
                        wait_consumed(dve, b, ("maxima", g, npm - 2))
                        dve.tensor_reduce(negm[:, g, :], mx[:, g % 2, :, :], AX_X, ALU.max,
                                          negate=True).then_inc(neg_ready, 1)
                    elif kind == "weigh" and apart:
                        a, tiles, _ = group(g)
                        m = min(P, LC - P * tiles[-1])
                        dve.wait_ge(s_free, START + nsu * b + nv + g + 1)
                        o, p = acc[0:m, a % 2, :], pr[0:m, g % 2, :]
                        if g % gps == 0:
                            dve.tensor_copy(o, p).then_inc(added, 1)
                        else:
                            dve.wait_ge(added, START + ns * b + g)
                            dve.tensor_tensor(o, o, p, ALU.add).then_inc(added, 1)
                    elif kind == "take":
                        if apart:
                            dve.wait_ge(summed, START + no * b + g + 1)
                        else:
                            dve.wait_ge(pv_done, START + ns * b + gps * (g + 1))
                        dve.wait_ge(y_full, START + no * b + g)
                        dve.tensor_copy(ot[:], obank).then_inc(o_free, 1)
                    elif kind == "turn":
                        dve.wait_ge(y_full, START + no * b + g + 1)
                        yb = ybank[:, 0:S].rearrange("p (q j n) -> p q j n", q=QT, j=og)
                        if apart:
                            sums = ybank[:, S:2 * S].rearrange("p (q j n) -> p q j n", q=QT, j=og)[:, :, :, 0]
                        else:
                            sums = yb[:, :, :, d]
                        dve.reciprocal(rden[:], sums).then_inc(rden_ready, 1)
                        dve.wait_ge(rden_ready, START + no * b + g + 1)
                        for qt in range(QT):
                            o = y[:, bass.ds(QT * b + qt, 1), d * og * g:d * og * (g + 1)]
                            dve.tensor_tensor(
                                o.rearrange("p t (j n) -> p (t j) n", n=d), yb[:, qt, :, 0:d],
                                rden[:, qt, :].rearrange("p (j n) -> p j n", n=1).broadcast_to([P, og, d]),
                                ALU.mult).then_inc(y_half if qt == 0 else y_free, 1)

            dve.memset(q2[:], 0.0).then_inc(cleared, 1)
            dve.memset((q1 if split else qlo_t)[:], 0.0).then_inc(cleared, 1)
            dve.memset(obank, 0.0).then_inc(o_free, 1)
            dve.wait_ge(cleared, START + 2)
            iterations(dve, emit)


def split_queries(nc, k, q, qtok):
    with ExitStack() as ctx:
        rest = k.sb("q_rest", [P, NT, C], F32, ctx)
        (cut,) = sems(nc, ctx, "cut")
        block = ctx.enter_context(nc.Block())
        qv = q.rearrange("p t (h c) -> p (t h) c", c=8)
        rv = rest[:].rearrange("p t (h c) -> p (t h) c", c=8)
        o = qtok[:].rearrange("p t (h s) -> p (t h) s", s=SLOT)

        @block.vector
        def _(dve):
            steps = [
                lambda: dve.tensor_copy(o[:, :, 0:8], qv),
                lambda: dve.tensor_tensor(rv, qv, o[:, :, 0:8], ALU.subtract),
                lambda: dve.tensor_copy(o[:, :, 24:32], rv),
                lambda: dve.tensor_tensor(o[:, :, 40:48], rv, o[:, :, 24:32], ALU.subtract),
                lambda: dve.tensor_copy(o[:, :, 8:16], o[:, :, 0:8]),
                lambda: dve.tensor_copy(o[:, :, 16:24], o[:, :, 0:8]),
                lambda: dve.tensor_copy(o[:, :, 32:40], o[:, :, 24:32]),
                lambda: dve.memset(o[:, :, 48:SLOT], 0.0),
            ]
            for n, step in enumerate(steps):
                step().then_inc(cut, 1)
                dve.wait_ge(cut, n + 1)




def vec_row(ap):
    return ap.rearrange("(a n) -> a n", a=1)


def vec_col(ap):
    return ap.rearrange("(n a) -> n a", a=1)


def clear(nc, *tiles):
    with ExitStack() as ctx:
        (cleared,) = sems(nc, ctx, "cleared")
        block = ctx.enter_context(nc.Block())

        @block.gpsimd
        def _(pool):
            for t, value in tiles:
                pool.memset(t, value).then_inc(cleared, 1)


def quantize_weight(nc, k, w, add, factor, floor, lo, hi, rescale):
    rounder = 1.5 * 2.0 ** 23
    with ExitStack() as ctx:
        m, ma, s, r = (k.sb(n, [P, 1], F32, ctx) for n in ("qm", "qma", "qs", "qr"))
        dve_step, reduced = sems(nc, ctx, "dve_step", "reduced")
        block = ctx.enter_context(nc.Block())

        @block.vector
        def _(dve):
            dve.tensor_reduce(m[:], w, AX_X, ALU.add if add else ALU.max,
                              apply_absolute_value=True).then_inc(dve_step, 1)
            dve.wait_ge(reduced, 1)
            dve.tensor_scalar(s[:], ma[:], factor, floor, ALU.mult, ALU.add).then_inc(dve_step, 1)
            dve.wait_ge(dve_step, 2)
            dve.reciprocal(r[:], s[:]).then_inc(dve_step, 1)
            dve.wait_ge(dve_step, 3)
            dve.tensor_scalar(w, w, r[:], rounder, ALU.mult, ALU.add).then_inc(dve_step, 1)
            dve.wait_ge(dve_step, 4)
            dve.tensor_scalar(w, w, rounder, hi, ALU.subtract, ALU.min).then_inc(dve_step, 1)
            dve.wait_ge(dve_step, 5)
            if rescale:
                dve.tensor_scalar(w, w, lo, s[:], ALU.max, ALU.mult).then_inc(dve_step, 1)
            else:
                dve.tensor_scalar(w, w, lo, None, ALU.max).then_inc(dve_step, 1)

        @block.gpsimd
        def _(pool):
            pool.wait_ge(dve_step, 1)
            pool.partition_all_reduce(ma[:], m[:], P, RADD if add else RMAX).then_inc(reduced, 1)


def quantize_fp4(nc, k, x, n):
    with ExitStack() as ctx:
        sb = lambda name, shape: k.sb(name, shape, F32, ctx)
        am, sc, rs = sb("fam", [P, n]), sb("fsc", [P, n]), sb("frs", [P, n])
        a, c, big = sb("fabs", [P, n, 16]), sb("fcount", [P, n, 16]), sb("fbig", [P, n, 16])
        dve_step, abs_ready, sign_ready = sems(nc, ctx, "dve_step", "abs_ready", "sign_ready")
        spread = lambda t: t[:].rearrange("p (n a) -> p n a", a=1).broadcast_to([P, n, 16])
        block = ctx.enter_context(nc.Block())

        @block.vector
        def _(dve):
            def above(out, v, rest):
                return dve.scalar_tensor_tensor(out=out[:], in0=a[:], scalar=v, in1=rest[:], op0=ALU.is_gt, op1=ALU.add)

            steps = [
                lambda: dve.tensor_reduce(am[:], x, AX_X, ALU.max, apply_absolute_value=True),
                lambda: dve.tensor_scalar(sc[:], am[:], 1.0 / 6.0, 1e-12, ALU.mult, ALU.max),
                lambda: dve.reciprocal(rs[:], sc[:]),
                lambda: dve.tensor_tensor(a[:], x, spread(rs), ALU.mult),
                lambda: dve.tensor_scalar(big[:], a[:], 5.0, 2.0, ALU.is_gt, ALU.mult),
                lambda: above(big, 3.5, big),
                lambda: above(big, 2.5, big),
                lambda: dve.tensor_scalar(c[:], a[:], 1.75, None, ALU.is_gt),
                lambda: dve.scalar_tensor_tensor(out=c[:], in0=big[:], scalar=2.0, in1=c[:], op0=ALU.mult, op1=ALU.add),
                lambda: above(c, 1.25, c),
                lambda: above(c, 0.75, c),
                lambda: above(c, 0.25, c),
                lambda: dve.scalar_tensor_tensor(out=c[:], in0=c[:], scalar=0.5, in1=x, op0=ALU.mult, op1=ALU.mult),
                lambda: dve.tensor_tensor(x, c[:], spread(sc), ALU.mult),
            ]
            for i, step in enumerate(steps):
                if i == 4:
                    dve.wait_ge(abs_ready, 1)
                if i == 12:
                    dve.wait_ge(sign_ready, 1)
                step().then_inc(dve_step, 1)
                dve.wait_ge(dve_step, i + 1)

        @block.scalar
        def _(act):
            act.wait_ge(dve_step, 4)
            act.activation(a[:], a[:], ACT.Abs).then_inc(abs_ready, 1)
            act.activation(x, x, ACT.Sign).then_inc(sign_ready, 1)


def transpose_weight(nc, k, pieces):
    with ExitStack() as ctx:
        turned, taken = sems(nc, ctx, "turned", "taken")
        block = ctx.enter_context(nc.Block())
        sizes = [(src.shape[0], src.shape[1]) for src, _ in pieces]

        @block.tensor
        def _(pe):
            for n, (src, _) in enumerate(pieces):
                r, c = sizes[n]
                if n >= 8:
                    pe.wait_ge(taken, n - 7)
                pe.transpose(k.ps[0:c, n % 8, 0:r], src, k.ident[0:r, 0:r]).then_inc(turned, 1)

        @block.vector
        def _(dve):
            for n, (_, dst) in enumerate(pieces):
                r, c = sizes[n]
                dve.wait_ge(turned, n + 1)
                dve.tensor_copy(dst, k.ps[0:c, n % 8, 0:r]).then_inc(taken, 1)


def gated(nc, k, n, lhs_a, lhs_b, rhs_a, rhs_b, out):
    count = len(out)
    with ExitStack() as ctx:
        s = k.sb("silu", [P, 2, n], F32, ctx)
        summed, silu_done, mult_done = sems(nc, ctx, "summed", "silu_done", "mult_done")
        block = ctx.enter_context(nc.Block())

        @block.tensor
        def _(pe):
            for i in range(count):
                if i >= 4:
                    pe.wait_ge(mult_done, i - 3)
                pe.matmul(k.ps[:, 2 * (i % 4), 0:n], lhs_a(i), rhs_a(i), start=True, stop=True)
                pe.matmul(k.ps[:, 2 * (i % 4) + 1, 0:n], lhs_b(i), rhs_b(i), start=True, stop=True).then_inc(summed, 1)

        @block.scalar
        def _(act):
            for i in range(count):
                act.wait_ge(summed, i + 1)
                if i >= 2:
                    act.wait_ge(mult_done, i - 1)
                act.activation(s[:, i % 2, :], k.ps[:, 2 * (i % 4), 0:n], ACT.Silu).then_inc(silu_done, 1)

        @block.vector
        def _(dve):
            for i in range(count):
                dve.wait_ge(silu_done, i + 1)
                dve.tensor_tensor(out[i], k.ps[:, 2 * (i % 4) + 1, 0:n], s[:, i % 2, :],
                                  ALU.mult).then_inc(mult_done, 1)


def normalize_context(nc, k, ctx_tokens, g_col, b_col, out_t):
    with ExitStack() as ctx:
        sb = lambda name, shape: [k.sb(f"{name}{u}", shape, F32, ctx) for u in range(2)]
        c, st, mv = sb("ctx_tok", [P, KT, CC]), sb("cst", [P, KT, 6]), sb("cmv", [P, KT, 2])
        ve, rstd, ct = sb("cve", [P, KT]), sb("crstd", [P, KT]), sb("ctx_norm_t", [CC, LC])
        mhalf = k.sb("cmhalf", [P, KT], F32, ctx)
        padded, c_in0, c_in1, stats_done, aggr_done, var_ready, rstd_ready, normed, turned, taken, stored0, stored1, \
            passed = sems(nc, ctx, "padded", "c_in0", "c_in1", "stats_done", "aggr_done", "var_ready", "rstd_ready",
                          "normed", "turned", "taken", "stored0", "stored1", "passed", start=START)
        c_in, stored = (c_in0, c_in1), (stored0, stored1)
        last = LC - LCP + P
        block = ctx.enter_context(nc.Block())

        @block.sync
        def _(sp):
            sp.wait_ge(padded, START + 3)
            with sp.Fori(0, B // 2) as i:
                for u in range(2):
                    b = 2 * i + u
                    sp.wait_ge(turned, START + 4 * (2 * i + max(u - 1, 0)))
                    sp.dma_start(c[u][:, 0:KT - 1, :], ctx_tokens[b][0:LCP - P, :].rearrange(
                        "(t p) c -> p t c", p=P)).then_inc(c_in[u], 16)
                    sp.dma_start(c[u][0:last, KT - 1, :], ctx_tokens[b][LCP - P:LC, :]).then_inc(c_in[u], 16)
                for u in range(2):
                    b = 2 * i + u
                    sp.wait_ge(taken, START + 4 * b + 4)
                    sp.dma_start(out_t[b], ct[u][:]).then_inc(stored[u], 16)
            for u in range(2):
                sp.wait_ge(stored[u], START + 16 * (B // 2))

        @block.gpsimd
        def _(pool):
            for u in range(2):
                pool.memset(c[u][:], 0.0).then_inc(padded, 1)
            pool.memset(mhalf[:], -0.5).then_inc(padded, 1)
            pool.wait_ge(padded, START + 3)
            with pool.Fori(0, B // 2) as i:
                for u in range(2):
                    pool.wait_ge(var_ready, START + 2 * i + u + 1)
                    pool.tensor_tensor(rstd[u][:], ve[u][:], mhalf[:], ALU.pow).then_inc(rstd_ready, 1)

        @block.vector
        def _(dve):
            with dve.Fori(0, B // 2) as i:
                for u in range(2):
                    b = 2 * i + u
                    dve.wait_ge(c_in[u], START + 32 * i + 32)
                    for t in range(KT):
                        dve.bn_stats(st[u][:, t, :], c[u][:, t, :]).then_inc(stats_done, 1)
                    dve.wait_ge(stats_done, START + KT * b + KT)
                    step_past(dve, passed)
                    for t in range(KT):
                        dve.bn_aggr(mv[u][:, t, :], st[u][:, t, :]).then_inc(aggr_done, 1)
                    dve.wait_ge(aggr_done, START + KT * b + KT)
                    dve.tensor_scalar(ve[u][:], mv[u][:, :, 1], EPS, None, ALU.add).then_inc(var_ready, 1)
                for u in range(2):
                    b = 2 * i + u
                    dve.wait_ge(rstd_ready, START + b + 1)
                    for t in range(KT):
                        dve.tensor_scalar(c[u][:, t, :], c[u][:, t, :], mv[u][:, t, 0:1], rstd[u][:, t:t + 1],
                                          ALU.subtract, ALU.mult).then_inc(normed, 1)

        @block.tensor
        def _(pe):
            with pe.Fori(0, B // 2) as i:
                for u in range(2):
                    b = 2 * i + u
                    for q in range(4):
                        pe.wait_ge(normed, START + KT * b + min(4 * q + 4, KT))
                        pe.wait_ge(taken, START + 4 * (2 * i + max(u - 1, 0)))
                        step_past(pe, passed)
                        for n, t in enumerate(GROUPS[q]):
                            ins = pe.transpose(k.ps[0:CC, 4 * u + q, P * n:P * n + P], c[u][:, t, :], k.ident[:])
                        ins.then_inc(turned, 1)

        @block.scalar
        def _(act):
            with act.Fori(0, B // 2) as i:
                for u in range(2):
                    b = 2 * i + u
                    act.wait_ge(stored[u], START + 16 * i)
                    for q in range(4):
                        lo, hi = BANK * q, min(BANK * q + BANK, LC)
                        act.wait_ge(turned, START + 4 * b + q + 1)
                        act.activation(ct[u][:, lo:hi], k.ps[0:CC, 4 * u + q, 0:hi - lo], ACT.Identity, scale=g_col,
                                       bias=b_col).then_inc(taken, 1)


def fold_keys(nc, k, wq_t, wk_t, out):
    with ExitStack() as ctx:
        folded, taken = sems(nc, ctx, "folded", "taken")
        block = ctx.enter_context(nc.Block())

        @block.tensor
        def _(pe):
            for j in range(4):
                for g in range(4):
                    ins = pe.matmul(k.ps[:, j, CC * g:CC * g + CC], wq_t[32 * j:32 * j + 32, g, :],
                                    wk_t[32 * j:32 * j + 32, g, :], start=True, stop=True)
                ins.then_inc(folded, 1)

        @block.vector
        def _(dve):
            for j in range(4):
                dve.wait_ge(folded, j + 1)
                dve.tensor_copy(out.rearrange("p (g j c) -> p j g c", j=4, c=CC)[:, j, :, :],
                                k.ps[:, j, 0:4 * CC].rearrange("p (g c) -> p g c", c=CC)).then_inc(taken, 1)


def route(nc, k, logits, w):
    E = 8
    with ExitStack() as ctx:
        sb = lambda name, shape: k.sb(name, shape, F32, ctx)
        m, p, s, r = sb("rm", [P, NT]), sb("rp", [P, NT, E]), sb("rs", [P, NT]), sb("rr", [P, NT])
        beat, rank = sb("beat", [P, NT, E]), sb("rank", [P, NT, E])
        dve_step, exped = sems(nc, ctx, "dve_step", "exped")
        wide = lambda ap, n: ap.rearrange("p (t a) -> p t a", a=1).broadcast_to([P, NT, n])
        block = ctx.enter_context(nc.Block())

        @block.vector
        def _(dve):
            steps = [
                lambda: dve.tensor_reduce(m[:], logits, AX_X, ALU.max),
                lambda: dve.tensor_tensor(p[:], logits, wide(m[:], E), ALU.subtract),
                lambda: dve.tensor_reduce(s[:], p[:], AX_X, ALU.add),
                lambda: dve.reciprocal(r[:], s[:]),
                lambda: dve.tensor_tensor(p[:], p[:], wide(r[:], E), ALU.mult),
                lambda: dve.memset(rank[:], 0.0),
            ]
            for j in range(E):
                if j:
                    steps.append(lambda j=j: dve.tensor_tensor(
                        beat[:, :, 0:j], p[:, :, j:j + 1].broadcast_to([P, NT, j]), p[:, :, 0:j], ALU.is_gt))
                if j < E - 1:
                    steps.append(lambda j=j: dve.tensor_tensor(
                        beat[:, :, j + 1:E], p[:, :, j:j + 1].broadcast_to([P, NT, E - 1 - j]), p[:, :, j + 1:E],
                        ALU.is_ge))
                steps.append(lambda j=j: dve.memset(beat[:, :, j:j + 1], 0.0))
                steps.append(lambda: dve.tensor_tensor(rank[:], rank[:], beat[:], ALU.add))
            steps.append(lambda: dve.scalar_tensor_tensor(out=w, in0=rank[:], scalar=2.0, in1=p[:], op0=ALU.is_lt,
                                                          op1=ALU.mult))
            for i, step in enumerate(steps):
                if i == 2:
                    dve.wait_ge(exped, 1)
                step().then_inc(dve_step, 1)
                dve.wait_ge(dve_step, i + 1)

        @block.scalar
        def _(act):
            act.wait_ge(dve_step, 2)
            act.activation(p[:], p[:], ACT.Exp).then_inc(exped, 1)


def experts(nc, k, hid_t, w2, w):
    with ExitStack() as ctx:
        summed, added = sems(nc, ctx, "summed", "added")
        block = ctx.enter_context(nc.Block())

        @block.tensor
        def _(pe):
            for t in range(NT):
                if t >= 4:
                    pe.wait_ge(added, 16 * ((t - 4) // 2 + 1))
                for f in range(2):
                    ins = pe.matmul(k.ps[:, 2 * (t % 4) + f, :], hid_t[:, P * t:P * t + P],
                                    w2[:, 4 * f:4 * f + 4, :].rearrange("p e c -> p (e c)"), start=True, stop=True)
                ins.then_inc(summed, 1)

        @block.vector
        def _(dve):
            for u in range(NT // 2):
                dve.wait_ge(summed, 2 * u + 2)
                for e in range(8):
                    for t in (2 * u, 2 * u + 1):
                        if e:
                            dve.wait_ge(added, 16 * u + 2 * (e - 1) + t % 2 + 1)
                        dve.scalar_tensor_tensor(
                            out=k.x[:, t, :], in0=k.ps[:, 2 * (t % 4) + e // 4, C * (e % 4):C * (e % 4) + C],
                            scalar=w[:, t, e:e + 1], in1=k.x[:, t, :], op0=ALU.mult, op1=ALU.add).then_inc(added, 1)


def residual(k):
    return dict(out=lambda ts: k.x[:, ts, :], add=lambda ts: k.x[:, ts, :])


def normalized_t(nc, k, src, xn, dsts):
    normalize(nc, k, src, xn, dsts)


def tile_of(xt):
    return lambda t: xt[:, P * t:P * t + P]


def layer0(nc, k, a, xn):
    with ExitStack() as c0:
        sb = lambda name, shape, dt=F32: k.sb(name, shape, dt, c0)
        xt, y, y2 = sb("xt", [P, TOK]), sb("y", [P, NT, C]), sb("y2", [P, NT, C])
        normalized_t(nc, k, k.x, xn, [(xt, None, None)])
        with ExitStack() as ctx:
            sb1 = lambda name, shape, dt=F32: k.sb(name, shape, dt, ctx)
            wq, wk, wv = sb1("wq_pad", [P, H * 32]), sb1("wk_pad", [P, H * 32]), sb1("wv_pad", [P, H * 9])
            qb, kb, vb = sb1("qb", [P, 4]), sb1("kb", [P, 4]), sb1("vb", [1, H * 9])
            load(nc, [(wq[:], a["l0_wq"]), (wk[:], a["l0_wk"]), (wv[:], a["l0_wv"]), (qb[:], a["l0_bq"]),
                      (kb[:], a["l0_bk"]), (vb[:], a["l0_bv"])])
            self_attention(nc, k, 8, 32, True, float(1.0 / np.sqrt(8)), xt, xt, wq[:], wk[:], wv[:], qb, kb, vb[:], y)
        with ExitStack() as ctx:
            sb1 = lambda name, shape, dt=F32: k.sb(name, shape, dt, ctx)
            w0, wk, wv = sb1("wcq", [P, C]), sb1("wck", [P, C]), sb1("wcv", [P, H * 9])
            bcq = sb1("bcq", [1, C])
            qtok = sb1("qtok_all", [P, NT, H * SLOT], BF16)
            load(nc, [(w0[:], a["L0_xattn_Wcq"]), (wk[:], a["l0_wck"]), (wv[:], a["l0_wcv"]),
                      (bcq[:], vec_row(a["L0_xattn_bcq"]))])
            linear_tokens(nc, k, C, [(tile_of(xt), w0[:])], bcq[:], lambda ts: y2[:, ts, :])
            split_queries(nc, k, y2[:], qtok)
            cross_attention(nc, k, True, H, 8, float(1.0 / np.sqrt(8)), a["ctx_t"], qtok, None, wk[:], wv[:], y2)
        w, b = sb("wp", [P, C]), sb("bp", [1, C])
        load(nc, [(w[:], a["L0_xattn_Wp"]), (b[:], vec_row(a["L0_xattn_bp"]))])
        add_tokens(nc, y[:], y[:], y2[:])
        transpose(nc, k, lambda t: y[:, t, :], C, [(xt, None, None)])
        linear_tokens(nc, k, C, [(tile_of(xt), w[:])], b[:], **residual(k))
        wa, wb, wf, bf = sb("lora_a", [P, 16]), sb("lora_b", [16, C]), sb("w_int4", [P, C]), sb("bf", [1, C])
        at = sb("xa_t", [16, TOK])
        load(nc, [(wa[:], a["L0_ffn_a"]), (wb[:], a["L0_ffn_b"]), (wf[:], a["L0_ffn_kernel"]),
                  (bf[:], vec_row(a["L0_ffn_bias"]))])
        quantize_weight(nc, k, wf[:], False, 1.0 / 7.0, 0.0, -8.0, 7.0, True)
        normalized_t(nc, k, k.x, xn, [(xt, None, None)])
        linear_channels(nc, k, [(wa[:], xt, at, None, 16)], ACT.Copy)
        linear_tokens(nc, k, C, [(tile_of(xt), wf[:]), (tile_of(at), wb[:])], bf[:], **residual(k))


def mha_end(nc, k, a, p, x, y, xn, xt, big, xo):
    with ExitStack() as ctx:
        sb = lambda name, shape: k.sb(name, shape, F32, ctx)
        w1, w2, w3 = sb("li1", [P, 4, C]), sb("li2", [P, 4 * C]), sb("li3", [P, 4, C])
        b1, b2, b3, g, b = sb("b1", [1, C]), sb("b2", [P, 4]), sb("b3", [1, C]), sb("g", [P, 1]), sb("b", [P, 1])
        load(nc, [(w1[:], a[p + "li1_w"].rearrange("(j p) c -> p j c", p=P)), (w2[:], a[p + "li2_w"]),
                  (w3[:], a[p + "li3_w"].rearrange("(j p) c -> p j c", p=P)), (b1[:], vec_row(a[p + "li1_b"])),
                  (b2[:], a[p + "li2_b_cols"]), (b3[:], vec_row(a[p + "li3_b"])), (g[:], vec_col(a[p + "ln3_g"])),
                  (b[:], vec_col(a[p + "ln3_b"]))])
        for j in range(4):
            transpose(nc, k, lambda t: y[:, t, C * j:C * j + C], C, [(big[:, j, :], None, None)])
        linear_tokens(nc, k, C, [(tile_of(big[:, j, :]), w1[:, j, :]) for j in range(4)], b1[:],
                      lambda ts: xo[:, ts, :], lambda ts: x[:, ts, :])
        normalized_t(nc, k, xo, xn, [(xt, g[:], b[:])])
        linear_channels(nc, k, [(w2[:, C * j:C * j + C], xt, big[:, j, :], b2[:, j:j + 1], P) for j in range(4)],
                        ACT.Gelu)
        linear_tokens(nc, k, C, [(tile_of(big[:, j, :]), w3[:, j, :]) for j in range(4)], b3[:],
                      lambda ts: xo[:, ts, :], lambda ts: xo[:, ts, :])


def layer1(nc, k, a, xn):
    p = "L1_xattn_"
    d = 32
    scale = float(d ** -0.5)
    with ExitStack() as c0:
        sb = lambda name, shape, dt=F32: k.sb(name, shape, dt, c0)
        x1, x2 = sb("x1", [P, NT, C]), sb("x2", [P, NT, C])
        xt, y, gb = sb("xt", [P, TOK]), sb("y", [P, NT, H * d]), sb("gb", [P, 2 * C])
        rows, cols = sb("ln_rows", [1, 4, C]), sb("ln_cols", [P, 6])
        ccols = sb("ctx_cols", [CC, 2])
        load(nc, [(rows[:, i, :], vec_row(a[p + n])) for i, n in enumerate(("ln1_g", "ln1_b", "ln2_g", "ln2_b"))] +
             [(cols[:, i:i + 1], vec_col(a[p + n])) for i, n in enumerate(
                 ("a1_lnx_g", "a1_lnx_b", "a1_lny_g", "a1_lny_b", "a2_lnx_g", "a2_lnx_b"))] +
             [(ccols[:, i:i + 1], vec_col(a[p + n])) for i, n in enumerate(("a2_lny_g", "a2_lny_b"))])
        normalize(nc, k, k.x, xn)
        normalize(nc, k, xn, xn)
        affine_rows(nc, k, xn[:], x1[:], rows[:, 0, :], rows[:, 1, :], gb)
        with ExitStack() as ctx:
            sb1 = lambda name, shape, dt=F32: k.sb(name, shape, dt, ctx)
            xkt = sb1("xkt", [P, TOK])
            wq, wk, wv = sb1("wq_pad", [P, H * 64]), sb1("wk_pad", [P, H * 64]), sb1("wv_pad", [P, H * 33])
            qb, kb, vb = sb1("qb", [P, 8]), sb1("kb", [P, 8]), sb1("vb", [1, H * 33])
            load(nc, [(wq[:], a["l1_wq"]), (wk[:], a["l1_wk"]), (wv[:], a["l1_wv"]), (qb[:], a["l1_qb"]),
                      (kb[:], a["l1_kb"])])
            clear(nc, (vb[:], 0.0))
            normalized_t(nc, k, x1, xn, [(xt, cols[:, 0:1], cols[:, 1:2]), (xkt, cols[:, 2:3], cols[:, 3:4])])
            self_attention(nc, k, d, 64, False, scale, xt, xkt, wq[:], wk[:], wv[:], qb, kb, vb[:], y)
        with ExitStack() as ctx:
            big = k.sb("big", [P, 4, TOK], F32, ctx)
            mha_end(nc, k, a, p + "a1_", x1, y, xn, xt, big, x2)
        add_tokens(nc, x2[:], x2[:], x1[:])
        normalize(nc, k, x2, xn)
        affine_rows(nc, k, xn[:], x1[:], rows[:, 2, :], rows[:, 3, :], gb)
        ctx_norm_t = nc.dram_tensor("ctx_norm_t", (B, CC, LC), F32, kind="Internal").ap()
        normalize_context(nc, k, a["ctx_512"], ccols[:, 0:1], ccols[:, 1:2], ctx_norm_t)
        normalized_t(nc, k, x1, xn, [(xt, cols[:, 4:5], cols[:, 5:6])])
        with ExitStack() as ctx:
            sb1 = lambda name, shape, dt=F32: k.sb(name, shape, dt, ctx)
            wqk, wv = sb1("wqk", [P, H * CC]), sb1("wv2", [P, H * d])
            wq_t, wk_t = sb1("wq_t", [P, 4, C]), sb1("wk_t", [P, 4, CC])
            load(nc, [(wq_t[:], a["l1_wq2_t"]), (wk_t[:], a["l1_wk2_t"]), (wv[:], a["l1_wv2"])])
            fold_keys(nc, k, wq_t, wk_t, wqk[:])
            cross_attention(nc, k, False, H, d, scale, ctx_norm_t, xt, wqk[:], None, wv[:], y)
        with ExitStack() as ctx:
            big = k.sb("big", [P, 4, TOK], F32, ctx)
            mha_end(nc, k, a, p + "a2_", x1, y, xn, xt, big, x2)
        add_tokens(nc, x2[:], x2[:], x1[:])
        add_tokens(nc, k.x[:], k.x[:], x2[:])
    with ExitStack() as c0:
        sb = lambda name, shape, dt=F32: k.sb(name, shape, dt, c0)
        xt, ht = sb("xt", [P, TOK]), sb("ht", [P, 4, TOK])
        w1, w2, b1, b2 = sb("w1", [P, 4 * C]), sb("w2", [P, 4 * C]), sb("b1", [P, 4]), sb("b2", [1, C])
        load(nc, [(w1[:], a["l1_w1_t"]), (w2[:].rearrange("p (j c) -> p j c", c=C),
                                          a["l1_w2_t"].rearrange("(j p) c -> p j c", p=P)),
                  (b1[:], a["l1_b1"]), (b2[:], vec_row(a["L1_ffn_b2"]))])
        for w in (w1, w2):
            quantize_weight(nc, k, w[:], True, 1.0 / (4 * C * C), EPS, -1.0, 1.0, False)
        normalized_t(nc, k, k.x, xn, [(xt, None, None)])
        linear_channels(nc, k, [(w1[:, C * j:C * j + C], xt, ht[:, j, :], b1[:, j:j + 1], P) for j in range(4)],
                        ACT.Relu)
        linear_tokens(nc, k, C, [(tile_of(ht[:, j, :]), w2[:, C * j:C * j + C]) for j in range(4)], b2[:],
                      **residual(k))


def layer2(nc, k, a, xn):
    with ExitStack() as c0:
        sb = lambda name, shape, dt=F32: k.sb(name, shape, dt, c0)
        xt, qt, yc = sb("xt", [P, TOK]), sb("qt", [P, TOK]), sb("yc", [P, NT, CC])
        wq, bq, wk, wv, bv = sb("wq", [P, C]), sb("bq", [P, 1]), sb("wk", [P, R]), sb("wv", [CC, C]), sb("bv", [1, C])
        load(nc, [(wq[:], a["L2_xattn_Wq"]), (bq[:], vec_col(a["L2_xattn_bq"])), (wk[:], a["l2_wk_t"]),
                  (wv[:], a["L2_xattn_Wv"]), (bv[:], vec_row(a["L2_xattn_bv"]))])
        normalized_t(nc, k, k.x, xn, [(xt, None, None)])
        linear_channels(nc, k, [(wq[:], xt, qt, bq[:], P)], ACT.Identity)
        cross_attention(nc, k, False, 1, CC, 1.0, a["ctx_t"], qt, wk[:], None, None, yc, a["ctx_512"])
        transpose(nc, k, lambda t: yc[:, t, :], CC, [(xt, None, None)])
        linear_tokens(nc, k, C, [(tile_of(xt[0:CC, :]), wv[:])], bv[:], **residual(k))
    with ExitStack() as c0:
        sb = lambda name, shape, dt=F32: k.sb(name, shape, dt, c0)
        xt, st, ht = sb("xt", [P, TOK]), sb("shared_t", [P, TOK]), sb("hid_t", [P, TOK])
        wi, wo, w1, w2 = sb("w_in", [P, 2 * C]), sb("w_out", [P, C]), sb("w1", [P, 2 * C]), sb("w2", [P, 8, C])
        wg, bg, lg, wd = sb("wg", [P, 8]), sb("bg", [1, 8]), sb("logits", [P, NT, 8]), sb("wdense", [P, NT, 8])
        load(nc, [(wi[:], a["L2_ffn_w_shared_in"]), (wo[:], a["L2_ffn_w_shared_out"]), (w1[:], a["L2_ffn_w1_shared"]),
                  (w2[:], a["L2_ffn_w2"].rearrange("e p c -> p e c")), (wg[:], a["L2_ffn_w_gate"]),
                  (bg[:], vec_row(a["L2_ffn_gate_bias"]))])
        normalized_t(nc, k, k.x, xn, [(xt, None, None)])
        linear_tokens(nc, k, 8, [(tile_of(xt), wg[:])], bg[:], lambda ts: lg[:, ts, :])
        route(nc, k, lg[:], wd[:])
        for w, o in ((wi, st), (w1, ht)):
            chunk = lambda i: xt[:, BANK * i:BANK * i + BANK]
            gated(nc, k, BANK, lambda i: w[:, 0:C], lambda i: w[:, C:2 * C], chunk, chunk,
                  [o[:, BANK * i:BANK * i + BANK] for i in range(4)])
        linear_tokens(nc, k, C, [(tile_of(st), wo[:])], None, **residual(k))
        experts(nc, k, ht, w2, wd)


def layer3(nc, k, a, xn):
    with ExitStack() as c0:
        sb = lambda name, shape, dt=F32: k.sb(name, shape, dt, c0)
        xt, y = sb("xt", [P, TOK]), sb("y", [P, NT, C])
        wq, wk, wv, wo = sb("wq", [P, C]), sb("wk", [P, C]), sb("wv", [P, H * 9]), sb("wo", [P, C])
        load(nc, [(wq[:], a["l3_wq_t"]), (wk[:], a["l3_wk_t"]), (wv[:], a["l3_wv_t"]), (wo[:], a["l3_wo_t"])])
        normalized_t(nc, k, k.x, xn, [(xt, None, None)])
        with ExitStack() as ctx:
            qtok = k.sb("qtok_all", [P, NT, H * SLOT], BF16, ctx)
            linear_tokens(nc, k, C, [(tile_of(xt), wq[:])], None, lambda ts: y[:, ts, :])
            split_queries(nc, k, y[:], qtok)
            cross_attention(nc, k, True, H, 8, float(8 ** -0.5), a["ctx_t"], qtok, None, wk[:], wv[:], y)
        transpose(nc, k, lambda t: y[:, t, :], C, [(xt, None, None)])
        linear_tokens(nc, k, C, [(tile_of(xt), wo[:])], None, **residual(k))
    with ExitStack() as c0:
        sb = lambda name, shape, dt=F32: k.sb(name, shape, dt, c0)
        I = 352
        rows = [(0, P), (P, 2 * P), (2 * P, I)]
        xt, h = sb("xt", [P, TOK]), sb("h", [P, NT, I])
        wg, wu, wd = sb("wg", [P, 3, C]), sb("wu", [P, 3, C]), sb("wd", [P, I])
        wgt, wut, wdt = sb("wgt", [P, I]), sb("wut", [P, I]), sb("wdt", [P, 3, C])
        clear(nc, (wg[:], 0.0), (wu[:], 0.0))
        load(nc, [(w[0:hi - lo, j, :], a[n][lo:hi, :]) for w, n in ((wg, "L3_ffn_w_gate"), (wu, "L3_ffn_w_up"))
                  for j, (lo, hi) in enumerate(rows)] + [(wd[:], a["L3_ffn_w_down"])])
        quantize_fp4(nc, k, wg[:].rearrange("p j (n e) -> p (j n) e", e=16), 24)
        quantize_fp4(nc, k, wu[:].rearrange("p j (n e) -> p (j n) e", e=16), 24)
        quantize_fp4(nc, k, wd[:].rearrange("p (n e) -> p n e", e=16), 22)
        transpose_weight(nc, k, [(w[0:hi - lo, j, :], wt[:, lo:hi]) for w, wt in ((wg, wgt), (wu, wut))
                                 for j, (lo, hi) in enumerate(rows)] +
                         [(wd[:, lo:hi], wdt[0:hi - lo, j, :]) for j, (lo, hi) in enumerate(rows)])
        normalize(nc, k, k.x, xn)
        quantize_fp4(nc, k, xn[:].rearrange("p t (n e) -> p (t n) e", e=16), NT * 8)
        transpose(nc, k, lambda t: xn[:, t, :], C, [(xt, None, None)])
        gated(nc, k, I, tile_of(xt), tile_of(xt), lambda i: wgt[:], lambda i: wut[:], [h[:, t, :] for t in range(NT)])
        quantize_fp4(nc, k, h[:].rearrange("p t (n e) -> p (t n) e", e=16), NT * 22)
        ht = sb("ht", [P, 3, TOK])
        for j, (lo, hi) in enumerate(rows):
            transpose(nc, k, lambda t: h[:, t, lo:hi], hi - lo, [(ht[:, j, :], None, None)])
        linear_tokens(nc, k, C, [(tile_of(ht[0:hi - lo, j, :]), wdt[0:hi - lo, j, :])
                                 for j, (lo, hi) in enumerate(rows)], None, **residual(k))


def network(nc, a, out):
    with ExitStack() as ctx:
        k = Chip(nc, ctx)
        tokens = lambda ap: ap.rearrange("b (t p) c -> p (b t) c", p=P)
        set_constants(nc, k)
        load(nc, [(k.x[:], tokens(a["x"]))])
        xn = k.sb("xn", [P, NT, C])
        for layer in (layer0, layer1, layer2, layer3):
            layer(nc, k, a, xn)
        load(nc, [(tokens(out), k.x[:])])


NATURAL = """x ctx_512 L0_xattn_Wcq L0_xattn_bcq L0_xattn_Wp L0_xattn_bp L0_ffn_kernel L0_ffn_bias L0_ffn_a L0_ffn_b
L1_xattn_ln1_g L1_xattn_ln1_b L1_xattn_ln2_g L1_xattn_ln2_b L1_xattn_a1_li1_w L1_xattn_a1_li1_b L1_xattn_a1_lnx_g
L1_xattn_a1_lnx_b L1_xattn_a1_lny_g L1_xattn_a1_lny_b L1_xattn_a1_ln3_g L1_xattn_a1_ln3_b L1_xattn_a1_li2_w
L1_xattn_a1_li3_w L1_xattn_a1_li3_b L1_xattn_a2_li1_w L1_xattn_a2_li1_b L1_xattn_a2_lnx_g L1_xattn_a2_lnx_b
L1_xattn_a2_lny_g L1_xattn_a2_lny_b L1_xattn_a2_ln3_g L1_xattn_a2_ln3_b L1_xattn_a2_li2_w L1_xattn_a2_li3_w
L1_xattn_a2_li3_b L1_ffn_b2 L2_xattn_Wq L2_xattn_bq L2_xattn_Wv L2_xattn_bv L2_ffn_w_shared_in
L2_ffn_w_shared_out L2_ffn_w1_shared L2_ffn_w2 L2_ffn_w_gate L2_ffn_gate_bias L3_ffn_w_gate L3_ffn_w_up
L3_ffn_w_down""".split()


def spaced(w, d, width, fill=0.0):
    w = np.asarray(w)
    w = w.reshape(w.shape[:-1] + (H, d))
    out = np.zeros(w.shape[:-1] + (width,), w.dtype)
    out[..., 0:d] = w
    if fill:
        out[..., d] = fill
    return out.reshape(w.shape[:-2] + (H * width,))


def columns(v):
    return np.asarray(v).reshape(-1, P).T


def with_row(w, row):
    w = np.asarray(w)
    return np.concatenate([w, np.asarray(row)[None], np.zeros((P - 1 - w.shape[0], w.shape[1]), w.dtype)], 0)


def laid_out(inputs):
    i = {n: np.asarray(v) for n, v in inputs.items()}
    a = {n: i[n] for n in NATURAL}
    p = "L0_xattn_"
    a["l0_wq"], a["l0_wk"] = spaced(i[p + "Wq"], 8, 32), spaced(i[p + "Wk"], 8, 32)
    a["l0_bq"], a["l0_bk"] = columns(spaced(i[p + "bq"], 8, 32)), columns(spaced(i[p + "bk"], 8, 32, 1.0))
    a["l0_wv"], a["l0_bv"] = spaced(i[p + "Wv"], 8, 9), spaced(i[p + "bv"], 8, 9, 1.0)[None]
    a["ctx_t"] = i["ctx_512"].transpose(0, 2, 1)
    a["l0_wck"] = with_row(i[p + "Wck"], i[p + "bck"])
    a["l0_wcv"] = with_row(spaced(i[p + "Wcv"], 8, 9), spaced(i[p + "bcv"], 8, 9, 1.0))
    p = "L1_xattn_"
    heads = lambda w: i[p + w].transpose(1, 0, 2).reshape(i[p + w].shape[1], -1)
    none = np.zeros(H * 32, np.float32)
    a["l1_wq"], a["l1_wk"] = spaced(heads("a1_wq"), 32, 64), spaced(heads("a1_wk"), 32, 64)
    a["l1_qb"], a["l1_kb"] = columns(spaced(none, 32, 64)), columns(spaced(none, 32, 64, 1.0))
    a["l1_wv"] = spaced(heads("a1_wv"), 32, 33)
    a["l1_wv2"] = with_row(heads("a2_wv"), none)
    a["l1_wq2_t"] = i[p + "a2_wq"].reshape(4, 4, C, 32).transpose(1, 3, 0, 2).reshape(P, 4, C)
    a["l1_wk2_t"] = i[p + "a2_wk"].reshape(4, 4, CC, 32).transpose(1, 3, 0, 2).reshape(P, 4, CC)
    for m in ("a1_", "a2_"):
        a[p + m + "li2_b_cols"] = columns(i[p + m + "li2_b"])
    a["l1_w1_t"], a["l1_w2_t"], a["l1_b1"] = i["L1_ffn_W1"].T, i["L1_ffn_W2"].T, columns(i["L1_ffn_b1"])
    a["l2_wk_t"] = np.concatenate([i["L2_xattn_Wk"].T, i["L2_xattn_bk"][:, None]], 1)
    kv = i["L3_xattn_Wkv"].T
    a["l3_wq_t"], a["l3_wo_t"] = i["L3_xattn_Wq"].T, i["L3_xattn_Wo"].T
    a["l3_wk_t"] = with_row(kv[:, 0:C], np.zeros(C, np.float32))
    a["l3_wv_t"] = with_row(spaced(kv[:, C:], 8, 9), spaced(np.zeros(C, np.float32), 8, 9, 1.0))
    return {n: np.ascontiguousarray(v) for n, v in a.items()}


def kernel(**inputs):
    import concourse.bacc as bacc
    from concourse.bass_utils import run_bass_kernel_spmd

    nc = bacc.Bacc("TRN2", target_bir_lowering=False, num_devices=1)
    arrays = laid_out(inputs)
    args = {n: nc.dram_tensor("in_" + n, v.shape, F32, kind="ExternalInput").ap() for n, v in arrays.items()}
    out = nc.dram_tensor("out_0_dram", (B, S, C), F32, kind="ExternalOutput").ap()
    network(nc, args, out)
    result = run_bass_kernel_spmd(nc, [{"in_" + n: v for n, v in arrays.items()}], core_ids=[0])
    return result.results[0]["out_0_dram"]
```
